# Optimizing a Trainium2 kernel written in Bass

```python
import numpy as np
import jax
import jax.numpy as jnp

def _softmax(x, axis=-1):
    return jax.nn.softmax(x, axis=axis)

def _gelu(x):
    return jax.nn.gelu(x, approximate=True)

def _silu(x):
    return jax.nn.silu(x)

def _sigmoid(x):
    return jax.nn.sigmoid(x)

def _layernorm(x, axis=-1, eps=1e-05):
    m = jnp.mean(x, axis=axis, keepdims=True)
    v = jnp.var(x, axis=axis, keepdims=True)
    return (x - m) / jnp.sqrt(v + eps)

def _scatter_add(tgt, idx, src, axis=0):
    return tgt.at[idx].add(src)

def _segment_sum(src, seg, n):
    return jax.ops.segment_sum(src, seg, n)
kernel_name = 'mk_gnn_preln_d4_gnn_r16_9e0f8b'

def setup_inputs(seed: int=0):
    np.random.seed(seed)
    _w = jnp.asarray

    def _rec_inputs():
        import jax
        import jax.numpy as jnp
        _gk = jax.random.key(seed)
        x = -0.0001006 + 1 * jax.random.normal(jax.random.fold_in(_gk, 1), (6250, 96), jnp.float32)
        src = jax.random.randint(jax.random.fold_in(_gk, 2), (100000,), 0, 6250, jnp.int32)
        dst = jax.random.randint(jax.random.fold_in(_gk, 3), (100000,), 0, 6250, jnp.int32)
        _o = jnp.argsort(dst, stable=True)
        src = src[_o]
        dst = dst[_o]
        return (x, src, dst)
    x, src, dst = _rec_inputs()

    def _L0_gnn_setup():
        import jax, jax.numpy as jnp
        import numpy as np
        N_NODES = 3125
        N_EDGES = 50000
        D_MODEL = 96
        HEADS = 4
        key = jax.random.key(seed)
        ks = jax.random.split(key, 6)
        scale = 1.0 / np.sqrt(D_MODEL)
        return {'embeds': jax.random.normal(ks[0], (N_NODES, D_MODEL), dtype=jnp.float32), 'qW': jax.random.normal(ks[1], (D_MODEL, D_MODEL), dtype=jnp.float32) * scale, 'kW': jax.random.normal(ks[2], (D_MODEL, D_MODEL), dtype=jnp.float32) * scale, 'vW': jax.random.normal(ks[3], (D_MODEL, D_MODEL), dtype=jnp.float32) * scale, 'rows': jax.random.randint(ks[4], (N_EDGES,), 0, N_NODES, dtype=jnp.int32), 'cols': jax.random.randint(ks[5], (N_EDGES,), 0, N_NODES, dtype=jnp.int32)}
    _L0_gnn_all = _L0_gnn_setup()
    _L0_gnn_in = {k: v for k, v in _L0_gnn_all.items() if k in ('qW', 'kW', 'vW')}
    del _L0_gnn_all

    def _L1_gnn_setup():
        import jax, jax.numpy as jnp
        import numpy as np
        EPS = 1e-07
        BETA = 1.0
        key = jax.random.key(seed)
        k1, k2, k3, k4 = jax.random.split(key, 4)
        N, E, D_IN, D_OUT = (3125, 50000, 96, 96)
        feat = jax.random.normal(k1, (N, D_IN), dtype=jnp.float32)
        src = jax.random.randint(k2, (E,), 0, N, dtype=jnp.int32)
        dst = jax.random.randint(k3, (E,), 0, N, dtype=jnp.int32)
        W = jax.random.normal(k4, (D_IN, D_OUT), dtype=jnp.float32) / np.sqrt(D_IN)
        b = jnp.zeros((D_OUT,), dtype=jnp.float32)
        return {'feat': feat, 'src': src, 'dst': dst, 'W': W, 'b': b}
    _L1_gnn_all = _L1_gnn_setup()
    _L1_gnn_in = {k: v for k, v in _L1_gnn_all.items() if k in ('W', 'b')}
    del _L1_gnn_all

    def _L2_gnn_setup():
        import jax, jax.numpy as jnp
        import numpy as np
        K = 10
        ALPHA = 0.1
        BETA = 0.9
        N_NODES = 3125
        N_EDGES = 50000
        D_FEAT = 96
        key = jax.random.key(seed)
        k1, k2, k3 = jax.random.split(key, 3)
        x = jax.random.normal(k1, (N_NODES, D_FEAT), dtype=jnp.float32)
        row = jax.random.randint(k2, (N_EDGES,), 0, N_NODES, dtype=jnp.int64)
        col = jax.random.randint(k3, (N_EDGES,), 0, N_NODES, dtype=jnp.int64)
        edge_index = jnp.stack([row, col], axis=0)
        return {'x': x, 'edge_index': edge_index}
    _L2_gnn_all = _L2_gnn_setup()
    _L2_gnn_in = {k: v for k, v in _L2_gnn_all.items() if k in ()}
    del _L2_gnn_all

    def _L3_gnn_setup():
        import jax, jax.numpy as jnp
        import numpy as np
        N_NODES = 3125
        N_EDGES = 50000
        IN_DIM = 96
        HID = 96

        def _gcn_conv(x, src, dst, norm, W, b, n_nodes):
            xw = x @ W
            msg = xw[src] * norm[:, None]
            agg = jax.ops.segment_sum(msg, dst, num_segments=n_nodes)
            return agg + b
        key = jax.random.key(seed)
        k1, k2, k3, k4 = jax.random.split(key, 4)
        x = jax.random.normal(k1, (N_NODES, IN_DIM), dtype=jnp.float32)
        edge_index = jax.random.randint(k2, (2, N_EDGES), 0, N_NODES, dtype=jnp.int64)
        s1 = 1.0 / np.sqrt(IN_DIM)
        s2 = 1.0 / np.sqrt(HID)
        W1 = jax.random.normal(k3, (IN_DIM, HID), dtype=jnp.float32) * s1
        b1 = jnp.zeros((HID,), dtype=jnp.float32)
        W2 = jax.random.normal(k4, (HID, HID), dtype=jnp.float32) * s2
        b2 = jnp.zeros((HID,), dtype=jnp.float32)
        return {'x': x, 'edge_index': edge_index, 'W1': W1, 'b1': b1, 'W2': W2, 'b2': b2}
    _L3_gnn_all = _L3_gnn_setup()
    _L3_gnn_in = {k: v for k, v in _L3_gnn_all.items() if k in ('W1', 'b1', 'W2', 'b2')}
    del _L3_gnn_all
    return {'x': x, 'src': src, 'dst': dst, 'L0_gnn_qW': _L0_gnn_in['qW'], 'L0_gnn_kW': _L0_gnn_in['kW'], 'L0_gnn_vW': _L0_gnn_in['vW'], 'L1_gnn_W': _L1_gnn_in['W'], 'L1_gnn_b': _L1_gnn_in['b'], 'L3_gnn_W1': _L3_gnn_in['W1'], 'L3_gnn_b1': _L3_gnn_in['b1'], 'L3_gnn_W2': _L3_gnn_in['W2'], 'L3_gnn_b2': _L3_gnn_in['b2']}

def reference(x, src, dst, L0_gnn_qW, L0_gnn_kW, L0_gnn_vW, L1_gnn_W, L1_gnn_b, L3_gnn_W1, L3_gnn_b1, L3_gnn_W2, L3_gnn_b2):
    import jax
    import jax.numpy as jnp

    def _L0_gnn_ref(embeds, qW, kW, vW, rows, cols):
        import jax, jax.numpy as jnp
        import numpy as np
        N_NODES = 3125
        N_EDGES = 50000
        D_MODEL = 96
        HEADS = 4
        nvar, d = embeds.shape
        dh = d // HEADS
        e = rows.shape[0]
        q = (embeds[rows] @ qW).reshape(e, HEADS, dh)
        k = (embeds[cols] @ kW).reshape(e, HEADS, dh)
        v = (embeds[cols] @ vW).reshape(e, HEADS, dh)
        scores = jnp.clip(jnp.einsum('ehd,ehd->eh', q, k), -10.0, 10.0)
        exp_s = jnp.exp(scores)
        norms = jax.ops.segment_sum(exp_s, rows, num_segments=nvar)[rows]
        w = exp_s / (norms + 1e-08)
        res = jax.ops.segment_sum(w[:, :, None] * v, rows, num_segments=nvar).reshape(nvar, d)
        return embeds + res

    def _L1_gnn_ref(feat, src, dst, W, b):
        import jax, jax.numpy as jnp
        import numpy as np
        EPS = 1e-07
        BETA = 1.0
        N = feat.shape[0]
        m = jax.nn.relu(feat[src]) + EPS
        logits = BETA * m
        seg_max = jax.ops.segment_max(logits, dst, num_segments=N)
        ex = jnp.exp(logits - seg_max[dst])
        denom = jax.ops.segment_sum(ex, dst, num_segments=N)
        a = ex / denom[dst]
        msg = jax.ops.segment_sum(a * m, dst, num_segments=N)
        feats = feat + msg
        return feats @ W + b

    def _L2_gnn_ref(x, edge_index):
        import jax, jax.numpy as jnp
        import numpy as np
        K = 10
        ALPHA = 0.1
        BETA = 0.9
        N_NODES = 3125
        N_EDGES = 50000
        D_FEAT = 96
        n = x.shape[0]
        row, col = (edge_index[0], edge_index[1])
        ones = jnp.ones((edge_index.shape[1],), dtype=x.dtype)
        deg_row = jnp.maximum(jax.ops.segment_sum(ones, row, num_segments=n), 1.0)
        deg_col = jnp.maximum(jax.ops.segment_sum(ones, col, num_segments=n), 1.0)
        w = jax.lax.rsqrt(deg_row[row] * deg_col[col])

        def spmm(feat):
            msg = feat[col] * w[:, None]
            return jax.ops.segment_sum(msg, row, num_segments=n)
        h = x
        out = h
        for _ in range(K):
            out = spmm(out) * BETA + h * ALPHA
        theta = BETA ** K + ALPHA * sum((BETA ** i for i in range(K)))
        return out / jnp.asarray(theta, dtype=x.dtype)

    def _L3_gnn_ref(x, edge_index, W1, b1, W2, b2):
        import jax, jax.numpy as jnp
        import numpy as np
        N_NODES = 3125
        N_EDGES = 50000
        IN_DIM = 96
        HID = 96

        def _gcn_conv(x, src, dst, norm, W, b, n_nodes):
            xw = x @ W
            msg = xw[src] * norm[:, None]
            agg = jax.ops.segment_sum(msg, dst, num_segments=n_nodes)
            return agg + b
        n_nodes = x.shape[0]
        loops = jnp.arange(n_nodes, dtype=edge_index.dtype)
        src = jnp.concatenate([edge_index[0], loops])
        dst = jnp.concatenate([edge_index[1], loops])
        deg = jax.ops.segment_sum(jnp.ones(dst.shape, dtype=x.dtype), dst, num_segments=n_nodes)
        dinv = jnp.where(deg > 0, jax.lax.rsqrt(deg), 0.0)
        norm = dinv[src] * dinv[dst]
        h = jax.nn.relu(_gcn_conv(x, src, dst, norm, W1, b1, n_nodes))
        h = jax.nn.relu(_gcn_conv(h, src, dst, norm, W2, b2, n_nodes))
        return h
    edge_index = jnp.stack([src, dst])
    h = jnp.maximum(_layernorm(x, axis=-1), 0.0)
    x = x + _L0_gnn_ref(h, L0_gnn_qW, L0_gnn_kW, L0_gnn_vW, src, dst)
    h = jnp.maximum(_layernorm(x, axis=-1), 0.0)
    x = x + _L1_gnn_ref(h, src, dst, L1_gnn_W, L1_gnn_b)
    h = jnp.maximum(_layernorm(x, axis=-1), 0.0)
    x = x + _L2_gnn_ref(h, edge_index)
    h = jnp.maximum(_layernorm(x, axis=-1), 0.0)
    x = x + _L3_gnn_ref(h, edge_index, L3_gnn_W1, L3_gnn_b1, L3_gnn_W2, L3_gnn_b2)
    return x

_drawn_inputs = setup_inputs


def setup_inputs(seed=0):
    import zlib

    import numpy as np

    out = dict(_drawn_inputs(seed))
    spreads = {'L1_gnn_b': (0.0, 0.1), 'L3_gnn_b1': (0.0, 0.471), 'L3_gnn_b2': (0.0, 0.396)}
    factors = {}
    for name, (base, spread) in spreads.items():
        noise = np.random.default_rng([zlib.crc32(name.encode()), seed]).standard_normal(out[name].shape)
        drawn = base * np.exp(spread * noise) if base else spread * noise
        out[name] = jnp.asarray(drawn.astype(out[name].dtype))
    for name, factor in factors.items():
        out[name] = (out[name] * factor).astype(out[name].dtype)
    return out
```

```python
from contextlib import ExitStack, contextmanager

import concourse.bass as bass
from concourse import mybir

ALU = mybir.AluOpType
ACT = mybir.ActivationFunctionType
AX = mybir.AxisListType
F32, F16, BF16, F8 = mybir.dt.float32, mybir.dt.float16, mybir.dt.bfloat16, mybir.dt.float8e4
I32, U8 = mybir.dt.int32, mybir.dt.uint8

P = 128
NODES, EDGES, D, HEADS = 6250, 100000, 96, 4
DH = D // HEADS
TILES = -(-NODES // P)
LAST = NODES - (TILES - 1) * P
GROUP = 2 * P
GROUPS = -(-NODES // GROUP)
WIDE = GROUPS * GROUP
PAIRS = (TILES + 1) // 2
BTILES = 2 * PAIRS
RUN = 36
CAP = P * RUN
SCAN = 125
COLS = EDGES // SCAN
CHUNK = 5
CHUNKS = GROUPS // CHUNK
AV = D + HEADS + 1
RING = 7
BODIES = TILES // RING
PANEL = TILES * P
LO = 2048.0
SCALE = 64.0
EXACT = 16.0
EPS_LN, EPS_ATT, EPS_MSG = 1e-5, 1e-8, 1e-7
STEPS, ALPHA, BETA = 10, 0.1, 0.9
THETA = BETA ** STEPS + ALPHA * sum(BETA ** i for i in range(STEPS))


class Sig:

    def __init__(self, ctx, nc, name):
        self.sem = ctx.enter_context(nc.semaphore(name))
        self.count = 0
        self.frames = []

    def now(self, more=0):
        value = self.count + more
        for i, per in self.frames:
            if per:
                value = i * per + value
        return self, value

    def by(self, ins, n=1):
        ins.then_inc(self.sem, n)
        self.count += n
        return self.now()


def wait(eng, *tokens):
    for sig, value in tokens:
        if not isinstance(value, int) or value > 0:
            eng.wait_ge(sig.sem, value)


def settle(eng, spare):
    eng.sem_inc(spare.sem, 1)


class Net:
    def __init__(self, nc, ctx):
        self.nc = nc
        self.v, self.a, self.pe, self.pool, self.sp = nc.vector, nc.scalar, nc.tensor, nc.gpsimd, nc.sync
        self.sigs = []

        def sig(name):
            self.sigs.append((name, Sig(ctx, nc, name)))
            return self.sigs[-1][1]

        self.sv, self.sa, self.se, self.sg = sig("sv"), sig("sa"), sig("se"), sig("sg")
        self.ld = sig("ld")
        self.kv = [sig("kv0"), sig("kv1")]
        self.row = sig("row")
        self.stored = sig("stored")
        self.spare = Sig(ctx, nc, "spare")
        self.used = sig("used")
        self.free = sig("free")
        self.done = sig("done")
        self.ring = [sig(f"ring{r}") for r in range(RING)]
        for s, start in ((self.se, 1), (self.stored, 1), (self.used, RING - 1), (self.free, RING),
                         (self.done, RING)):
            self.pe.sem_inc(s.sem, start)
            s.count = start

    def buf(self, ctx, name, shape, dt):
        return ctx.enter_context(self.nc.sbuf_tensor(name, shape, dt))

    def bank(self, ctx, name, dt=F32):
        return ctx.enter_context(self.nc.psum_tensor(name, [P, 2048 // mybir.dt.size(dt)], dt))

    def V(self, ins):
        return self.sv.by(ins)

    def A(self, ins):
        return self.sa.by(ins)

    def E(self, ins):
        return self.se.by(ins)

    def G(self, ins):
        return self.sg.by(ins)

    def meet(self, *engines):
        own = [(self.v, self.sv), (self.a, self.sa), (self.pe, self.se), (self.pool, self.sg)]
        for e in engines:
            for _, s in own:
                wait(e, s.now())

    @contextmanager
    def loop(self, trips, **per):
        start = {n: s.count for n, s in self.sigs}
        if self.se.frames:
            for e in (self.v, self.a, self.pe, self.pool, self.sp):
                settle(e, self.spare)
        with self.nc.Fori(0, trips) as i:
            for n, s in self.sigs:
                s.frames.append((i, per.get(n, 0)))
            yield i
        found = {n: s.count - start[n] for n, s in self.sigs if s.count != start[n]}
        if found != per:
            raise ValueError(f"increments in one pass: {found}")
        for n, s in self.sigs:
            s.frames.pop()
            s.count = start[n] + trips * per.get(n, 0)


def over(ap, n):
    return ap.unsqueeze(2).to_broadcast([ap.shape[0], ap.shape[1], n])


def under(ap, n):
    return ap.unsqueeze(1).to_broadcast([ap.shape[0], n, ap.shape[1]])


def layernorm_relu(n, s):
    v, a = n.v, n.a
    m, var, rstd = s.col
    n.meet(v, a)
    t = n.V(v.tensor_reduce(m[:], s.X[:], AX.X, ALU.add))
    wait(v, t)
    t = n.V(v.tensor_scalar(m[:], m[:], 1.0 / D, None, ALU.mult))
    wait(v, t)
    t = n.V(v.tensor_tensor(s.H[:], s.X[:], over(m[:], D), ALU.subtract))
    wait(a, t)
    t = n.A(a.square(s.T, s.H[:]))
    wait(v, t)
    t = n.V(v.tensor_reduce(var[:], s.T, AX.X, ALU.add))
    wait(v, t)
    t = n.V(v.tensor_scalar(var[:], var[:], 1.0 / D, EPS_LN, ALU.mult, ALU.add))
    t = inv_sqrt(n, rstd, var, t)
    wait(v, t)
    return n.V(v.scalar_tensor_tensor(s.H[:], s.H[:], 0.0, over(rstd[:], D), ALU.max, ALU.mult))


def inv_sqrt(n, y, x, t):
    wait(n.a, t)
    t = n.A(n.a.sqrt(y[:], x[:]))
    wait(n.v, t)
    return n.V(n.v.reciprocal(y[:], y[:]))


def linear(n, s, name, src, w, cols, bias, finish, **per):
    a, pe, nc = n.a, n.pe, n.nc
    rows_in = D + 1 if bias else D
    n.meet(n.v, a, pe, n.pool)
    with ExitStack() as ctx:
        tr = [n.bank(ctx, f"{name}_tr{i}") for i in range(2)]
        mm = [n.bank(ctx, f"{name}_mm{i}") for i in range(4)]
        with n.loop(BODIES, **per) as i:
            n.meet(n.v, a, pe)
            t = n.A(a.activation(s.stage[:], src[:, bass.ts(i, RING), :], ACT.Copy))
            wait(pe, t)
            moved = []
            for j in range(RING):
                t = n.E(pe.transpose(tr[j // 4][0:D, (j % 4) * P:(j % 4 + 1) * P], s.stage[:, j, :], s.ident[:]))
                if j in (3, RING - 1):
                    wait(a, t)
                    moved.append(n.A(a.activation(s.aT[0:D, (j // 4) * 4 * P:(j + 1) * P],
                                                  tr[j // 4][0:D, 0:(j % 4 + 1) * P], ACT.Copy)))
            ends = []
            for j in range(RING):
                if j in (0, 4):
                    wait(pe, moved[j // 4])
                if j >= 4:
                    wait(pe, ends[j - 4])
                o = mm[j % 4][:, 0:cols]
                t = n.E(pe.matmul(o, s.aT[0:rows_in, j * P:(j + 1) * P], w[0:rows_in, 0:cols], start=True, stop=True))
                ends.append(finish(i, j, o, t))
    n.meet(n.v, a, pe, n.pool)


def bucket_edges(n, s, src_in, dst_in):
    v, a, pe, pool, sp, nc = n.v, n.a, n.pe, n.pool, n.sp, n.nc
    with ExitStack() as ctx:
        dall = n.buf(ctx, "dall", [SCAN, COLS], I32)
        below = n.buf(ctx, "below", [SCAN, GROUPS], F32)
        junk = n.buf(ctx, "junk", [SCAN, COLS], BF16)
        first_f = n.buf(ctx, "first_f", [1, GROUPS], F32)
        first = n.buf(ctx, "first", [1, GROUPS], I32)
        es = n.buf(ctx, "es", [P, GROUPS, RUN], I32)
        ed = n.buf(ctx, "ed", [P, GROUPS, RUN], I32)
        ti = n.buf(ctx, "ti", [P, GROUPS, RUN], I32)
        base = n.buf(ctx, "base", [P, GROUPS], F32)
        valid = n.buf(ctx, "valid", [P, GROUPS, RUN], F32)
        tile1 = n.buf(ctx, "tile1", [P, GROUPS, RUN], F32)
        sloc = n.buf(ctx, "sloc", [P, GROUPS, RUN], F32)
        dloc = n.buf(ctx, "dloc", [P, GROUPS, RUN], F32)
        keep = n.buf(ctx, "keep", [P, TILES, RUN], BF16)
        bt = n.buf(ctx, "bt", [P, TILES, RUN], BF16)
        seen = n.buf(ctx, "seen", [P, TILES, RUN], BF16)
        prod = n.buf(ctx, "prod", [P, TILES, RUN], F32)
        rank = n.buf(ctx, "rank", [P, RUN], F32)
        onerank = n.buf(ctx, "onerank", [P, RUN, P], BF16)
        vals = n.buf(ctx, "vals", [P, RUN, 2, TILES], BF16)
        pc = n.bank(ctx, "pc")
        pp = n.bank(ctx, "pp")
        po = n.bank(ctx, "po")

        sp.dma_start(dall[:], dst_in.rearrange("(p e) -> p e", p=SCAN)).then_inc(n.ld.sem, 16)
        n.ld.count += 16
        wait(v, n.ld.now())
        for g in range(GROUPS):
            t = n.V(v.tensor_scalar(junk[:], dall[:], float(g * GROUP), None, ALU.is_lt, ALU.add,
                                    accum_out=below[:, g:g + 1]))
            wait(v, t)
        wait(pe, t)
        t = n.E(pe.matmul(pc[0:1, 0:GROUPS], s.ones[0:SCAN, 0:1], below[:], start=True, stop=True))
        wait(v, t)
        t = n.V(v.tensor_scalar(first_f[:], pc[0:1, 0:GROUPS], float(EDGES - CAP), None, ALU.min))
        wait(v, t)
        t = n.V(v.tensor_copy(first[:], first_f[:]))
        wait(sp, t)
        for g in range(GROUPS):
            at = sp.value_load(first[0:1, g:g + 1], min_val=0, max_val=EDGES - CAP)
            for buf_, arr in ((es, src_in), (ed, dst_in)):
                sp.dma_start(buf_[:, g, :], arr[bass.ds(at, CAP)].rearrange("(p r) -> p r", p=P)).then_inc(n.ld.sem, 16)
        n.ld.count += 32 * GROUPS
        t = n.G(pool.iota(base[:], [[GROUP, GROUPS]], base=0, channel_multiplier=0,
                          allow_small_or_imprecise_dtypes=True))
        wait(v, t)
        t = n.V(v.memset(keep[:], 1.0))
        wait(v, t)
        n.V(v.memset(keep[:, :, 0:1], 0.0))
        wait(v, n.ld.now())
        t = n.V(v.tensor_tensor(dloc[:], ed[:], over(base[:], RUN), ALU.subtract))
        wait(v, t)
        t = n.V(v.tensor_scalar(valid[:], dloc[:], float(GROUP - 1), None, ALU.is_le))
        wait(v, t)
        t = n.V(v.scalar_tensor_tensor(valid[:], dloc[:], 0.0, valid[:], ALU.is_ge, ALU.mult))
        wait(v, t)
        n.V(v.tensor_scalar(dloc[:], dloc[:], 1.0, None, ALU.add))
        t = n.V(v.tensor_scalar(ti[:], es[:], P - 1, None, ALU.bitwise_and))
        wait(v, t)
        t = n.V(v.tensor_scalar(sloc[:], ti[:], 1.0, None, ALU.add))
        wait(v, t)
        t = n.V(v.tensor_scalar(ti[:], es[:], 7, None, ALU.logical_shift_right))
        wait(v, t)
        t = n.V(v.scalar_tensor_tensor(tile1[:], ti[:], 1.0, valid[:], ALU.add, ALU.mult))

        number = s.count1[:, 0:TILES]
        flat = "p k r -> p (k r)"
        with n.loop(GROUPS, sv=5 + RUN, sg=2, se=1 + RUN, sa=1) as g:
            n.meet(v, a, pe, pool)
            t_b = n.V(v.tensor_tensor(bt[:], over(number, RUN), under(tile1[:, g, :], TILES), ALU.is_equal))
            wait(v, t_b)
            wait(pool, t_b)
            for i, val in enumerate((sloc, dloc)):
                t_vals = n.G(pool.tensor_tensor(vals[:, :, i, :], bt[:].rearrange("p k r -> p r k"),
                                                over(val[:, g, :], TILES), ALU.mult))
            t = n.V(v.tensor_tensor_scan(seen[:].rearrange(flat), keep[:].rearrange(flat), bt[:].rearrange(flat), 0.0,
                                         ALU.mult, ALU.add))
            wait(pe, t)
            t = n.E(pe.matmul(pp[:, 0:TILES], s.tri[:], seen[:, :, RUN - 1], start=True, stop=True))
            wait(v, t)
            t = n.V(v.tensor_tensor(prod[:], seen[:], over(pp[:, 0:TILES], RUN), ALU.add))
            wait(v, t)
            t = n.V(v.tensor_tensor(prod[:], prod[:], bt[:], ALU.mult))
            wait(v, t)
            t = n.V(v.tensor_reduce(rank[:], prod[:].rearrange("p k r -> p r k"), AX.X, ALU.add))
            wait(v, t)
            for r in range(RUN):
                t = n.V(v.tensor_scalar(onerank[:, r, :], s.count1[:, 0:P], rank[:, r:r + 1], None, ALU.is_equal))
                if r == 0:
                    wait(pe, t_vals)
                wait(pe, t)
                te = n.E(pe.matmul(po[:, 0:2 * TILES], onerank[:, r, :], vals[:, r, :, :].rearrange("p i k -> p (i k)"),
                                   start=r == 0, stop=r == RUN - 1))
            wait(a, te)
            n.A(a.activation(s.slots[:, :, 0:TILES, g],
                             po[:, 0:2 * TILES].rearrange("p (i k) -> p i k", i=2), ACT.Copy))
        n.meet(v, a, pe, pool)
        t = n.V(v.tensor_scalar(base[:], base[:], -1.0, None, ALU.add))
        wait(v, t)
        n.V(v.scalar_tensor_tensor(s.idx[:], s.slots[:, 1, :, :], 1.0,
                                   under(base[:], BTILES), ALU.max, ALU.add))
        t = n.V(v.tensor_scalar(s.slotmax[:], s.slots[:, 0, :, :].rearrange("p k g -> p (k g)"), 0.5, None,
                                ALU.is_gt, ALU.add, accum_out=s.full[:]))
        wait(pe, t)
        t = n.E(pe.matmul(pc[0:1, 0:1], s.ones[:, 0:1], s.full[:], start=True, stop=True))
        wait(v, t)
        n.V(v.tensor_copy(s.filled[:], pc[0:1, 0:1]))
        n.meet(v, a, pe, pool)


def attention_and_adjacency(n, s):
    v, a, pe, pool, sp = n.v, n.a, n.pe, n.pool, n.sp
    with ExitStack() as ctx:
        ix = [n.buf(ctx, f"ix{i}", [P, GROUPS], I32) for i in range(2)]
        sd = [n.buf(ctx, f"sd{i}", [P, 2, GROUPS], F32) for i in range(2)]
        q3 = [n.buf(ctx, f"q3_{i}", [P, 3, D], BF16) for i in range(2)]
        kv = [n.buf(ctx, f"kv_{i}", [P, GROUPS, 2 * D], F32) for i in range(2)]
        row = [n.buf(ctx, f"row_{i}", [P, WIDE], F8) for i in range(2)]
        col = [n.buf(ctx, f"col_{i}", [P, 2 * GROUPS, P], F8) for i in range(2)]
        hs = [n.buf(ctx, f"hs{i}", [P, CHUNK, P], BF16) for i in range(2)]
        hd = [n.buf(ctx, f"hd{i}", [P, CHUNK, GROUP], BF16) for i in range(2)]
        hsT = [n.buf(ctx, f"hsT{i}", [P, CHUNK, P], BF16) for i in range(2)]
        hs32 = [n.buf(ctx, f"hs32_{i}", [P, CHUNK, P], F32) for i in range(3)]
        qk = [n.buf(ctx, f"qk{i}", [P, CHUNK * D], F32) for i in range(2)]
        sc = [n.buf(ctx, f"sc{i}", [P, CHUNK * HEADS], F32) for i in range(2)]
        wv = [n.buf(ctx, f"wv{i}", [P, CHUNK, AV], F32) for i in range(2)]
        rden = n.buf(ctx, "rden", [P, HEADS], F32)
        most = n.buf(ctx, "most", [P, 2 * (GROUPS // 2 + 1)], F32)
        pt = n.bank(ctx, "pt", BF16)
        pq = [n.bank(ctx, f"pq{i}") for i in range(2)]
        pr = n.bank(ctx, "pr")
        pa = [n.bank(ctx, f"pa{i}") for i in range(4)]
        units = GROUPS // 2 + 1
        n.meet(v, a, pe, pool)
        for i in range(2):
            n.V(v.memset(wv[i][:, :, AV - 1:AV], 1.0))
        n.V(v.memset(most[:], 0.0))
        n.V(v.memset(s.most[:], 0.0))
        n.meet(v, a, pe, pool)
        PER = dict(sv=178, sa=58, se=220, sg=2, kv0=16 * GROUPS, kv1=16 * GROUPS, row=64, stored=1)
        with n.loop(PAIRS, **PER) as i:
            n.meet(v, a, pe)
            t_kvread = [None, None]
            end_row, end_col, q_in, sd_in = [None, None], [None, None], [None, None], [None, None]
            wait(v, n.stored.now())
            wait(a, n.stored.now())
            kv_here = [n.kv[b].now(16 * GROUPS) for b in range(2)]
            for b in range(2):
                sd_in[b] = n.V(v.tensor_copy(sd[b][:], s.slots[:, :, 2 * i + b, :]))
                q_in[b] = n.A(a.activation(q3[b][:], s.q3[:, 2 * i + b, :, :], ACT.Copy))
            onehot, turned, summed, queried, evacuated = {}, {}, {}, {}, {}
            stepq, exped, weighted, adj_read = {}, {}, {}, {}
            n_ch = 2 * CHUNKS
            unit = 0
            pa_free = [None] * 4
            for c in range(n_ch + 3):
                if c < n_ch:
                    b, k = c // CHUNKS, c % 2
                    if c in (0, CHUNKS):
                        wait(v, sd_in[b])
                    if c >= 2:
                        wait(v, turned[c - 2], adj_read[c - 2], summed32[c - 2])
                    else:
                        summed32 = {} if c == 0 else summed32
                    for g in range(CHUNK):
                        at = (c % CHUNKS) * CHUNK + g
                        n.V(v.tensor_scalar(hs[k][:, g, :], s.count1[:, 0:P], sd[b][:, 0, at:at + 1], None, ALU.is_equal))
                        t = n.V(v.tensor_scalar(hd[k][:, g, :], s.count1[:], sd[b][:, 1, at:at + 1], None, ALU.is_equal))
                    onehot[c] = t
                if c < n_ch:
                    wait(pe, onehot[c])
                    if c >= 1:
                        wait(pe, q_turned[c - 1])
                    for g in range(CHUNK):
                        t = n.E(pe.transpose(pt[:, g * P:(g + 1) * P], hs[k][:, g, :], s.identb[:]))
                    turned[c] = t
                    if c == 0:
                        q_turned = {}
                    wait(a, t)
                    q_turned[c] = n.A(a.activation(hsT[k][:].rearrange("p g e -> p (g e)"), pt[:, 0:CHUNK * P], ACT.Copy))
                    if c >= 3:
                        wait(a, summed[c - 3])
                    summed32[c] = n.A(a.activation(hs32[c % 3][:], hs[k][:], ACT.Copy))
                    jobs = []
                    for g in range(CHUNK):
                        at = (c % CHUNKS) * CHUNK + g
                        half = at % 2
                        if half == 0:
                            units_here = (unit % 4, (unit + 1) % 4)
                            unit += 2
                        for which in range(2):
                            pbank = units_here[which]
                            if half == 0 and pa_free[pbank] is not None:
                                wait(pe, pa_free[pbank])
                            if which == 0:
                                t = n.E(pe.matmul(pa[pbank][:, half * GROUP:(half + 1) * GROUP], hs[k][:, g, :],
                                                  hd[k][:, g, :], start=True, stop=True))
                            else:
                                for m in range(2):
                                    t = n.E(pe.matmul(pa[pbank][:, half * GROUP + m * P:half * GROUP + (m + 1) * P],
                                                      hd[k][:, g, m * P:(m + 1) * P], hs[k][:, g, :],
                                                      start=True, stop=True))
                            if half == 1 or at == GROUPS - 1:
                                jobs.append((which, at - half, half + 1, pbank, t, b))
                                pa_free[pbank] = None
                                held = jobs[-1]
                                width = held[2] * GROUP
                                if which == 0:
                                    wait(v, t)
                                    settle(v, n.spare)
                                    o = row[b][:, held[1] * GROUP:held[1] * GROUP + width]
                                    u = (held[1] // 2) + b * units
                                    pa_free[pbank] = n.V(v.tensor_scalar(o, pa[pbank][:, 0:width], 0.0, None, ALU.add,
                                                                         ALU.max, accum_out=most[:, u:u + 1],
                                                                         saturate=False))
                                    end_row[b] = pa_free[pbank]
                                else:
                                    wait(a, t)
                                    settle(a, n.spare)
                                    o = col[b][:, 2 * held[1]:2 * held[1] + width // P, :].rearrange("p m e -> p (m e)")
                                    pa_free[pbank] = n.A(a.activation(o, pa[pbank][:, 0:width], ACT.Copy, saturate=False))
                                    end_col[b] = pa_free[pbank]
                    adj_read[c] = t
                if 1 <= c <= n_ch:
                    e = c - 1
                    b, k = e // CHUNKS, e % 2
                    if e in (0, CHUNKS):
                        wait(pe, q_in[b])
                    wait(pe, q_turned[e])
                    if e >= 2:
                        wait(pe, stepq[e - 2])
                    for g in range(CHUNK):
                        for part in range(3):
                            t = pe.matmul(pq[k][:, g * D:(g + 1) * D], hsT[k][:, g, :], q3[b][:, part, :],
                                          start=part == 0, stop=part == 2)
                    queried[e] = n.E(t)
                    if e in (0, CHUNKS):
                        wait(v, kv_here[b])
                    wait(v, queried[e])
                    g0 = (e % CHUNKS) * CHUNK
                    t = n.V(v.tensor_tensor(qk[k][:].rearrange("p (g d) -> p g d", d=D),
                                            pq[k][:, 0:CHUNK * D].rearrange("p (g d) -> p g d", d=D),
                                            kv[b][:, g0:g0 + CHUNK, 0:D], ALU.mult))
                    stepq[e] = t
                    wait(v, t)
                    t = n.V(v.tensor_reduce(sc[k][:], qk[k][:].rearrange("p (h d) -> p h d", d=DH), AX.X, ALU.add))
                    wait(v, t)
                    t = n.V(v.tensor_scalar(sc[k][:], sc[k][:], 10.0, -10.0, ALU.min, ALU.max))
                    wait(a, t)
                    if e >= 2:
                        wait(a, summed[e - 2])
                    exped[e] = n.A(a.activation(wv[k][:, :, D:D + HEADS], sc[k][:].rearrange("p (g h) -> p g h", h=HEADS),
                                                ACT.Exp))
                if 2 <= c <= n_ch + 1:
                    e = c - 2
                    b, k = e // CHUNKS, e % 2
                    g0 = (e % CHUNKS) * CHUNK
                    wait(v, exped[e])
                    t = n.V(v.tensor_tensor(
                        wv[k][:, :, 0:D].rearrange("p g (h d) -> p g h d", d=DH),
                        kv[b][:, g0:g0 + CHUNK, D:2 * D].rearrange("p g (h d) -> p g h d", d=DH),
                        wv[k][:, :, D:D + HEADS].unsqueeze(3).to_broadcast([P, CHUNK, HEADS, DH]), ALU.mult))
                    t_kvread[b] = t
                    wait(pe, t)
                    if e == CHUNKS:
                        wait(pe, pr_read)
                    for g in range(CHUNK):
                        first, last = g0 + g == 0, g0 + g == GROUPS - 1
                        t = pe.matmul(pr[:, 0:AV], hs32[e % 3][:, g, :], wv[k][:, g, :], start=first, stop=last)
                    summed[e] = n.E(t)
                    if e % CHUNKS == CHUNKS - 1:
                        wait(v, summed[e], n.sv.now())
                        t = n.V(v.tensor_scalar(rden[:], pr[:, D:D + HEADS], EPS_ATT, None, ALU.add))
                        wait(v, t)
                        t = n.V(v.reciprocal(rden[:], rden[:]))
                        wait(v, t)
                        n.V(v.tensor_tensor(s.R[:, 2 * i + b, :].rearrange("p (h d) -> p h d", d=DH),
                                            pr[:, 0:D].rearrange("p (h d) -> p h d", d=DH), over(rden[:], DH), ALU.mult))
                        pr_read = n.V(v.tensor_copy(s.odeg[:, bass.ds(2 * i + b, 1)], pr[:, AV - 1:AV]))
            wait(v, n.sv.now())
            t = n.V(v.tensor_reduce(rden[:, 0:1], most[:], AX.X, ALU.max))
            wait(v, t)
            n.V(v.tensor_tensor(s.most[:], s.most[:], rden[:, 0:1], ALU.max))
            for b in range(2):
                for t in (end_row[b], end_col[b]):
                    wait(sp, t)
                    settle(sp, n.spare)
                n.row.by(sp.dma_start(s.c_d[2 * i + b, :, :], row[b][:].bitcast(U8)), 16)
                n.row.by(sp.dma_start(s.t_d[2 * i + b, :, :], col[b][:].bitcast(U8).rearrange("p m e -> p (m e)")), 16)
            wait(sp, n.row.now())
            sp.sem_inc(n.stored.sem, 1)
            n.stored.count += 1
            for b in range(2):
                sig, value = t_kvread[b]
                wait(pool, (sig, value - PER["sv"]))
                t = n.G(pool.tensor_copy(ix[b][:], s.idx[:, 2 * i + b, :]))
                wait(pool, t)
                settle(pool, n.spare)
                for g in range(GROUPS):
                    n.kv[b].by(pool.indirect_dma_start(kv[b][:, g, :], None, s.kv_d,
                                                       bass.IndirectOffsetOnAxis(ap=ix[b][:, g:g + 1], axis=0)), 16)
        n.meet(v, a, pe, pool, sp)
        for e in (v, a, pe, pool, sp):
            wait(e, n.row.now())


def aggregate(n, s, ps, panels, U, cols, finish):
    pe, sp = n.pe, n.sp
    mat = s.t_d if panels else s.c_d

    if not panels:
        wait(sp, n.done.now())

    def body(i):
        used0, free0, done0 = n.used.now(), n.free.now(), n.done.now()
        for r in range(RING):
            if panels or r == RING - 1:
                wait(sp, (n.done, done0[1] + (r + 1) - RING))
            else:
                wait(sp, (n.used, used0[1] + (r + 1) - (RING - 1)))
            settle(sp, n.spare)
            slot = s.ring[:, r, :]
            if panels:
                src = mat[RING * i + r, :, 0:PANEL]
                n.ring[r].by(sp.dma_start(slot, src), 16)
            else:
                src = mat[r * RING:(r + 1) * RING, :, bass.ds(i * (RING * P), RING * P)].rearrange("t p e -> p t e")
                n.ring[r].by(sp.dma_start(slot.rearrange("p (t e) -> p t e", t=RING), src), 16)
        w8 = s.ring[:].bitcast(F8)
        if panels:
            for r in range(RING):
                wait(pe, n.ring[r].now(), (n.free, free0[1] + (r + 1) - RING))
                settle(pe, n.spare)
                w = w8[:, r, :].rearrange("p (k e) -> p k e", e=P)
                for k in range(TILES):
                    t = pe.matmul(ps[r][:, 0:cols], w[:, k, :], U[:, k, 0:cols], start=k == 0, stop=k == TILES - 1)
                t = n.done.by(t)
                finish(i, r, ps[r], t)
        else:
            ends = []
            for r in range(RING):
                wait(pe, n.ring[r].now())
                settle(pe, n.spare)
                w = w8[:, r, :].rearrange("p (t j e) -> p t j e", t=RING, j=RING)
                for q in range(RING):
                    for j in range(RING):
                        if r == 0 and q == 0:
                            wait(pe, (n.free, free0[1] + (j + 1) - RING))
                            settle(pe, n.spare)
                        t = pe.matmul(ps[j][:, 0:cols], w[:, q, j, :], U[:, r * RING + q, 0:cols],
                                      start=r == q == 0, stop=r == q == RING - 1)
                        if r == q == RING - 1:
                            ends.append(n.done.by(t))
                if r < RING - 1:
                    n.used.by(t)
            for j in range(RING):
                finish(i, j, ps[j], ends[j])
    return body


def split16(n, src, U, at, t):
    v, a = n.v, n.a
    hi = U[:, :, at:at + D]
    wait(a, t)
    t = n.A(a.activation(hi, src, ACT.Copy))
    wait(v, t)
    t = n.V(v.tensor_tensor(src, src, hi, ALU.subtract))
    wait(a, t)
    return n.A(a.activation(U[:, :, at + D:at + 2 * D], src, ACT.Copy, scale=LO))


def softmax_dense(n, s, ps):
    v, a = n.v, n.a
    t_h = layernorm_relu(n, s)
    with ExitStack() as ctx:
        cols = 4 * D + 1
        U = n.buf(ctx, "u1", [P, TILES, cols], F16)
        lo = [n.buf(ctx, f"lo1_{j}", [P, 2, D], F32) for j in range(RING)]
        dn = [n.buf(ctx, f"dn1_{j}", [P, 2, D], F32) for j in range(RING)]
        e = [n.buf(ctx, f"e1_{j}", [P, D], F32) for j in range(RING)]
        Y = n.buf(ctx, "y1", [P, TILES, D], F32)
        n.V(v.memset(U[:, :, cols - 1:cols], 1.0))
        wait(a, t_h)
        t = n.A(a.activation(s.T, s.H[:], ACT.Exp))
        wait(v, t)
        t = n.V(v.scalar_tensor_tensor(Y[:], s.H[:], 0.25, s.T, ALU.mult, ALU.mult))
        split16(n, s.T, U, 0, t)
        split16(n, Y[:], U, 2 * D, t)

        def finish(i, j, p_, t):
            tile = bass.ds(RING * i + j, 1)
            sums = p_[:, 0:4 * D].rearrange("p (w h d) -> p w h d", w=2, h=2)
            wait(a, t)
            t = n.A(a.activation(lo[j][:], sums[:, :, 1, :], ACT.Copy, scale=1.0 / LO))
            wait(v, t)
            t = n.V(v.tensor_tensor(dn[j][:], lo[j][:], sums[:, :, 0, :], ALU.add))
            n.free.by(v.tensor_copy(s.ideg[:, tile], p_[:, cols - 1:cols]))
            wait(v, t)
            n.V(v.tensor_scalar(e[j][:], dn[j][:, 0, :], 0.5, EPS_MSG, ALU.is_gt, ALU.mult))
            t = n.V(v.tensor_scalar(lo[j][:, 0, :], dn[j][:, 0, :], 0.5, None, ALU.max))
            wait(v, t)
            t = n.V(v.reciprocal(lo[j][:, 0, :], lo[j][:, 0, :]))
            wait(v, t)
            t = n.V(v.scalar_tensor_tensor(dn[j][:, 1, :], dn[j][:, 1, :], 4.0, lo[j][:, 0, :], ALU.mult, ALU.mult))
            wait(v, t)
            t = n.V(v.tensor_tensor(dn[j][:, 1, :], dn[j][:, 1, :], e[j][:], ALU.add))
            wait(v, t)
            n.V(v.tensor_tensor(s.T[:, tile, :], dn[j][:, 1, :].unsqueeze(1), s.H[:, tile, :], ALU.add))

        n.meet(v, a, n.pe)
        body = aggregate(n, s, ps, False, U, cols, finish)
        with n.loop(BODIES, used=RING - 1, free=RING, done=RING, sv=7 * RING, sa=RING,
                    **{f"ring{r}": 16 for r in range(RING)}) as i:
            n.meet(v, a)
            body(i)
        n.meet(v, a, n.pe, n.pool)


def appnp_begin(n, s):
    v = n.v
    t_h = layernorm_relu(n, s)
    rs, rc, g = s.col
    wait(v, t_h)
    t = n.V(v.tensor_scalar(rs[:], s.odeg[:, 0:TILES], 1.0, None, ALU.max))
    t = n.V(v.tensor_scalar(rc[:], s.ideg[:], 1.0, None, ALU.max))
    inv_sqrt(n, rs, rs, t)
    t = inv_sqrt(n, rc, rc, t)
    wait(v, t)
    n.V(v.scalar_tensor_tensor(g[:], rs[:], BETA, rc[:], ALU.mult, ALU.mult))
    t = n.V(v.scalar_tensor_tensor(s.T, s.H[:], SCALE, over(rc[:], D), ALU.mult, ALU.mult))
    wait(v, t)
    return n.V(v.tensor_scalar(s.H[:], s.T, ALPHA, None, ALU.mult))


def appnp_end(n, s, u):
    v = n.v
    rc = s.col[1]
    t = n.V(v.reciprocal(rc[:], rc[:]))
    wait(v, t)
    t = n.V(v.scalar_tensor_tensor(s.T, u, 1.0 / (SCALE * THETA), over(rc[:], D), ALU.mult, ALU.mult))
    wait(v, t)
    n.V(v.tensor_tensor(s.X[:], s.X[:], s.T, ALU.add))
    n.meet(v, n.a, n.pe, n.pool)


def appnp_dense(n, s, ps):
    v, a, pe = n.v, n.a, n.pe
    t = appnp_begin(n, s)
    g = s.col[2]
    with ExitStack() as ctx:
        Ua = n.buf(ctx, "u2a", [P, TILES, 2 * D], F16)
        Ub = n.buf(ctx, "u2b", [P, TILES, 2 * D], F16)
        UF = n.buf(ctx, "u2f", [P, TILES, D], F32)
        lo = [n.buf(ctx, f"lo2_{j}", [P, D], F32) for j in range(RING)]
        z = [n.buf(ctx, f"z2_{j}", [P, D], F32) for j in range(RING)]
        uf = [n.buf(ctx, f"uf2_{j}", [P, D], F32) for j in range(RING)]
        res = [n.buf(ctx, f"r2_{j}", [P, D], F32) for j in range(RING)]
        split16(n, s.T, Ua, 0, t)

        def finish_into(Un):
            def finish(i, j, p_, t):
                tile = bass.ds(RING * i + j, 1)
                wait(a, t)
                t = n.A(a.activation(lo[j][:], p_[:, D:2 * D], ACT.Copy, scale=1.0 / LO))
                wait(v, t)
                t = n.free.by(v.tensor_tensor(z[j][:], lo[j][:], p_[:, 0:D], ALU.add))
                wait(v, t)
                t = n.V(v.scalar_tensor_tensor(uf[j][:], z[j][:], g[:, tile], s.H[:, tile, :].rearrange("p a d -> p (a d)"),
                                               ALU.mult, ALU.add))
                wait(a, t)
                n.A(a.activation(UF[:, tile, :], uf[j][:].unsqueeze(1), ACT.Copy))
                hi = Un[:, tile, 0:D].rearrange("p a d -> p (a d)")
                t = n.A(a.activation(hi, uf[j][:], ACT.Copy))
                wait(v, t)
                t = n.V(v.tensor_tensor(res[j][:], uf[j][:], hi, ALU.subtract))
                wait(a, t)
                n.A(a.activation(Un[:, tile, D:2 * D].rearrange("p a d -> p (a d)"), res[j][:], ACT.Copy, scale=LO))
            return finish

        per = dict(free=RING, done=RING, sv=2 * RING, sa=4 * RING,
                   **{f"ring{r}": 16 for r in range(RING)})
        with n.loop(STEPS // 2, **{k: 2 * BODIES * c for k, c in per.items()}):
            for U, Un in ((Ua, Ub), (Ub, Ua)):
                n.meet(pe)
                body = aggregate(n, s, ps, True, U, 2 * D, finish_into(Un))
                with n.loop(BODIES, **per) as i:
                    n.meet(v, a)
                    body(i)
        n.meet(v, a, pe, n.pool)
        appnp_end(n, s, UF[:])


def gcn_begin(n, s):
    v = n.v
    t_h = layernorm_relu(n, s)
    deg, dinv, g = s.col
    wait(v, t_h)
    t = n.V(v.tensor_scalar(deg[:], s.ideg[:], 1.0, None, ALU.add))
    t = inv_sqrt(n, dinv, deg, t)
    wait(v, t)
    n.V(v.tensor_scalar(g[:], dinv[:], 1.0 / SCALE, None, ALU.mult))


def gcn_dense(n, s, ps):
    v, a, pe = n.v, n.a, n.pe
    gcn_begin(n, s)
    _, dinv, g = s.col
    ring_per = dict(used=RING - 1, free=RING, done=RING, **{f"ring{r}": 16 for r in range(RING)})
    with ExitStack() as ctx:
        U = n.buf(ctx, "u3", [P, TILES, 3 * D], F16)
        UD = n.buf(ctx, "ud3", [P, TILES, D], F32)
        lo = [n.buf(ctx, f"lo3_{j}", [P, D], F32) for j in range(RING)]
        z = [n.buf(ctx, f"z3_{j}", [P, D], F32) for j in range(RING)]
        t = n.V(v.scalar_tensor_tensor(UD[:], s.H[:], SCALE, over(dinv[:], D), ALU.mult, ALU.mult))
        wait(v, t)
        t = n.V(v.tensor_copy(s.T, UD[:]))
        split16(n, s.T, U, 0, t)

        def close(i, j, t, scale):
            tile = bass.ds(RING * i + j, 1)
            wait(v, t)
            t = n.V(v.tensor_tensor(z[j][:], z[j][:], UD[:, tile, :].rearrange("p a d -> p (a d)"), ALU.add))
            wait(v, t)
            n.V(v.tensor_scalar(s.T[:, tile, :].rearrange("p a d -> p (a d)"), z[j][:], scale[:, tile], None, ALU.mult))

        def finish1(i, j, p_, t):
            wait(a, t)
            t = n.A(a.activation(lo[j][:], p_[:, D:2 * D], ACT.Copy, scale=1.0 / LO))
            wait(v, t)
            t = n.free.by(v.tensor_tensor(z[j][:], lo[j][:], p_[:, 0:D], ALU.add))
            close(i, j, t, g)

        n.meet(v, a, pe)
        body = aggregate(n, s, ps, False, U, 2 * D, finish1)
        with n.loop(BODIES, sv=2 * RING, sa=RING, **ring_per) as i:
            n.meet(v, a)
            body(i)
        n.meet(v, a, pe, n.pool)


def gcn_second_dense(n, s, ps):
    v, a, pe = n.v, n.a, n.pe
    _, dinv, _ = s.col
    ring_per = dict(used=RING - 1, free=RING, done=RING, **{f"ring{r}": 16 for r in range(RING)})
    with ExitStack() as ctx:
        U = n.buf(ctx, "u4", [P, TILES, 3 * D], BF16)
        UD = n.buf(ctx, "ud4", [P, TILES, D], F32)
        lo = [n.buf(ctx, f"lo4_{j}", [P, D], F32) for j in range(RING)]
        z = [n.buf(ctx, f"z4_{j}", [P, D], F32) for j in range(RING)]
        t = n.V(v.tensor_tensor(UD[:], s.H[:], over(dinv[:], D), ALU.mult))
        wait(v, t)
        t = n.V(v.tensor_copy(s.T, UD[:]))
        for part in range(3):
            o = U[:, :, part * D:(part + 1) * D]
            wait(a, t)
            t = n.A(a.activation(o, s.T, ACT.Copy))
            if part < 2:
                wait(v, t)
                t = n.V(v.tensor_tensor(s.T, s.T, o, ALU.subtract))

        def finish(i, j, p_, t):
            tile = bass.ds(RING * i + j, 1)
            wait(a, t)
            t = n.A(a.activation(lo[j][:], p_[:, 2 * D:3 * D], ACT.Copy))
            wait(v, t)
            t = n.V(v.tensor_tensor(z[j][:], lo[j][:], p_[:, D:2 * D], ALU.add))
            wait(v, t)
            t = n.free.by(v.tensor_tensor(z[j][:], z[j][:], p_[:, 0:D], ALU.add))
            wait(v, t)
            t = n.V(v.tensor_tensor(z[j][:], z[j][:], UD[:, tile, :].rearrange("p a d -> p (a d)"), ALU.add))
            wait(v, t)
            n.V(v.tensor_scalar(s.T[:, tile, :].rearrange("p a d -> p (a d)"), z[j][:], dinv[:, tile], None, ALU.mult))

        n.meet(v, a, pe)
        body = aggregate(n, s, ps, False, U, 3 * D, finish)
        with n.loop(BODIES, sv=3 * RING, sa=RING, **ring_per) as i:
            n.meet(v, a)
            body(i)
        n.meet(v, a, pe, n.pool)


class Store:
    pass


def add_to_x(n, s):
    def finish(i, j, p_, t):
        x = s.X[:, bass.ds(RING * i + j, 1), :].rearrange("p a d -> p (a d)")
        wait(n.v, t)
        return n.V(n.v.tensor_tensor(x, p_, x, ALU.add))
    return finish


def relu_to_h(n, s):
    def finish(i, j, p_, t):
        wait(n.a, t)
        return n.A(n.a.activation(s.H[:, bass.ds(RING * i + j, 1), :].rearrange("p a d -> p (a d)"), p_, ACT.Relu))
    return finish


def relu_add_to_x(n, s):
    def finish(i, j, p_, t):
        x = s.X[:, bass.ds(RING * i + j, 1), :].rearrange("p a d -> p (a d)")
        wait(n.v, t)
        return n.V(n.v.scalar_tensor_tensor(x, p_, 0.0, x, ALU.max, ALU.add))
    return finish


def split_q_keep_kv(n, s, kvall, qf):
    def finish(i, j, p_, t):
        tile = bass.ds(RING * i + j, 1)
        v, a = n.v, n.a
        wait(v, t, n.sv.now())
        n.V(v.tensor_copy(kvall[:, tile, :].rearrange("p a d -> p (a d)"), p_[:, D:3 * D]))
        t_read = n.V(v.tensor_copy(qf[:], p_[:, 0:D]))
        t = t_read
        for part in range(3):
            o = s.q3[:, tile, part, :].rearrange("p a d -> p (a d)")
            wait(v, t)
            t = n.V(v.tensor_copy(o, qf[:]))
            if part < 2:
                wait(v, t)
                t = n.V(v.tensor_tensor(qf[:], qf[:], o, ALU.subtract))
        return t_read
    return finish


def gnn(nc, x_in, src_in, dst_in, qw, kw, vw, w1, b1, w31, b31, w32, b32, out):
    with ExitStack() as top:
        n = Net(nc, top)
        v, a, pe, pool, sp = n.v, n.a, n.pe, n.pool, n.sp
        s = Store()
        s.kv_d = nc.dram_tensor("kv_rows", [NODES, 2 * D], F32).ap()
        s.c_d = nc.dram_tensor("adjacency", [BTILES, P, WIDE], U8).ap()
        s.t_d = nc.dram_tensor("adjacency_t", [BTILES, P, WIDE], U8).ap()
        s.X = n.buf(top, "X", [P, TILES, D], F32)
        s.H = n.buf(top, "H", [P, TILES, D], F32)
        s.R = n.buf(top, "T", [P, BTILES, D], F32)
        s.T = s.R[:, 0:TILES, :]
        s.ident = n.buf(top, "ident", [P, P], F32)
        s.identb = n.buf(top, "identb", [P, P], BF16)
        s.count1 = n.buf(top, "count1", [P, GROUP], BF16)
        s.tri = n.buf(top, "tri", [P, P], BF16)
        s.ones = n.buf(top, "ones", [P, P], F32)
        s.odeg = n.buf(top, "odeg", [P, BTILES], F32)
        s.ideg = n.buf(top, "ideg", [P, TILES], F32)
        s.most = n.buf(top, "most_all", [P, 1], F32)
        s.full = n.buf(top, "full", [P, 1], F32)
        fits = n.buf(top, "fits", [1, 1], I32)
        s.filled = n.buf(top, "filled", [1, 1], F32)
        s.col = [n.buf(top, f"col{i}", [P, TILES], F32) for i in range(3)]
        s.stage = n.buf(top, "stage", [P, RING, D], F32)
        s.aT = n.buf(top, "aT", [P, RING * P], F32)
        wq = n.buf(top, "wq", [D, 3 * D], F32)
        wl = [n.buf(top, f"wl{i}", [D + 1, D], F32) for i in range(3)]

        t = n.V(v.memset(s.X[:, TILES - 1, :], 0.0))
        for i, w in enumerate((qw, kw, vw)):
            sp.dma_start(wq[:, i * D:(i + 1) * D], w).then_inc(n.ld.sem, 16)
        for b_, w, bias in zip(wl, (w1, w31, w32), (b1, b31, b32)):
            sp.dma_start(b_[0:D, :], w).then_inc(n.ld.sem, 16)
            sp.dma_start(b_[D:D + 1, :], bias.rearrange("(a n) -> a n", a=1)).then_inc(n.ld.sem, 16)
        sp.dma_start(s.X[:, 0:TILES - 1, :],
                     x_in[0:NODES - LAST, :].rearrange("(k p) f -> p k f", p=P)).then_inc(n.ld.sem, 16)
        wait(sp, t)
        sp.dma_start(s.X[0:LAST, TILES - 1, :], x_in[NODES - LAST:NODES, :]).then_inc(n.ld.sem, 16)
        n.ld.count += 16 * 11
        t_loaded = n.ld.now()

        n.G(pool.memset(s.ones[:], 1.0))
        n.G(pool.memset(s.ident[:], 0.0))
        t = n.G(pool.iota(s.count1[:], [[1, GROUP]], base=1, channel_multiplier=0,
                          allow_small_or_imprecise_dtypes=True))
        wait(pool, t)
        n.G(pool.affine_select(out=s.ident[:], in_=s.ident[:], compare_op=ALU.not_equal, fill=1.0, base=0,
                               pattern=[[-1, P]], channel_multiplier=1))
        t_const = n.G(pool.affine_select(out=s.tri[:], in_=s.ones[:], compare_op=ALU.is_gt, fill=0.0, base=0,
                                         pattern=[[1, P]], channel_multiplier=-1))
        wait(v, t_const, t_loaded)
        n.V(v.tensor_copy(s.identb[:], s.ident[:]))
        n.V(v.memset(s.aT[D:D + 1, :], 1.0))
        wait(pe, t_const, t_loaded)
        wait(a, t_loaded)

        layernorm_relu(n, s)
        with ExitStack() as ctx:
            s.q3 = n.buf(ctx, "q3", [P, BTILES, 3, D], BF16)
            s.slots = n.buf(ctx, "slots", [P, 2, BTILES, GROUPS], F32)
            s.idx = n.buf(ctx, "idx", [P, BTILES, GROUPS], I32)
            s.slotmax = n.buf(ctx, "slotmax", [P, BTILES * GROUPS], BF16)
            n.V(v.memset(s.q3[:, TILES:BTILES, :, :], 0.0))
            n.V(v.memset(s.slots[:, :, TILES:BTILES, :], 0.0))
            with ExitStack() as c2:
                kvall = n.buf(c2, "kvall", [P, TILES, 2 * D], F32)
                qf = n.buf(c2, "qf", [P, D], F32)
                linear(n, s, "qkv", s.H, wq, 3 * D, False, split_q_keep_kv(n, s, kvall, qf),
                       sv=7 * RING, sa=3, se=2 * RING)
                wait(sp, n.sv.now())
                sp.dma_start(s.kv_d[0:NODES - LAST, :].rearrange("(k p) f -> p k f", p=P),
                             kvall[:, 0:TILES - 1, :]).then_inc(n.ld.sem, 16)
                sp.dma_start(s.kv_d[NODES - LAST:NODES, :], kvall[0:LAST, TILES - 1, :]).then_inc(n.ld.sem, 16)
                n.ld.count += 32
                for e in (v, pool, sp, a):
                    wait(e, n.ld.now())
            bucket_edges(n, s, src_in, dst_in)
            attention_and_adjacency(n, s)
        with ExitStack() as ctx:
            pf = n.bank(ctx, "pf")
            high = n.buf(ctx, "high", [1, 1], F32)
            wait(pe, n.sv.now())
            t = n.E(pe.matmul(pf[0:1, 0:P], s.most[:], s.ident[:], start=True, stop=True))
            wait(v, t)
            t = n.V(v.tensor_reduce(high[:], pf[0:1, 0:P], AX.X, ALU.max))
            wait(v, t)
            t = n.V(v.tensor_scalar(high[:], high[:], EXACT, None, ALU.is_le))
            wait(v, t)
            t = n.V(v.tensor_scalar(s.filled[:], s.filled[:], float(EDGES), None, ALU.is_equal))
            wait(v, t)
            t = n.V(v.tensor_tensor(fits[:], s.filled[:], high[:], ALU.mult))
            for e in (v, a, pe, pool, sp):
                wait(e, t)
            dense = nc.values_load(fits[0:1, 0:1], min_val=0, max_val=1)
            n.meet(v, a, pe, pool, sp)
        before = [sig.count for _, sig in n.sigs]
        with nc.If(dense > 0):
            dense_layers(n, s, wl, out)
        for (_, sig), count in zip(n.sigs, before):
            sig.count = count
        with nc.Else():
            edge_layers(n, s, wq, wl, src_in, dst_in, out)


def add_attention(n, s):
    t = n.V(n.v.tensor_tensor(s.X[:], s.X[:], s.H[:], ALU.add))
    wait(n.v, t)
    n.V(n.v.tensor_tensor(s.X[:], s.X[:], s.T, ALU.add))


def store_x(n, s, out):
    wait(n.sp, n.sv.now())
    n.sp.dma_start(out[0:NODES - LAST, :].rearrange("(k p) f -> p k f", p=P),
                   s.X[:, 0:TILES - 1, :]).then_inc(n.ld.sem, 16)
    n.sp.dma_start(out[NODES - LAST:NODES, :], s.X[0:LAST, TILES - 1, :]).then_inc(n.ld.sem, 16)
    n.ld.count += 32
    wait(n.sp, n.ld.now())


def dense_layers(n, s, wl, out):
    add_attention(n, s)
    with ExitStack() as ctx:
        s.ring = n.buf(ctx, "ring", [P, RING, PANEL], U8)
        with ExitStack() as banks:
            ps = [n.bank(banks, f"sum1_{j}") for j in range(RING)]
            softmax_dense(n, s, ps)
        linear(n, s, "l1", s.T, wl[0], D, True, add_to_x(n, s), sv=RING, sa=3, se=2 * RING)
        with ExitStack() as banks:
            ps = [n.bank(banks, f"sum2_{j}") for j in range(RING)]
            appnp_dense(n, s, ps)
            gcn_dense(n, s, ps)
        linear(n, s, "l3a", s.T, wl[1], D, True, relu_to_h(n, s), sa=3 + RING, se=2 * RING)
        with ExitStack() as banks:
            ps = [n.bank(banks, f"sum3_{j}") for j in range(RING)]
            gcn_second_dense(n, s, ps)
        linear(n, s, "l3b", s.T, wl[2], D, True, relu_add_to_x(n, s), sv=RING, sa=3, se=2 * RING)
    store_x(n, s, out)


class Edges:

    def __init__(self, n, s, ctx, src_in, dst_in):
        self.n, self.s = n, s
        self.src = n.buf(ctx, "e_src", [SCAN, COLS], I32)
        self.dst = n.buf(ctx, "e_dst", [SCAN, COLS], I32)
        self.ix = n.buf(ctx, "e_ix", [SCAN, 2], I32)
        self.rel = n.buf(ctx, "e_rel", [SCAN, 1], F32)
        self.hot = n.buf(ctx, "e_hot", [SCAN, P], F32)
        self.count0 = n.buf(ctx, "e_count0", [SCAN, P], F32)
        self.row = n.buf(ctx, "e_row", [SCAN, 3 * D], F32)
        self.msg = n.buf(ctx, "e_msg", [SCAN, 2 * D + 1], F32)
        self.sc = n.buf(ctx, "e_sc", [SCAN, HEADS], F32)
        self.acc = n.buf(ctx, "e_acc", [P, TILES, 2 * D + 1], F32)
        self.ps = n.bank(ctx, "e_ps")
        self.m_d = n.nc.dram_tensor("e_pairs", [TILES * P, 2 * D + 1], F32).ap()
        self.u_d = n.nc.dram_tensor("e_rows", [TILES * P, D], F32).ap()
        for b, arr in ((self.src, src_in), (self.dst, dst_in)):
            n.sp.dma_start(b[:], arr.rearrange("(p e) -> p e", p=SCAN)).then_inc(n.ld.sem, 16)
        n.ld.count += 32
        n.V(n.v.tensor_scalar(self.count0[:], s.count1[0:SCAN, 0:P], 1.0, None, ALU.subtract))
        wait(n.v, n.ld.now())
        wait(n.pool, n.ld.now())

    def publish(self, table, rows):
        n = self.n
        n.meet(n.sp)
        n.sp.dma_start(table.rearrange("(k p) f -> p k f", p=P), rows).then_inc(n.ld.sem, 16)
        n.ld.count += 16
        for e in (n.v, n.a, n.pool):
            wait(e, n.ld.now())

    def sum(self, loads, key, width, message=None, **per):
        n, s = self.n, self.s
        v, a, pe, pool = n.v, n.a, n.pe, n.pool
        acc = self.acc[:, :, 0:width]
        n.meet(v, a, pe, pool)
        n.V(v.memset(acc, 0.0))
        per = {"sv": per.get("sv", 0) + 1 + 3 * TILES, "sa": per.get("sa", 0), "se": TILES,
               "sg": len(loads), "kv0": 16 * len(loads)}
        with n.loop(COLS, **{k: c for k, c in per.items() if c}) as e:
            n.meet(v, a, pe, pool)
            for m, (table, index, into) in enumerate(loads):
                t = n.G(pool.tensor_copy(self.ix[:, m:m + 1], index[:, bass.ds(e, 1)]))
                wait(pool, t)
                settle(pool, n.spare)
                n.kv[0].by(pool.indirect_dma_start(into, None, table, bass.IndirectOffsetOnAxis(
                    ap=self.ix[:, m:m + 1], axis=0)), 16)
            n.V(v.tensor_copy(self.rel[:], key[:, bass.ds(e, 1)]))
            wait(v, n.kv[0].now())
            wait(a, n.kv[0].now())
            wait(pe, n.kv[0].now())
            if message is not None:
                message()
            with n.loop(TILES, sv=3, se=1) as b:
                n.meet(v, pe)
                t = n.V(v.tensor_scalar(self.hot[:], self.count0[:], self.rel[:], None, ALU.is_equal))
                wait(pe, t)
                tp = n.E(pe.matmul(self.ps[:, 0:width], self.hot[:], self.msg[:, 0:width], start=True, stop=True))
                wait(v, t)
                n.V(v.tensor_scalar(self.rel[:], self.rel[:], float(P), None, ALU.subtract))
                wait(v, tp)
                part = acc[:, bass.ds(b, 1), :].rearrange("p a d -> p (a d)")
                n.V(v.tensor_tensor(part, part, self.ps[:, 0:width], ALU.add))
        n.meet(v, a, pe, pool)


def edge_layers(n, s, wq, wl, src_in, dst_in, out):
    v, a, nc = n.v, n.a, n.nc
    with ExitStack() as ctx:
        qkv = n.buf(ctx, "e_all", [P, TILES, 3 * D], F32)

        def keep(i, j, p_, t):
            wait(a, t)
            return n.A(a.activation(qkv[:, bass.ds(RING * i + j, 1), :].rearrange("p a d -> p (a d)"), p_, ACT.Copy))

        linear(n, s, "e_qkv_lin", s.H, wq, 3 * D, False, keep, sa=3 + RING, se=2 * RING)
        q_d = nc.dram_tensor("e_qkv", [TILES * P, 3 * D], F32).ap()
        n.meet(n.sp)
        n.sp.dma_start(q_d.rearrange("(k p) f -> p k f", p=P), qkv[:]).then_inc(n.ld.sem, 16)
        n.ld.count += 16
        for e in (v, a, n.sp, n.pool):
            wait(e, n.ld.now())
    with ExitStack() as ctx:
        E = Edges(n, s, ctx, src_in, dst_in)
        E.q_d = q_d
        kv = n.buf(ctx, "e_kv", [SCAN, 3 * D], F32)
        wide = n.buf(ctx, "e_wide", [P, TILES, 2 * D + 1], F32)

        def attend():
            q, k, val = E.row[:, 0:D], kv[:, D:2 * D], kv[:, 2 * D:3 * D]
            t = n.V(v.tensor_tensor(E.msg[:, 0:D], q, k, ALU.mult))
            wait(v, t)
            t = n.V(v.tensor_reduce(E.sc[:], E.msg[:, 0:D].rearrange("p (h d) -> p h d", d=DH), AX.X, ALU.add))
            wait(v, t)
            t = n.V(v.tensor_scalar(E.sc[:], E.sc[:], 10.0, -10.0, ALU.min, ALU.max))
            wait(a, t)
            t = n.A(a.activation(E.msg[:, D:D + HEADS], E.sc[:], ACT.Exp))
            n.V(v.memset(E.msg[:, D + HEADS:AV], 1.0))
            wait(v, t)
            n.V(v.tensor_tensor(E.msg[:, 0:D].rearrange("p (h d) -> p h d", d=DH),
                                val.rearrange("p (h d) -> p h d", d=DH), over(E.msg[:, D:D + HEADS], DH), ALU.mult))

        E.sum([(E.q_d, E.src, E.row[:]), (E.q_d, E.dst, kv[:])], E.src, AV, attend, sv=5, sa=1)
        den = wide[:, :, 0:HEADS]
        t = n.V(v.tensor_scalar(den, E.acc[:, :, D:D + HEADS], EPS_ATT, None, ALU.add))
        wait(v, t)
        t = n.V(v.reciprocal(den, den))
        wait(v, t)
        for h in range(HEADS):
            t = n.V(v.tensor_tensor(s.T[:, :, h * DH:(h + 1) * DH], E.acc[:, :, h * DH:(h + 1) * DH],
                                    den[:, :, h:h + 1].to_broadcast([P, TILES, DH]), ALU.mult))
        n.V(v.tensor_copy(s.odeg[:, 0:TILES], E.acc[:, :, AV - 1]))
        wait(v, t)
        add_attention(n, s)

        t = layernorm_relu(n, s)
        wait(a, t)
        t = n.A(a.activation(wide[:, :, 0:D], s.H[:], ACT.Exp))
        wait(v, t)
        n.V(v.tensor_tensor(wide[:, :, D:2 * D], s.H[:], wide[:, :, 0:D], ALU.mult))
        n.V(v.memset(wide[:, :, 2 * D:2 * D + 1], 1.0))
        E.publish(E.m_d, wide[:])
        E.sum([(E.m_d, E.src, E.msg[:])], E.dst, 2 * D + 1)
        e, m = wide[:, :, 0:D], wide[:, :, D:2 * D]
        den, num = E.acc[:, :, 0:D], E.acc[:, :, D:2 * D]
        n.V(v.tensor_scalar(e, den, 0.5, EPS_MSG, ALU.is_gt, ALU.mult))
        t = n.V(v.tensor_scalar(m, den, 0.5, None, ALU.max))
        wait(v, t)
        t = n.V(v.reciprocal(m, m))
        wait(v, t)
        t = n.V(v.tensor_tensor(m, m, num, ALU.mult))
        wait(v, t)
        t = n.V(v.tensor_tensor(m, m, e, ALU.add))
        wait(v, t)
        n.V(v.tensor_tensor(s.T, m, s.H[:], ALU.add))
        n.V(v.tensor_copy(s.ideg[:], E.acc[:, :, 2 * D]))
        linear(n, s, "e_l1", s.T, wl[0], D, True, add_to_x(n, s), sv=RING, sa=3, se=2 * RING)

        appnp_begin(n, s)
        with n.loop(STEPS, sv=1 + COLS * (1 + 3 * TILES) + 2, se=COLS * TILES, sg=COLS, kv0=16 * COLS, ld=16):
            E.publish(E.u_d, s.T)
            E.sum([(E.u_d, E.dst, E.msg[:, 0:D])], E.src, D)
            t = n.V(v.tensor_tensor(s.T, E.acc[:, :, 0:D], over(s.col[2][:], D), ALU.mult))
            wait(v, t)
            n.V(v.tensor_tensor(s.T, s.T, s.H[:], ALU.add))
        n.meet(v)
        appnp_end(n, s, s.T)

        gcn_begin(n, s)
        dinv = s.col[1]
        for name, w, finish, per in (("e_l3a", wl[1], relu_to_h, dict(sa=3 + RING)),
                                     ("e_l3b", wl[2], relu_add_to_x, dict(sv=RING, sa=3))):
            n.meet(v)
            t = n.V(v.tensor_tensor(s.T, s.H[:], over(dinv[:], D), ALU.mult))
            E.publish(E.u_d, s.T)
            E.sum([(E.u_d, E.src, E.msg[:, 0:D])], E.dst, D)
            t = n.V(v.tensor_tensor(s.T, s.T, E.acc[:, :, 0:D], ALU.add))
            wait(v, t)
            n.V(v.tensor_tensor(s.T, s.T, over(dinv[:], D), ALU.mult))
            linear(n, s, name, s.T, w, D, True, finish(n, s), se=2 * RING, **per)
    store_x(n, s, out)


_INS = ["x", "src", "dst", "L0_gnn_qW", "L0_gnn_kW", "L0_gnn_vW", "L1_gnn_W", "L1_gnn_b",
        "L3_gnn_W1", "L3_gnn_b1", "L3_gnn_W2", "L3_gnn_b2"]
_OUTS = [((NODES, D), "float32")]


def kernel(**inputs):
    import numpy as np
    import concourse.bacc as bacc
    from concourse.bass_utils import run_bass_kernel_spmd as run

    nc = bacc.Bacc("TRN2", target_bir_lowering=False, num_devices=1)
    arrays, args = {}, []
    for name in _INS:
        arr = np.ascontiguousarray(inputs[name])
        arrays[f"in_{name}_dram"] = arr
        args.append(nc.dram_tensor(f"in_{name}_dram", arr.shape, mybir.dt.from_np(arr.dtype), kind="ExternalInput").ap())
    for i, (shape, dtype) in enumerate(_OUTS):
        args.append(nc.dram_tensor(f"out_{i}_dram", shape, mybir.dt.from_np(np.dtype(dtype)), kind="ExternalOutput").ap())
    gnn(nc, *args)
    r = run(nc, [arrays], core_ids=[0])
    return r.results[0]["out_0_dram"]
```

```python
from contextlib import ExitStack, contextmanager

import concourse.bass as bass
from concourse import mybir

ALU = mybir.AluOpType
ACT = mybir.ActivationFunctionType
AX = mybir.AxisListType
F32, F16, BF16, F8 = mybir.dt.float32, mybir.dt.float16, mybir.dt.bfloat16, mybir.dt.float8e4
I32, U8 = mybir.dt.int32, mybir.dt.uint8

P = 128
NODES, EDGES, D, HEADS = 6250, 100000, 96, 4
DH = D // HEADS
TILES = -(-NODES // P)
LAST = NODES - (TILES - 1) * P
GROUP = 2 * P
GROUPS = -(-NODES // GROUP)
WIDE = GROUPS * GROUP
PAIRS = (TILES + 1) // 2
BTILES = 2 * PAIRS
RUN = 36
CAP = P * RUN
SCAN = 125
COLS = EDGES // SCAN
CHUNK = 5
CHUNKS = GROUPS // CHUNK
AV = D + HEADS + 1
RING = 7
BODIES = TILES // RING
PANEL = TILES * P
LO = 2048.0
SCALE = 64.0
EXACT = 16.0
EPS_LN, EPS_ATT, EPS_MSG = 1e-5, 1e-8, 1e-7
STEPS, ALPHA, BETA = 10, 0.1, 0.9
THETA = BETA ** STEPS + ALPHA * sum(BETA ** i for i in range(STEPS))


class Sig:

    def __init__(self, ctx, nc, name):
        self.sem = ctx.enter_context(nc.semaphore(name))
        self.count = 0
        self.frames = []

    def now(self, more=0):
        value = self.count + more
        for i, per in self.frames:
            if per:
                value = i * per + value
        return self, value

    def by(self, ins, n=1):
        ins.then_inc(self.sem, n)
        self.count += n
        return self.now()


def wait(eng, *tokens):
    for sig, value in tokens:
        if not isinstance(value, int) or value > 0:
            eng.wait_ge(sig.sem, value)


def settle(eng, spare):
    eng.sem_inc(spare.sem, 1)


class Net:
    def __init__(self, nc, ctx):
        self.nc = nc
        self.v, self.a, self.pe, self.pool, self.sp = nc.vector, nc.scalar, nc.tensor, nc.gpsimd, nc.sync
        self.sigs = []

        def sig(name):
            self.sigs.append((name, Sig(ctx, nc, name)))
            return self.sigs[-1][1]

        self.sv, self.sa, self.se, self.sg = sig("sv"), sig("sa"), sig("se"), sig("sg")
        self.ld = sig("ld")
        self.eg = sig("eg")
        self.kv = [sig("kv0"), sig("kv1")]
        self.row = sig("row")
        self.spare = Sig(ctx, nc, "spare")
        self.used = sig("used")
        self.free = sig("free")
        self.done = sig("done")
        self.ring = [sig(f"ring{r}") for r in range(RING)]
        for s, start in ((self.se, 1), (self.used, RING - 1), (self.free, RING),
                         (self.done, RING)):
            self.pe.sem_inc(s.sem, start)
            s.count = start

    def buf(self, ctx, name, shape, dt):
        return ctx.enter_context(self.nc.sbuf_tensor(name, shape, dt))

    def bank(self, ctx, name, dt=F32):
        return ctx.enter_context(self.nc.psum_tensor(name, [P, 2048 // mybir.dt.size(dt)], dt))

    def V(self, ins):
        return self.sv.by(ins)

    def A(self, ins):
        return self.sa.by(ins)

    def E(self, ins):
        return self.se.by(ins)

    def G(self, ins):
        return self.sg.by(ins)

    def meet(self, *engines):
        own = [(self.v, self.sv), (self.a, self.sa), (self.pe, self.se), (self.pool, self.sg)]
        for e in engines:
            for _, s in own:
                wait(e, s.now())

    @contextmanager
    def loop(self, trips, **per):
        start = {n: s.count for n, s in self.sigs}
        if self.se.frames:
            for e in (self.v, self.a, self.pe, self.pool, self.sp):
                settle(e, self.spare)
        with self.nc.Fori(0, trips) as i:
            for n, s in self.sigs:
                s.frames.append((i, per.get(n, 0)))
            yield i
        found = {n: s.count - start[n] for n, s in self.sigs if s.count != start[n]}
        if found != per:
            raise ValueError(f"increments in one pass: {found}")
        for n, s in self.sigs:
            s.frames.pop()
            s.count = start[n] + trips * per.get(n, 0)


def over(ap, n):
    return ap.unsqueeze(2).to_broadcast([ap.shape[0], ap.shape[1], n])


def under(ap, n):
    return ap.unsqueeze(1).to_broadcast([ap.shape[0], n, ap.shape[1]])


def layernorm_relu(n, s):
    v, a = n.v, n.a
    m, var, rstd = s.col
    n.meet(v, a)
    t = n.V(v.tensor_reduce(m[:], s.X[:], AX.X, ALU.add))
    wait(v, t)
    t = n.V(v.tensor_scalar(m[:], m[:], 1.0 / D, None, ALU.mult))
    wait(v, t)
    t = n.V(v.tensor_tensor(s.H[:], s.X[:], over(m[:], D), ALU.subtract))
    wait(a, t)
    t = n.A(a.square(s.T, s.H[:]))
    wait(v, t)
    t = n.V(v.tensor_reduce(var[:], s.T, AX.X, ALU.add))
    wait(v, t)
    t = n.V(v.tensor_scalar(var[:], var[:], 1.0 / D, EPS_LN, ALU.mult, ALU.add))
    t = inv_sqrt(n, rstd, var, t)
    wait(v, t)
    return n.V(v.scalar_tensor_tensor(s.H[:], s.H[:], 0.0, over(rstd[:], D), ALU.max, ALU.mult))


def inv_sqrt(n, y, x, t):
    wait(n.a, t)
    t = n.A(n.a.sqrt(y[:], x[:]))
    wait(n.v, t)
    return n.V(n.v.reciprocal(y[:], y[:]))


def linear(n, s, name, src, w, cols, bias, finish, **per):
    a, pe = n.a, n.pe
    rows_in = D + 1 if bias else D
    n.meet(n.v, a, pe, n.pool)
    with ExitStack() as ctx:
        tr = [n.bank(ctx, f"{name}_tr{i}") for i in range(2)]
        mm = [n.bank(ctx, f"{name}_mm{i}") for i in range(4)]

        def stage(i):
            n.A(a.activation(s.stage[:], src[:, bass.ds(RING * i, RING), :], ACT.Copy))

        def body(i, more):
            wait(pe, n.sa.now(), n.sv.now())
            before = n.se.now()
            moved = []
            for j in range(RING):
                t = n.E(pe.transpose(tr[j // 4][0:D, (j % 4) * P:(j % 4 + 1) * P], s.stage[:, j, :], s.ident[:]))
                if j in (3, RING - 1):
                    wait(a, before, t)
                    moved.append(n.A(a.activation(s.aT[0:D, (j // 4) * 4 * P:(j + 1) * P],
                                                  tr[j // 4][0:D, 0:(j % 4 + 1) * P], ACT.Copy)))
            if more:
                stage(i + 1)
            ends = []
            for j in range(RING):
                if j in (0, 4):
                    wait(pe, moved[j // 4])
                if j >= 4:
                    wait(pe, ends[j - 4])
                o = mm[j % 4][:, 0:cols]
                t = n.E(pe.matmul(o, s.aT[0:rows_in, j * P:(j + 1) * P], w[0:rows_in, 0:cols], start=True, stop=True))
                ends.append(finish(i, j, o, t))

        stage(0)
        with n.loop(BODIES - 1, **per) as i:
            body(i, True)
        body(BODIES - 1, False)
    n.meet(n.v, a, pe, n.pool)


def load_edges(n, s, src_in, dst_in):
    v, pe, sp = n.v, n.pe, n.sp
    with ExitStack() as ctx:
        dall = n.buf(ctx, "dall", [SCAN, COLS], I32)
        below = n.buf(ctx, "below", [SCAN, GROUPS], F32)
        junk = n.buf(ctx, "junk", [SCAN, COLS], BF16)
        first_f = n.buf(ctx, "first_f", [1, GROUPS], F32)
        first = n.buf(ctx, "first", [1, GROUPS], I32)
        pc = n.bank(ctx, "pc")
        sp.dma_start(dall[:], dst_in.rearrange("(p e) -> p e", p=SCAN)).then_inc(n.eg.sem, 16)
        n.eg.count += 16
        wait(v, n.eg.now())
        for g in range(GROUPS):
            t = n.V(v.tensor_scalar(junk[:], dall[:], float(g * GROUP), None, ALU.is_lt, ALU.add,
                                    accum_out=below[:, g:g + 1]))
            wait(v, t)
        wait(pe, t)
        t = n.E(pe.matmul(pc[0:1, 0:GROUPS], s.ones[0:SCAN, 0:1], below[:], start=True, stop=True))
        wait(v, t)
        t = n.V(v.tensor_scalar(first_f[:], pc[0:1, 0:GROUPS], float(EDGES - CAP), None, ALU.min))
        wait(v, t)
        t = n.V(v.tensor_copy(first[:], first_f[:]))
        wait(sp, t)
        for g in range(GROUPS):
            at = sp.value_load(first[0:1, g:g + 1], min_val=0, max_val=EDGES - CAP)
            for buf_, arr in ((s.es, src_in), (s.ed, dst_in)):
                sp.dma_start(buf_[:, g, :], arr[bass.ds(at, CAP)].rearrange("(p r) -> p r", p=P)).then_inc(n.eg.sem, 16)
        n.eg.count += 32 * GROUPS
    return n.eg.now()


def bucket_edges(n, s):
    v, a, pe, pool = n.v, n.a, n.pe, n.pool
    with ExitStack() as ctx:
        ti = n.buf(ctx, "ti", [P, GROUPS, RUN], I32)
        base = n.buf(ctx, "base", [P, GROUPS], F32)
        valid = n.buf(ctx, "valid", [P, GROUPS, RUN], F32)
        tile1 = n.buf(ctx, "tile1", [P, GROUPS, RUN], F32)
        sloc = n.buf(ctx, "sloc", [P, GROUPS, RUN], F32)
        dloc = n.buf(ctx, "dloc", [P, GROUPS, RUN], F32)
        keep = n.buf(ctx, "keep", [P, TILES, RUN + 1], BF16)
        bt = [n.buf(ctx, f"bt{k}", [P, TILES, RUN + 1], BF16) for k in range(2)]
        seen = n.buf(ctx, "seen", [P, TILES, RUN + 1], BF16)
        vals = [n.buf(ctx, f"vals{k}", [P, RUN, 2, TILES], BF16) for k in range(2)]
        prod = n.buf(ctx, "prod", [P, TILES, RUN], BF16)
        rank = n.buf(ctx, "rank", [P, RUN], F32)
        onerank = n.buf(ctx, "onerank", [P, RUN, P], BF16)
        pc = n.bank(ctx, "pc2")
        pp = [n.bank(ctx, f"pp{k}") for k in range(2)]
        po = n.bank(ctx, "po")

        t = n.G(pool.iota(base[:], [[GROUP, GROUPS]], base=0, channel_multiplier=0,
                          allow_small_or_imprecise_dtypes=True))
        wait(v, t)
        t = n.V(v.memset(keep[:], 1.0))
        wait(v, t)
        n.V(v.memset(keep[:, :, 0:1], 0.0))
        t = n.V(v.tensor_tensor(dloc[:], s.ed[:], over(base[:], RUN), ALU.subtract))
        wait(v, t)
        t = n.V(v.tensor_scalar(valid[:], dloc[:], float(GROUP - 1), None, ALU.is_le))
        wait(v, t)
        t = n.V(v.scalar_tensor_tensor(valid[:], dloc[:], 0.0, valid[:], ALU.is_ge, ALU.mult))
        wait(v, t)
        n.V(v.tensor_scalar(dloc[:], dloc[:], 1.0, None, ALU.add))
        t = n.V(v.tensor_scalar(ti[:], s.es[:], P - 1, None, ALU.bitwise_and))
        wait(v, t)
        t = n.V(v.tensor_scalar(sloc[:], ti[:], 1.0, None, ALU.add))
        wait(v, t)
        t = n.V(v.tensor_scalar(ti[:], s.es[:], 7, None, ALU.logical_shift_right))
        wait(v, t)
        t = n.V(v.scalar_tensor_tensor(tile1[:], ti[:], 1.0, valid[:], ALU.add, ALU.mult))
        n.meet(v, a, pe, pool)

        flat = "p k r -> p (k r)"

        def count(g, k):
            of_g = bass.ds(g, 1)
            n.meet(pool)
            wait(v, n.sv.now(), n.sg.now(), n.sa.now(-1))
            t = n.V(v.tensor_tensor(bt[k][:, :, 1:RUN + 1], over(s.count1[:, 0:TILES], RUN),
                                    under(tile1[:, of_g, :].rearrange("p g r -> p (g r)"), TILES), ALU.is_equal))
            wait(pool, t)
            for i, val in enumerate((sloc, dloc)):
                t_vals = n.G(pool.tensor_tensor(vals[k][:, :, i, :], bt[k][:, :, 1:RUN + 1].rearrange("p k r -> p r k"),
                                                over(val[:, of_g, :].rearrange("p g r -> p (g r)"), TILES), ALU.mult))
            wait(pe, t, n.sa.now())
            for r in range(RUN):
                t = pe.matmul(pp[k][:, 0:TILES], s.tri[:], bt[k][:, :, 1 + r], start=r == 0, stop=r == RUN - 1)
            t = n.E(t)
            wait(a, t)
            return t_vals, n.A(a.activation(bt[k][:, :, 0], pp[k][:, 0:TILES], ACT.Copy))

        def place(g, k, t_vals, t_before, later=1):
            wait(v, t_before, n.sv.now(), n.se.now(-later))
            t = n.V(v.tensor_tensor_scan(seen[:].rearrange(flat), keep[:].rearrange(flat), bt[k][:].rearrange(flat), 0.0,
                                         ALU.mult, ALU.add))
            wait(v, t)
            t = n.V(v.tensor_tensor(prod[:], seen[:, :, 1:RUN + 1], bt[k][:, :, 1:RUN + 1], ALU.mult))
            wait(v, t)
            t = n.V(v.tensor_reduce(rank[:], prod[:].rearrange("p k r -> p r k"), AX.X, ALU.add))
            wait(v, t)
            for r in range(RUN):
                t = n.V(v.tensor_scalar(onerank[:, r, :], s.count1[:, 0:P], rank[:, r:r + 1], None, ALU.is_equal))
                if r == 0:
                    wait(pe, t_vals, n.sa.now(-later))
                wait(pe, t)
                te = n.E(pe.matmul(po[:, 0:2 * TILES], onerank[:, r, :], vals[k][:, r, :, :].rearrange("p i k -> p (i k)"),
                                   start=r == 0, stop=r == RUN - 1))
            wait(a, te)
            n.A(a.activation(s.slots[:, :, 0:TILES, bass.ds(g, 1)],
                             po[:, 0:2 * TILES].rearrange("p (i k) -> p i k", i=2).unsqueeze(3), ACT.Copy))

        count(0, 0)
        with n.loop((GROUPS - 1) // 2, sv=2 * (4 + RUN), sg=4, se=2 * (1 + RUN), sa=4) as i:
            was = n.sg.now(), n.sa.now()
            now = count(2 * i + 1, 1)
            place(2 * i, 0, *was)
            count(2 * i + 2, 0)
            place(2 * i + 1, 1, *now)
        place(GROUPS - 1, 0, n.sg.now(), n.sa.now(), later=0)
        n.meet(v, a, pe, pool)
        t = n.V(v.tensor_scalar(base[:], base[:], -1.0, None, ALU.add))
        wait(v, t)
        n.V(v.scalar_tensor_tensor(s.idx[:], s.slots[:, 1, :, :], 1.0,
                                   under(base[:], BTILES), ALU.max, ALU.add))
        t = n.V(v.tensor_scalar(s.slotmax[:], s.slots[:, 0, :, :].rearrange("p k g -> p (k g)"), 0.5, None,
                                ALU.is_gt, ALU.add, accum_out=s.full[:]))
        wait(pe, t)
        t = n.E(pe.matmul(pc[0:1, 0:1], s.ones[:, 0:1], s.full[:], start=True, stop=True))
        wait(v, t)
        n.V(v.tensor_copy(s.filled[:], pc[0:1, 0:1]))
        n.meet(v, a, pe, pool)


def attention_and_adjacency(n, s, ctx):
    nc, v, a, pe, pool, sp = n.nc, n.v, n.a, n.pe, n.pool, n.sp
    CP = 2 * CHUNKS
    UP = GROUPS // 2 + 1
    HOT32 = 5

    class Stage:

        def __init__(self, name, per):
            self.sem, self.per = ctx.enter_context(nc.semaphore(name)), per
            pe.sem_inc(self.sem, per)

        def at(self, pair, e):
            return self, pair * self.per + (e + 1 + self.per)

        def by(self, ins):
            ins.then_inc(self.sem, 1)

    hot, turned, copied, wide = (Stage(f"at_{x}", CP) for x in ("hot", "turned", "copied", "wide"))
    queried, scored, clipped, exped = (Stage(f"at_{x}", CP) for x in ("queried", "scored", "clipped", "exped"))
    weighted, summed = Stage("at_weighted", CP), Stage("at_summed", CP)
    q_in, normed, stored = Stage("at_q_in", 2), Stage("at_normed", 2), Stage("at_stored", 2)
    built_c, built_t, out_c, out_t = (Stage(f"at_{x}", 2 * UP) for x in ("built_c", "built_t", "out_c", "out_t"))

    ix = [n.buf(ctx, f"ix{i}", [P, GROUPS], I32) for i in range(2)]
    sd = [n.buf(ctx, f"sd{i}", [P, 2, GROUPS], F32) for i in range(2)]
    q3 = [n.buf(ctx, f"q3_{i}", [P, 3, D], BF16) for i in range(2)]
    kv = [n.buf(ctx, f"kv_{i}", [P, GROUPS, 2 * D], F32) for i in range(2)]
    row = [n.buf(ctx, f"row_{i}", [P, WIDE], F8) for i in range(2)]
    col = [n.buf(ctx, f"col_{i}", [P, 2 * GROUPS, P], F8) for i in range(2)]
    hs = [n.buf(ctx, f"hs{i}", [P, CHUNK, P], BF16) for i in range(2)]
    hd = [n.buf(ctx, f"hd{i}", [P, CHUNK, GROUP], BF16) for i in range(2)]
    hsT = [n.buf(ctx, f"hsT{i}", [P, CHUNK, P], BF16) for i in range(2)]
    hs32 = [n.buf(ctx, f"hs32_{i}", [P, CHUNK, P], F32) for i in range(HOT32)]
    qk = [n.buf(ctx, f"qk{i}", [P, CHUNK * D], F32) for i in range(2)]
    sc = [n.buf(ctx, f"sc{i}", [P, CHUNK * HEADS], F32) for i in range(2)]
    wv = [n.buf(ctx, f"wv{i}", [P, CHUNK, AV], F32) for i in range(2)]
    rden = [n.buf(ctx, f"rden{i}", [P, HEADS], F32) for i in range(2)]
    most = n.buf(ctx, "most", [P, 2 * UP], F32)
    pt = n.bank(ctx, "pt", BF16)
    pq = [n.bank(ctx, f"pq{i}") for i in range(2)]
    pr = n.bank(ctx, "pr")
    pa = [n.bank(ctx, f"pa{i}") for i in range(4)]

    def gather(X, b):
        wait(pool, weighted.at(X, CHUNKS * (b + 1) - 1 - CP))
        t = n.G(pool.tensor_copy(ix[b][:], s.idx[:, 2 * X + b, :]))
        wait(pool, t)
        settle(pool, n.spare)
        for g in range(GROUPS):
            pool.indirect_dma_start(kv[b][:, g, :], None, s.kv_d, bass.IndirectOffsetOnAxis(
                ap=ix[b][:, g:g + 1], axis=0)).then_inc(n.kv[b].sem, 16)

    def store(X, b):
        for t in (out_c.at(X, UP * (b + 1) - 1), out_t.at(X, UP * (b + 1) - 1)):
            wait(sp, t)
            settle(sp, n.spare)
        sp.dma_start(s.c_d[2 * X + b, :, :], row[b][:].bitcast(U8)).then_inc(n.row.sem, 16)
        sp.dma_start(s.t_d[2 * X + b, :, :], col[b][:].bitcast(U8).rearrange("p m e -> p (m e)")).then_inc(n.row.sem, 16)
        wait(sp, (n.row, X * 64 + 32 * (b + 1)))
        sp.sem_inc(stored.sem, 1)

    def units(e):
        g1 = (e % CHUNKS + 1) * CHUNK
        return [(g // 2 + UP * (e // CHUNKS), g - g % 2, g % 2 + 1)
                for g in range(g1 - CHUNK, g1) if g % 2 == 1 or g == GROUPS - 1]

    def one_hots(X, e):
        b, k, g0 = e // CHUNKS, e % 2, (e % CHUNKS) * CHUNK
        if g0 == 0:
            wait(v, hot.at(X, e - 1))
            t = n.V(v.tensor_copy(sd[b][:], s.slots[:, :, 2 * X + b, :]))
            wait(v, t)
        wait(v, queried.at(X, e - 2), wide.at(X, e - 2))
        for g in range(CHUNK):
            v.tensor_scalar(hs[k][:, g, :], s.count1[:, 0:P], sd[b][:, 0, g0 + g:g0 + g + 1], None, ALU.is_equal)
            t = v.tensor_scalar(hd[k][:, g, :], s.count1[:], sd[b][:, 1, g0 + g:g0 + g + 1], None, ALU.is_equal)
        hot.by(t)

    def turn(X, e):
        wait(pe, hot.at(X, e), copied.at(X, e - 1))
        for g in range(CHUNK):
            t = pe.transpose(pt[:, g * P:(g + 1) * P], hs[e % 2][:, g, :], s.identb[:])
        turned.by(t)

    def copy_turned(X, e):
        wait(a, turned.at(X, e), queried.at(X, e - 2))
        copied.by(a.activation(hsT[e % 2][:].rearrange("p g e -> p (g e)"), pt[:, 0:CHUNK * P], ACT.Copy))

    def copy_wide(X, e):
        wait(a, hot.at(X, e), summed.at(X, e - HOT32))
        wide.by(a.activation(hs32[e % HOT32][:], hs[e % 2][:], ACT.Copy))

    def copy_q(X, b):
        wait(a, queried.at(X, CHUNKS * (b + 1) - 1 - CP))
        q_in.by(a.activation(q3[b][:], s.q3[:, 2 * X + b, :, :], ACT.Copy))

    def query(X, e):
        b, k = e // CHUNKS, e % 2
        wait(pe, copied.at(X, e), scored.at(X, e - 2))
        if e % CHUNKS == 0:
            wait(pe, q_in.at(X, b))
        for g in range(CHUNK):
            for part in range(3):
                t = pe.matmul(pq[k][:, g * D:(g + 1) * D], hsT[k][:, g, :], q3[b][:, part, :],
                              start=part == 0, stop=part == 2)
        queried.by(t)

    def build(X, e):
        k, b, g0 = e % 2, e // CHUNKS, (e % CHUNKS) * CHUNK
        for g in range(CHUNK):
            at = g0 + g
            u, half = at // 2 + UP * b, at % 2
            last = half == 1 or at == GROUPS - 1
            bc, bt = pa[2 * (u % 2)], pa[2 * (u % 2) + 1]
            if half == 0:
                wait(pe, out_c.at(X, u - 2), out_t.at(X, u - 2))
            t = pe.matmul(bc[:, half * GROUP:(half + 1) * GROUP], hs[k][:, g, :], hd[k][:, g, :], start=True, stop=True)
            if last:
                built_c.by(t)
            for m in range(2):
                t = pe.matmul(bt[:, half * GROUP + m * P:half * GROUP + (m + 1) * P],
                              hd[k][:, g, m * P:(m + 1) * P], hs[k][:, g, :], start=True, stop=True)
            if last:
                built_t.by(t)

    def evacuate_c(X, e):
        b = e // CHUNKS
        if e % CHUNKS == 0:
            wait(v, stored.at(X, b - 2))
        for u, g, count in units(e):
            wait(v, built_c.at(X, u), out_c.at(X, u - 1))
            settle(v, n.spare)
            out_c.by(v.tensor_scalar(row[b][:, g * GROUP:(g + count) * GROUP], pa[2 * (u % 2)][:, 0:count * GROUP],
                                     0.0, most[:, u:u + 1], ALU.add, ALU.max, accum_out=most[:, u:u + 1],
                                     saturate=False))

    def evacuate_t(X, e):
        b = e // CHUNKS
        if e % CHUNKS == 0:
            wait(a, stored.at(X, b - 2))
        for u, g, count in units(e):
            wait(a, built_t.at(X, u))
            settle(a, n.spare)
            out_t.by(a.activation(col[b][:, 2 * g:2 * (g + count), :].rearrange("p m e -> p (m e)"),
                                  pa[2 * (u % 2) + 1][:, 0:count * GROUP], ACT.Copy, saturate=False))

    def score(X, e):
        b, k, g0 = e // CHUNKS, e % 2, (e % CHUNKS) * CHUNK
        if g0 == 0:
            wait(v, (n.kv[b], X * (16 * GROUPS) + 16 * GROUPS))
        wait(v, queried.at(X, e), clipped.at(X, e - 2), exped.at(X, e - 2))
        scored.by(v.tensor_tensor(qk[k][:].rearrange("p (g d) -> p g d", d=D),
                                  pq[k][:, 0:CHUNK * D].rearrange("p (g d) -> p g d", d=D),
                                  kv[b][:, g0:g0 + CHUNK, 0:D], ALU.mult))
        wait(v, scored.at(X, e))
        t = n.V(v.tensor_reduce(sc[k][:], qk[k][:].rearrange("p (h d) -> p h d", d=DH), AX.X, ALU.add))
        wait(v, t)
        clipped.by(v.tensor_scalar(sc[k][:], sc[k][:], 10.0, -10.0, ALU.min, ALU.max))

    def exponent(X, e):
        k = e % 2
        wait(a, clipped.at(X, e), summed.at(X, e - 2))
        exped.by(a.activation(wv[k][:, :, D:D + HEADS], sc[k][:].rearrange("p (g h) -> p g h", h=HEADS), ACT.Exp))

    def weigh(X, e):
        b, k, g0 = e // CHUNKS, e % 2, (e % CHUNKS) * CHUNK
        wait(v, exped.at(X, e))
        weighted.by(v.tensor_tensor(
            wv[k][:, :, 0:D].rearrange("p g (h d) -> p g h d", d=DH),
            kv[b][:, g0:g0 + CHUNK, D:2 * D].rearrange("p g (h d) -> p g h d", d=DH),
            wv[k][:, :, D:D + HEADS].unsqueeze(3).to_broadcast([P, CHUNK, HEADS, DH]), ALU.mult))

    def total(X, e):
        b, k, g0 = e // CHUNKS, e % 2, (e % CHUNKS) * CHUNK
        wait(pe, weighted.at(X, e), wide.at(X, e))
        if g0 == 0:
            wait(pe, normed.at(X, b - 1))
        for g in range(CHUNK):
            t = pe.matmul(pr[:, 0:AV], hs32[e % HOT32][:, g, :], wv[k][:, g, :],
                          start=g0 + g == 0, stop=g0 + g == GROUPS - 1)
        summed.by(t)

    def normalize(X, e):
        b = e // CHUNKS
        wait(v, summed.at(X, e), normed.at(X, b - 2))
        t = n.V(v.tensor_scalar(rden[b][:], pr[:, D:D + HEADS], EPS_ATT, None, ALU.add))
        wait(v, t)
        t = n.V(v.reciprocal(rden[b][:], rden[b][:]))
        wait(v, t)
        n.V(v.tensor_tensor(s.R[:, 2 * X + b, :].rearrange("p (h d) -> p h d", d=DH),
                            pr[:, 0:D].rearrange("p (h d) -> p h d", d=DH), over(rden[b][:], DH), ALU.mult))
        wait(v, n.sv.now())
        normed.by(v.tensor_copy(s.odeg[:, bass.ds(2 * X + b, 1)], pr[:, AV - 1:AV]))

    def step(X, c, first=False):
        def behind(stages, lag):
            e = c - lag
            if e < 0 and not first:
                for f in stages:
                    f(X - 1, e + CP)
            elif 0 <= e < CP:
                for f in stages:
                    f(X, e)

        behind([one_hots], 0)
        behind([evacuate_c, evacuate_t], 1)
        if (c - 4) % CP in (CHUNKS - 1, CP - 1):
            behind([normalize], 4)
        if c % CP in (0, CHUNKS - 2) and c < CP:
            copy_q(X, int(c > 0))
        behind([turn, copy_turned], 0)
        behind([query], 1)
        behind([build], 0)
        behind([score, exponent], 2)
        behind([copy_wide], 0)
        behind([weigh, total], 3)
        if c % CHUNKS == 0:
            behind([lambda x, e: store(x, e // CHUNKS)], 1)

    n.meet(v, a, pe, pool)
    for i in range(2):
        n.V(v.memset(wv[i][:, :, AV - 1:AV], 1.0))
    n.V(v.memset(most[:], 0.0))
    n.meet(v, a, pe, pool)
    LAG = 4
    for b in range(2):
        gather(0, b)
    for c in range(LAG):
        step(0, c, first=True)
    with n.loop(PAIRS - 1, sv=18, sg=2) as i:
        for b in range(2):
            gather(i + 1, b)
        for c in range(LAG, CP):
            step(i, c, first=True)
        for c in range(LAG):
            step(i + 1, c)
    for c in range(LAG, CP + LAG):
        step(PAIRS - 1, c, first=True)
    n.row.count += 64 * PAIRS
    for sig in n.kv:
        sig.count += 16 * GROUPS * PAIRS
    n.meet(v, a, pe, pool, sp)
    for e in (v, a, pe, pool, sp):
        wait(e, (n.row, 64 * PAIRS), normed.at(PAIRS - 1, 1), out_t.at(PAIRS - 1, 2 * UP - 1))
    t = n.V(v.tensor_reduce(s.most[:], most[:], AX.X, ALU.max))
    n.meet(v, a, pe, pool, sp)


def aggregate(n, s, ps, panels, U, cols, finish):
    pe, sp = n.pe, n.sp
    mat = s.t_d if panels else s.c_d

    if not panels:
        wait(sp, n.done.now())

    def body(i):
        used0, free0, done0 = n.used.now(), n.free.now(), n.done.now()
        for r in range(RING):
            if panels or r == RING - 1:
                wait(sp, (n.done, done0[1] + (r + 1) - RING))
            else:
                wait(sp, (n.used, used0[1] + (r + 1) - (RING - 1)))
            settle(sp, n.spare)
            slot = s.ring[:, r, :]
            if panels:
                src = mat[RING * i + r, :, 0:PANEL]
                n.ring[r].by(sp.dma_start(slot, src), 16)
            else:
                src = mat[r * RING:(r + 1) * RING, :, bass.ds(i * (RING * P), RING * P)].rearrange("t p e -> p t e")
                n.ring[r].by(sp.dma_start(slot.rearrange("p (t e) -> p t e", t=RING), src), 16)
        w8 = s.ring[:].bitcast(F8)
        if panels:
            for r in range(RING):
                wait(pe, n.ring[r].now(), (n.free, free0[1] + (r + 1) - RING))
                settle(pe, n.spare)
                w = w8[:, r, :].rearrange("p (k e) -> p k e", e=P)
                for k in range(TILES):
                    t = pe.matmul(ps[r][:, 0:cols], w[:, k, :], U[:, k, 0:cols], start=k == 0, stop=k == TILES - 1)
                t = n.done.by(t)
                finish(i, r, ps[r], t)
        else:
            ends = []
            for r in range(RING):
                wait(pe, n.ring[r].now())
                settle(pe, n.spare)
                w = w8[:, r, :].rearrange("p (t j e) -> p t j e", t=RING, j=RING)
                for q in range(RING):
                    for j in range(RING):
                        if r == 0 and q == 0:
                            wait(pe, (n.free, free0[1] + (j + 1) - RING))
                            settle(pe, n.spare)
                        t = pe.matmul(ps[j][:, 0:cols], w[:, q, j, :], U[:, r * RING + q, 0:cols],
                                      start=r == q == 0, stop=r == q == RING - 1)
                        if r == q == RING - 1:
                            ends.append(n.done.by(t))
                if r < RING - 1:
                    n.used.by(t)
            for j in range(RING):
                finish(i, j, ps[j], ends[j])
    return body


def split16(n, src, U, at, t):
    v, a = n.v, n.a
    hi = U[:, :, at:at + D]
    wait(a, t)
    t = n.A(a.activation(hi, src, ACT.Copy))
    wait(v, t)
    t = n.V(v.tensor_tensor(src, src, hi, ALU.subtract))
    wait(a, t)
    return n.A(a.activation(U[:, :, at + D:at + 2 * D], src, ACT.Copy, scale=LO))


def softmax_dense(n, s, ps):
    v, a = n.v, n.a
    t_h = layernorm_relu(n, s)
    with ExitStack() as ctx:
        cols = 4 * D + 1
        U = n.buf(ctx, "u1", [P, TILES, cols], F16)
        lo = [n.buf(ctx, f"lo1_{j}", [P, 2, D], F32) for j in range(RING)]
        dn = [n.buf(ctx, f"dn1_{j}", [P, 2, D], F32) for j in range(RING)]
        e = [n.buf(ctx, f"e1_{j}", [P, D], F32) for j in range(RING)]
        Y = n.buf(ctx, "y1", [P, TILES, D], F32)
        n.V(v.memset(U[:, :, cols - 1:cols], 1.0))
        wait(a, t_h)
        t = n.A(a.activation(s.T, s.H[:], ACT.Exp))
        wait(v, t)
        t = n.V(v.scalar_tensor_tensor(Y[:], s.H[:], 0.25, s.T, ALU.mult, ALU.mult))
        split16(n, s.T, U, 0, t)
        split16(n, Y[:], U, 2 * D, t)

        def finish(i, j, p_, t):
            tile = bass.ds(RING * i + j, 1)
            sums = p_[:, 0:4 * D].rearrange("p (w h d) -> p w h d", w=2, h=2)
            wait(a, t)
            t = n.A(a.activation(lo[j][:], sums[:, :, 1, :], ACT.Copy, scale=1.0 / LO))
            wait(v, t)
            t = n.V(v.tensor_tensor(dn[j][:], lo[j][:], sums[:, :, 0, :], ALU.add))
            n.free.by(v.tensor_copy(s.ideg[:, tile], p_[:, cols - 1:cols]))
            wait(v, t)
            n.V(v.tensor_scalar(e[j][:], dn[j][:, 0, :], 0.5, EPS_MSG, ALU.is_gt, ALU.mult))
            t = n.V(v.tensor_scalar(lo[j][:, 0, :], dn[j][:, 0, :], 0.5, None, ALU.max))
            wait(v, t)
            t = n.V(v.reciprocal(lo[j][:, 0, :], lo[j][:, 0, :]))
            wait(v, t)
            t = n.V(v.scalar_tensor_tensor(dn[j][:, 1, :], dn[j][:, 1, :], 4.0, lo[j][:, 0, :], ALU.mult, ALU.mult))
            wait(v, t)
            t = n.V(v.tensor_tensor(dn[j][:, 1, :], dn[j][:, 1, :], e[j][:], ALU.add))
            wait(v, t)
            n.V(v.tensor_tensor(s.T[:, tile, :], dn[j][:, 1, :].unsqueeze(1), s.H[:, tile, :], ALU.add))

        n.meet(v, a, n.pe)
        body = aggregate(n, s, ps, False, U, cols, finish)
        with n.loop(BODIES, used=RING - 1, free=RING, done=RING, sv=7 * RING, sa=RING,
                    **{f"ring{r}": 16 for r in range(RING)}) as i:
            n.meet(v, a)
            body(i)
        n.meet(v, a, n.pe, n.pool)


def appnp_begin(n, s):
    v = n.v
    t_h = layernorm_relu(n, s)
    rs, rc, g = s.col
    wait(v, t_h)
    t = n.V(v.tensor_scalar(rs[:], s.odeg[:, 0:TILES], 1.0, None, ALU.max))
    t = n.V(v.tensor_scalar(rc[:], s.ideg[:], 1.0, None, ALU.max))
    inv_sqrt(n, rs, rs, t)
    t = inv_sqrt(n, rc, rc, t)
    wait(v, t)
    n.V(v.scalar_tensor_tensor(g[:], rs[:], BETA, rc[:], ALU.mult, ALU.mult))
    t = n.V(v.scalar_tensor_tensor(s.T, s.H[:], SCALE, over(rc[:], D), ALU.mult, ALU.mult))
    wait(v, t)
    return n.V(v.tensor_scalar(s.H[:], s.T, ALPHA, None, ALU.mult))


def appnp_end(n, s, u):
    v = n.v
    rc = s.col[1]
    t = n.V(v.reciprocal(rc[:], rc[:]))
    wait(v, t)
    t = n.V(v.scalar_tensor_tensor(s.T, u, 1.0 / (SCALE * THETA), over(rc[:], D), ALU.mult, ALU.mult))
    wait(v, t)
    n.V(v.tensor_tensor(s.X[:], s.X[:], s.T, ALU.add))
    n.meet(v, n.a, n.pe, n.pool)


def appnp_dense(n, s, ps):
    v, a, pe = n.v, n.a, n.pe
    t = appnp_begin(n, s)
    g = s.col[2]
    with ExitStack() as ctx:
        Ua = n.buf(ctx, "u2a", [P, TILES, 2 * D], F16)
        Ub = n.buf(ctx, "u2b", [P, TILES, 2 * D], F16)
        UF = n.buf(ctx, "u2f", [P, TILES, D], F32)
        lo = [n.buf(ctx, f"lo2_{j}", [P, D], F32) for j in range(RING)]
        z = [n.buf(ctx, f"z2_{j}", [P, D], F32) for j in range(RING)]
        uf = [n.buf(ctx, f"uf2_{j}", [P, D], F32) for j in range(RING)]
        res = [n.buf(ctx, f"r2_{j}", [P, D], F32) for j in range(RING)]
        split16(n, s.T, Ua, 0, t)

        def finish_into(Un):
            def finish(i, j, p_, t):
                tile = bass.ds(RING * i + j, 1)
                wait(a, t)
                t = n.A(a.activation(lo[j][:], p_[:, D:2 * D], ACT.Copy, scale=1.0 / LO))
                wait(v, t)
                t = n.free.by(v.tensor_tensor(z[j][:], lo[j][:], p_[:, 0:D], ALU.add))
                wait(v, t)
                t = n.V(v.scalar_tensor_tensor(uf[j][:], z[j][:], g[:, tile], s.H[:, tile, :].rearrange("p a d -> p (a d)"),
                                               ALU.mult, ALU.add))
                wait(a, t)
                n.A(a.activation(UF[:, tile, :], uf[j][:].unsqueeze(1), ACT.Copy))
                hi = Un[:, tile, 0:D].rearrange("p a d -> p (a d)")
                t = n.A(a.activation(hi, uf[j][:], ACT.Copy))
                wait(v, t)
                t = n.V(v.tensor_tensor(res[j][:], uf[j][:], hi, ALU.subtract))
                wait(a, t)
                n.A(a.activation(Un[:, tile, D:2 * D].rearrange("p a d -> p (a d)"), res[j][:], ACT.Copy, scale=LO))
            return finish

        per = dict(free=RING, done=RING, sv=2 * RING, sa=4 * RING,
                   **{f"ring{r}": 16 for r in range(RING)})
        with n.loop(STEPS // 2, **{k: 2 * BODIES * c for k, c in per.items()}):
            for U, Un in ((Ua, Ub), (Ub, Ua)):
                n.meet(pe)
                body = aggregate(n, s, ps, True, U, 2 * D, finish_into(Un))
                with n.loop(BODIES, **per) as i:
                    n.meet(v, a)
                    body(i)
        n.meet(v, a, pe, n.pool)
        appnp_end(n, s, UF[:])


def gcn_begin(n, s):
    v = n.v
    t_h = layernorm_relu(n, s)
    deg, dinv, g = s.col
    wait(v, t_h)
    t = n.V(v.tensor_scalar(deg[:], s.ideg[:], 1.0, None, ALU.add))
    t = inv_sqrt(n, dinv, deg, t)
    wait(v, t)
    n.V(v.tensor_scalar(g[:], dinv[:], 1.0 / SCALE, None, ALU.mult))


def gcn_dense(n, s, ps):
    v, a, pe = n.v, n.a, n.pe
    gcn_begin(n, s)
    _, dinv, g = s.col
    ring_per = dict(used=RING - 1, free=RING, done=RING, **{f"ring{r}": 16 for r in range(RING)})
    with ExitStack() as ctx:
        U = n.buf(ctx, "u3", [P, TILES, 3 * D], F16)
        UD = n.buf(ctx, "ud3", [P, TILES, D], F32)
        lo = [n.buf(ctx, f"lo3_{j}", [P, D], F32) for j in range(RING)]
        z = [n.buf(ctx, f"z3_{j}", [P, D], F32) for j in range(RING)]
        t = n.V(v.scalar_tensor_tensor(UD[:], s.H[:], SCALE, over(dinv[:], D), ALU.mult, ALU.mult))
        wait(v, t)
        t = n.V(v.tensor_copy(s.T, UD[:]))
        split16(n, s.T, U, 0, t)

        def close(i, j, t, scale):
            tile = bass.ds(RING * i + j, 1)
            wait(v, t)
            t = n.V(v.tensor_tensor(z[j][:], z[j][:], UD[:, tile, :].rearrange("p a d -> p (a d)"), ALU.add))
            wait(v, t)
            n.V(v.tensor_scalar(s.T[:, tile, :].rearrange("p a d -> p (a d)"), z[j][:], scale[:, tile], None, ALU.mult))

        def finish1(i, j, p_, t):
            wait(a, t)
            t = n.A(a.activation(lo[j][:], p_[:, D:2 * D], ACT.Copy, scale=1.0 / LO))
            wait(v, t)
            t = n.free.by(v.tensor_tensor(z[j][:], lo[j][:], p_[:, 0:D], ALU.add))
            close(i, j, t, g)

        n.meet(v, a, pe)
        body = aggregate(n, s, ps, False, U, 2 * D, finish1)
        with n.loop(BODIES, sv=2 * RING, sa=RING, **ring_per) as i:
            n.meet(v, a)
            body(i)
        n.meet(v, a, pe, n.pool)


def gcn_second_dense(n, s, ps):
    v, a, pe = n.v, n.a, n.pe
    _, dinv, _ = s.col
    ring_per = dict(used=RING - 1, free=RING, done=RING, **{f"ring{r}": 16 for r in range(RING)})
    with ExitStack() as ctx:
        U = n.buf(ctx, "u4", [P, TILES, 3 * D], BF16)
        UD = n.buf(ctx, "ud4", [P, TILES, D], F32)
        lo = [n.buf(ctx, f"lo4_{j}", [P, D], F32) for j in range(RING)]
        z = [n.buf(ctx, f"z4_{j}", [P, D], F32) for j in range(RING)]
        t = n.V(v.tensor_tensor(UD[:], s.H[:], over(dinv[:], D), ALU.mult))
        wait(v, t)
        t = n.V(v.tensor_copy(s.T, UD[:]))
        for part in range(3):
            o = U[:, :, part * D:(part + 1) * D]
            wait(a, t)
            t = n.A(a.activation(o, s.T, ACT.Copy))
            if part < 2:
                wait(v, t)
                t = n.V(v.tensor_tensor(s.T, s.T, o, ALU.subtract))

        def finish(i, j, p_, t):
            tile = bass.ds(RING * i + j, 1)
            wait(a, t)
            t = n.A(a.activation(lo[j][:], p_[:, 2 * D:3 * D], ACT.Copy))
            wait(v, t)
            t = n.V(v.tensor_tensor(z[j][:], lo[j][:], p_[:, D:2 * D], ALU.add))
            wait(v, t)
            t = n.free.by(v.tensor_tensor(z[j][:], z[j][:], p_[:, 0:D], ALU.add))
            wait(v, t)
            t = n.V(v.tensor_tensor(z[j][:], z[j][:], UD[:, tile, :].rearrange("p a d -> p (a d)"), ALU.add))
            wait(v, t)
            n.V(v.tensor_scalar(s.T[:, tile, :].rearrange("p a d -> p (a d)"), z[j][:], dinv[:, tile], None, ALU.mult))

        n.meet(v, a, pe)
        body = aggregate(n, s, ps, False, U, 3 * D, finish)
        with n.loop(BODIES, sv=3 * RING, sa=RING, **ring_per) as i:
            n.meet(v, a)
            body(i)
        n.meet(v, a, pe, n.pool)


class Store:
    pass


def add_to_x(n, s):
    def finish(i, j, p_, t):
        x = s.X[:, bass.ds(RING * i + j, 1), :].rearrange("p a d -> p (a d)")
        wait(n.v, t)
        return n.V(n.v.tensor_tensor(x, p_, x, ALU.add))
    return finish


def relu_to_h(n, s):
    def finish(i, j, p_, t):
        wait(n.a, t)
        return n.A(n.a.activation(s.H[:, bass.ds(RING * i + j, 1), :].rearrange("p a d -> p (a d)"), p_, ACT.Relu))
    return finish


def relu_add_to_x(n, s):
    def finish(i, j, p_, t):
        x = s.X[:, bass.ds(RING * i + j, 1), :].rearrange("p a d -> p (a d)")
        wait(n.v, t)
        return n.V(n.v.scalar_tensor_tensor(x, p_, 0.0, x, ALU.max, ALU.add))
    return finish


def keep_tile(n, into):
    def finish(i, j, p_, t):
        wait(n.v, t)
        return n.V(n.v.tensor_copy(into[:, bass.ds(RING * i + j, 1), :].rearrange("p a d -> p (a d)"), p_))
    return finish


def split_q(n, s, q):
    half = TILES // 2
    parts = [slice(0, half), slice(half, TILES)]
    at = [n.sv.now()] * 2
    for part in range(3):
        for h, tiles in enumerate(parts):
            wait(n.a, at[h])
            at[h] = n.A(n.a.activation(s.q3[:, tiles, part, :], q[:, tiles, :], ACT.Copy))
        for h, tiles in enumerate(parts):
            if part < 2:
                wait(n.v, at[h])
                at[h] = n.V(n.v.tensor_tensor(q[:, tiles, :], q[:, tiles, :], s.q3[:, tiles, part, :], ALU.subtract))


def gnn(nc, x_in, src_in, dst_in, qw, kw, vw, w1, b1, w31, b31, w32, b32, out):
    with ExitStack() as top:
        n = Net(nc, top)
        v, a, pe, pool, sp = n.v, n.a, n.pe, n.pool, n.sp
        s = Store()
        s.kv_d = nc.dram_tensor("kv_rows", [NODES, 2 * D], F32).ap()
        s.c_d = nc.dram_tensor("adjacency", [BTILES, P, WIDE], U8).ap()
        s.t_d = nc.dram_tensor("adjacency_t", [BTILES, P, WIDE], U8).ap()
        s.X = n.buf(top, "X", [P, TILES, D], F32)
        s.H = n.buf(top, "H", [P, TILES, D], F32)
        s.R = n.buf(top, "T", [P, BTILES, D], F32)
        s.T = s.R[:, 0:TILES, :]
        s.ident = n.buf(top, "ident", [P, P], F32)
        s.identb = n.buf(top, "identb", [P, P], BF16)
        s.count1 = n.buf(top, "count1", [P, GROUP], BF16)
        s.tri = n.buf(top, "tri", [P, P], BF16)
        s.ones = n.buf(top, "ones", [P, P], F32)
        s.odeg = n.buf(top, "odeg", [P, BTILES], F32)
        s.ideg = n.buf(top, "ideg", [P, TILES], F32)
        s.most = n.buf(top, "most_all", [P, 1], F32)
        s.full = n.buf(top, "full", [P, 1], F32)
        fits = n.buf(top, "fits", [1, 1], I32)
        s.filled = n.buf(top, "filled", [1, 1], F32)
        s.col = [n.buf(top, f"col{i}", [P, TILES], F32) for i in range(3)]
        s.stage = n.buf(top, "stage", [P, RING, D], F32)
        s.aT = n.buf(top, "aT", [P, RING * P], F32)
        wq = n.buf(top, "wq", [D, 3 * D], F32)
        wl = [n.buf(top, f"wl{i}", [D + 1, D], F32) for i in range(3)]

        t = n.V(v.memset(s.X[:, TILES - 1, :], 0.0))
        for i, w in enumerate((qw, kw, vw)):
            sp.dma_start(wq[:, i * D:(i + 1) * D], w).then_inc(n.ld.sem, 16)
        for b_, w, bias in zip(wl, (w1, w31, w32), (b1, b31, b32)):
            sp.dma_start(b_[0:D, :], w).then_inc(n.ld.sem, 16)
            sp.dma_start(b_[D:D + 1, :], bias.rearrange("(a n) -> a n", a=1)).then_inc(n.ld.sem, 16)
        sp.dma_start(s.X[:, 0:TILES - 1, :],
                     x_in[0:NODES - LAST, :].rearrange("(k p) f -> p k f", p=P)).then_inc(n.ld.sem, 16)
        wait(sp, t)
        sp.dma_start(s.X[0:LAST, TILES - 1, :], x_in[NODES - LAST:NODES, :]).then_inc(n.ld.sem, 16)
        n.ld.count += 16 * 11
        t_loaded = n.ld.now()

        n.G(pool.memset(s.ones[:], 1.0))
        n.G(pool.memset(s.ident[:], 0.0))
        t = n.G(pool.iota(s.count1[:], [[1, GROUP]], base=1, channel_multiplier=0,
                          allow_small_or_imprecise_dtypes=True))
        wait(pool, t)
        n.G(pool.affine_select(out=s.ident[:], in_=s.ident[:], compare_op=ALU.not_equal, fill=1.0, base=0,
                               pattern=[[-1, P]], channel_multiplier=1))
        t_const = n.G(pool.affine_select(out=s.tri[:], in_=s.ones[:], compare_op=ALU.is_gt, fill=0.0, base=0,
                                         pattern=[[1, P]], channel_multiplier=-1))
        wait(v, t_const)
        n.V(v.tensor_copy(s.identb[:], s.ident[:]))
        n.V(v.memset(s.aT[D:D + 1, :], 1.0))
        wait(pe, t_const, t_loaded)
        wait(a, t_loaded)

        with ExitStack() as ctx:
            s.q3 = n.buf(ctx, "q3", [P, BTILES, 3, D], BF16)
            s.slots = n.buf(ctx, "slots", [P, 2, BTILES, GROUPS], F32)
            s.idx = n.buf(ctx, "idx", [P, BTILES, GROUPS], I32)
            s.slotmax = n.buf(ctx, "slotmax", [P, BTILES * GROUPS], BF16)
            with ExitStack() as c2:
                s.es = n.buf(c2, "es", [P, GROUPS, RUN], I32)
                s.ed = n.buf(c2, "ed", [P, GROUPS, RUN], I32)
                t_edges = load_edges(n, s, src_in, dst_in)
                wait(v, t_loaded)
                layernorm_relu(n, s)
                n.V(v.memset(s.q3[:, TILES:BTILES, :, :], 0.0))
                n.V(v.memset(s.slots[:, :, TILES:BTILES, :], 0.0))
                for e in (v, a, pe, pool):
                    wait(e, t_edges)
                with ExitStack() as c3:
                    qkv = n.buf(c3, "qkv", [P, TILES, 3 * D], F32)
                    linear(n, s, "qkv", s.H, wq, 3 * D, False, keep_tile(n, qkv), sv=RING, sa=3, se=2 * RING)
                    wait(sp, n.sv.now())
                    sp.dma_start(s.kv_d[0:NODES - LAST, :].rearrange("(k p) f -> p k f", p=P),
                                 qkv[:, 0:TILES - 1, D:3 * D]).then_inc(n.ld.sem, 16)
                    sp.dma_start(s.kv_d[NODES - LAST:NODES, :], qkv[0:LAST, TILES - 1, D:3 * D]).then_inc(n.ld.sem, 16)
                    n.ld.count += 32
                    split_q(n, s, qkv[:, :, 0:D])
                    for e in (v, pool, sp, a):
                        wait(e, n.ld.now())
                    n.meet(v, a, pe, pool)
                bucket_edges(n, s)
            attention_and_adjacency(n, s, ctx)
        with ExitStack() as ctx:
            pf = n.bank(ctx, "pf")
            high = n.buf(ctx, "high", [1, 1], F32)
            wait(pe, n.sv.now())
            t = n.E(pe.matmul(pf[0:1, 0:P], s.most[:], s.ident[:], start=True, stop=True))
            wait(v, t)
            t = n.V(v.tensor_reduce(high[:], pf[0:1, 0:P], AX.X, ALU.max))
            wait(v, t)
            t = n.V(v.tensor_scalar(high[:], high[:], EXACT, None, ALU.is_le))
            wait(v, t)
            t = n.V(v.tensor_scalar(s.filled[:], s.filled[:], float(EDGES), None, ALU.is_equal))
            wait(v, t)
            t = n.V(v.tensor_tensor(fits[:], s.filled[:], high[:], ALU.mult))
            for e in (v, a, pe, pool, sp):
                wait(e, t)
            dense = nc.values_load(fits[0:1, 0:1], min_val=0, max_val=1)
            n.meet(v, a, pe, pool, sp)
        before = [sig.count for _, sig in n.sigs]
        with nc.If(dense > 0):
            dense_layers(n, s, wl, out)
        for (_, sig), count in zip(n.sigs, before):
            sig.count = count
        with nc.Else():
            edge_layers(n, s, wq, wl, src_in, dst_in, out)


def add_attention(n, s):
    t = n.V(n.v.tensor_tensor(s.X[:], s.X[:], s.H[:], ALU.add))
    wait(n.v, t)
    n.V(n.v.tensor_tensor(s.X[:], s.X[:], s.T, ALU.add))


def store_x(n, s, out):
    wait(n.sp, n.sv.now())
    n.sp.dma_start(out[0:NODES - LAST, :].rearrange("(k p) f -> p k f", p=P),
                   s.X[:, 0:TILES - 1, :]).then_inc(n.ld.sem, 16)
    n.sp.dma_start(out[NODES - LAST:NODES, :], s.X[0:LAST, TILES - 1, :]).then_inc(n.ld.sem, 16)
    n.ld.count += 32
    wait(n.sp, n.ld.now())


def dense_layers(n, s, wl, out):
    add_attention(n, s)
    with ExitStack() as ctx:
        s.ring = n.buf(ctx, "ring", [P, RING, PANEL], U8)
        with ExitStack() as banks:
            ps = [n.bank(banks, f"sum1_{j}") for j in range(RING)]
            softmax_dense(n, s, ps)
        linear(n, s, "l1", s.T, wl[0], D, True, add_to_x(n, s), sv=RING, sa=3, se=2 * RING)
        with ExitStack() as banks:
            ps = [n.bank(banks, f"sum2_{j}") for j in range(RING)]
            appnp_dense(n, s, ps)
            gcn_dense(n, s, ps)
        linear(n, s, "l3a", s.T, wl[1], D, True, relu_to_h(n, s), sa=3 + RING, se=2 * RING)
        with ExitStack() as banks:
            ps = [n.bank(banks, f"sum3_{j}") for j in range(RING)]
            gcn_second_dense(n, s, ps)
        linear(n, s, "l3b", s.T, wl[2], D, True, relu_add_to_x(n, s), sv=RING, sa=3, se=2 * RING)
    store_x(n, s, out)


class Edges:

    def __init__(self, n, s, ctx, src_in, dst_in):
        self.n, self.s = n, s
        self.src = n.buf(ctx, "e_src", [SCAN, COLS], I32)
        self.dst = n.buf(ctx, "e_dst", [SCAN, COLS], I32)
        self.ix = n.buf(ctx, "e_ix", [SCAN, 2], I32)
        self.rel = n.buf(ctx, "e_rel", [SCAN, 1], F32)
        self.hot = n.buf(ctx, "e_hot", [SCAN, P], F32)
        self.count0 = n.buf(ctx, "e_count0", [SCAN, P], F32)
        self.row = n.buf(ctx, "e_row", [SCAN, 3 * D], F32)
        self.msg = n.buf(ctx, "e_msg", [SCAN, 2 * D + 1], F32)
        self.sc = n.buf(ctx, "e_sc", [SCAN, HEADS], F32)
        self.acc = n.buf(ctx, "e_acc", [P, TILES, 2 * D + 1], F32)
        self.ps = n.bank(ctx, "e_ps")
        self.m_d = n.nc.dram_tensor("e_pairs", [TILES * P, 2 * D + 1], F32).ap()
        self.u_d = n.nc.dram_tensor("e_rows", [TILES * P, D], F32).ap()
        for b, arr in ((self.src, src_in), (self.dst, dst_in)):
            n.sp.dma_start(b[:], arr.rearrange("(p e) -> p e", p=SCAN)).then_inc(n.ld.sem, 16)
        n.ld.count += 32
        n.V(n.v.tensor_scalar(self.count0[:], s.count1[0:SCAN, 0:P], 1.0, None, ALU.subtract))
        wait(n.v, n.ld.now())
        wait(n.pool, n.ld.now())

    def publish(self, table, rows):
        n = self.n
        n.meet(n.sp)
        n.sp.dma_start(table.rearrange("(k p) f -> p k f", p=P), rows).then_inc(n.ld.sem, 16)
        n.ld.count += 16
        for e in (n.v, n.a, n.pool):
            wait(e, n.ld.now())

    def sum(self, loads, key, width, message=None, **per):
        n, s = self.n, self.s
        v, a, pe, pool = n.v, n.a, n.pe, n.pool
        acc = self.acc[:, :, 0:width]
        n.meet(v, a, pe, pool)
        n.V(v.memset(acc, 0.0))
        per = {"sv": per.get("sv", 0) + 1 + 3 * TILES, "sa": per.get("sa", 0), "se": TILES,
               "sg": len(loads), "kv0": 16 * len(loads)}
        with n.loop(COLS, **{k: c for k, c in per.items() if c}) as e:
            n.meet(v, a, pe, pool)
            for m, (table, index, into) in enumerate(loads):
                t = n.G(pool.tensor_copy(self.ix[:, m:m + 1], index[:, bass.ds(e, 1)]))
                wait(pool, t)
                settle(pool, n.spare)
                n.kv[0].by(pool.indirect_dma_start(into, None, table, bass.IndirectOffsetOnAxis(
                    ap=self.ix[:, m:m + 1], axis=0)), 16)
            n.V(v.tensor_copy(self.rel[:], key[:, bass.ds(e, 1)]))
            wait(v, n.kv[0].now())
            wait(a, n.kv[0].now())
            wait(pe, n.kv[0].now())
            if message is not None:
                message()
            with n.loop(TILES, sv=3, se=1) as b:
                n.meet(v, pe)
                t = n.V(v.tensor_scalar(self.hot[:], self.count0[:], self.rel[:], None, ALU.is_equal))
                wait(pe, t)
                tp = n.E(pe.matmul(self.ps[:, 0:width], self.hot[:], self.msg[:, 0:width], start=True, stop=True))
                wait(v, t)
                n.V(v.tensor_scalar(self.rel[:], self.rel[:], float(P), None, ALU.subtract))
                wait(v, tp)
                part = acc[:, bass.ds(b, 1), :].rearrange("p a d -> p (a d)")
                n.V(v.tensor_tensor(part, part, self.ps[:, 0:width], ALU.add))
        n.meet(v, a, pe, pool)


def edge_layers(n, s, wq, wl, src_in, dst_in, out):
    v, a, nc = n.v, n.a, n.nc
    with ExitStack() as ctx:
        qkv = n.buf(ctx, "e_all", [P, TILES, 3 * D], F32)

        def keep(i, j, p_, t):
            wait(a, t)
            return n.A(a.activation(qkv[:, bass.ds(RING * i + j, 1), :].rearrange("p a d -> p (a d)"), p_, ACT.Copy))

        linear(n, s, "e_qkv_lin", s.H, wq, 3 * D, False, keep, sa=3 + RING, se=2 * RING)
        q_d = nc.dram_tensor("e_qkv", [TILES * P, 3 * D], F32).ap()
        n.meet(n.sp)
        n.sp.dma_start(q_d.rearrange("(k p) f -> p k f", p=P), qkv[:]).then_inc(n.ld.sem, 16)
        n.ld.count += 16
        for e in (v, a, n.sp, n.pool):
            wait(e, n.ld.now())
    with ExitStack() as ctx:
        E = Edges(n, s, ctx, src_in, dst_in)
        E.q_d = q_d
        kv = n.buf(ctx, "e_kv", [SCAN, 3 * D], F32)
        wide = n.buf(ctx, "e_wide", [P, TILES, 2 * D + 1], F32)

        def attend():
            q, k, val = E.row[:, 0:D], kv[:, D:2 * D], kv[:, 2 * D:3 * D]
            t = n.V(v.tensor_tensor(E.msg[:, 0:D], q, k, ALU.mult))
            wait(v, t)
            t = n.V(v.tensor_reduce(E.sc[:], E.msg[:, 0:D].rearrange("p (h d) -> p h d", d=DH), AX.X, ALU.add))
            wait(v, t)
            t = n.V(v.tensor_scalar(E.sc[:], E.sc[:], 10.0, -10.0, ALU.min, ALU.max))
            wait(a, t)
            t = n.A(a.activation(E.msg[:, D:D + HEADS], E.sc[:], ACT.Exp))
            n.V(v.memset(E.msg[:, D + HEADS:AV], 1.0))
            wait(v, t)
            n.V(v.tensor_tensor(E.msg[:, 0:D].rearrange("p (h d) -> p h d", d=DH),
                                val.rearrange("p (h d) -> p h d", d=DH), over(E.msg[:, D:D + HEADS], DH), ALU.mult))

        E.sum([(E.q_d, E.src, E.row[:]), (E.q_d, E.dst, kv[:])], E.src, AV, attend, sv=5, sa=1)
        den = wide[:, :, 0:HEADS]
        t = n.V(v.tensor_scalar(den, E.acc[:, :, D:D + HEADS], EPS_ATT, None, ALU.add))
        wait(v, t)
        t = n.V(v.reciprocal(den, den))
        wait(v, t)
        for h in range(HEADS):
            t = n.V(v.tensor_tensor(s.T[:, :, h * DH:(h + 1) * DH], E.acc[:, :, h * DH:(h + 1) * DH],
                                    den[:, :, h:h + 1].to_broadcast([P, TILES, DH]), ALU.mult))
        n.V(v.tensor_copy(s.odeg[:, 0:TILES], E.acc[:, :, AV - 1]))
        wait(v, t)
        add_attention(n, s)

        t = layernorm_relu(n, s)
        wait(a, t)
        t = n.A(a.activation(wide[:, :, 0:D], s.H[:], ACT.Exp))
        wait(v, t)
        n.V(v.tensor_tensor(wide[:, :, D:2 * D], s.H[:], wide[:, :, 0:D], ALU.mult))
        n.V(v.memset(wide[:, :, 2 * D:2 * D + 1], 1.0))
        E.publish(E.m_d, wide[:])
        E.sum([(E.m_d, E.src, E.msg[:])], E.dst, 2 * D + 1)
        e, m = wide[:, :, 0:D], wide[:, :, D:2 * D]
        den, num = E.acc[:, :, 0:D], E.acc[:, :, D:2 * D]
        n.V(v.tensor_scalar(e, den, 0.5, EPS_MSG, ALU.is_gt, ALU.mult))
        t = n.V(v.tensor_scalar(m, den, 0.5, None, ALU.max))
        wait(v, t)
        t = n.V(v.reciprocal(m, m))
        wait(v, t)
        t = n.V(v.tensor_tensor(m, m, num, ALU.mult))
        wait(v, t)
        t = n.V(v.tensor_tensor(m, m, e, ALU.add))
        wait(v, t)
        n.V(v.tensor_tensor(s.T, m, s.H[:], ALU.add))
        n.V(v.tensor_copy(s.ideg[:], E.acc[:, :, 2 * D]))
        linear(n, s, "e_l1", s.T, wl[0], D, True, add_to_x(n, s), sv=RING, sa=3, se=2 * RING)

        appnp_begin(n, s)
        with n.loop(STEPS, sv=1 + COLS * (1 + 3 * TILES) + 2, se=COLS * TILES, sg=COLS, kv0=16 * COLS, ld=16):
            E.publish(E.u_d, s.T)
            E.sum([(E.u_d, E.dst, E.msg[:, 0:D])], E.src, D)
            t = n.V(v.tensor_tensor(s.T, E.acc[:, :, 0:D], over(s.col[2][:], D), ALU.mult))
            wait(v, t)
            n.V(v.tensor_tensor(s.T, s.T, s.H[:], ALU.add))
        n.meet(v)
        appnp_end(n, s, s.T)

        gcn_begin(n, s)
        dinv = s.col[1]
        for name, w, finish, per in (("e_l3a", wl[1], relu_to_h, dict(sa=3 + RING)),
                                     ("e_l3b", wl[2], relu_add_to_x, dict(sv=RING, sa=3))):
            n.meet(v)
            t = n.V(v.tensor_tensor(s.T, s.H[:], over(dinv[:], D), ALU.mult))
            E.publish(E.u_d, s.T)
            E.sum([(E.u_d, E.src, E.msg[:, 0:D])], E.dst, D)
            t = n.V(v.tensor_tensor(s.T, s.T, E.acc[:, :, 0:D], ALU.add))
            wait(v, t)
            n.V(v.tensor_tensor(s.T, s.T, over(dinv[:], D), ALU.mult))
            linear(n, s, name, s.T, w, D, True, finish(n, s), se=2 * RING, **per)
    store_x(n, s, out)


_INS = ["x", "src", "dst", "L0_gnn_qW", "L0_gnn_kW", "L0_gnn_vW", "L1_gnn_W", "L1_gnn_b",
        "L3_gnn_W1", "L3_gnn_b1", "L3_gnn_W2", "L3_gnn_b2"]
_OUTS = [((NODES, D), "float32")]


def kernel(**inputs):
    import numpy as np
    import concourse.bacc as bacc
    from concourse.bass_utils import run_bass_kernel_spmd as run

    nc = bacc.Bacc("TRN2", target_bir_lowering=False, num_devices=1)
    arrays, args = {}, []
    for name in _INS:
        arr = np.ascontiguousarray(inputs[name])
        arrays[f"in_{name}_dram"] = arr
        args.append(nc.dram_tensor(f"in_{name}_dram", arr.shape, mybir.dt.from_np(arr.dtype), kind="ExternalInput").ap())
    for i, (shape, dtype) in enumerate(_OUTS):
        args.append(nc.dram_tensor(f"out_{i}_dram", shape, mybir.dt.from_np(np.dtype(dtype)), kind="ExternalOutput").ap())
    gnn(nc, *args)
    r = run(nc, [arrays], core_ids=[0])
    return r.results[0]["out_0_dram"]
```

```python
from contextlib import ExitStack, contextmanager

import concourse.bass as bass
from concourse import mybir

ALU = mybir.AluOpType
ACT = mybir.ActivationFunctionType
AX = mybir.AxisListType
F32, F16, BF16, F8 = mybir.dt.float32, mybir.dt.float16, mybir.dt.bfloat16, mybir.dt.float8e4
I32, U8 = mybir.dt.int32, mybir.dt.uint8

P = 128
NODES, EDGES, D, HEADS = 6250, 100000, 96, 4
DH = D // HEADS
TILES = -(-NODES // P)
LAST = NODES - (TILES - 1) * P
GROUP = 2 * P
GROUPS = -(-NODES // GROUP)
WIDE = GROUPS * GROUP
PAIRS = (TILES + 1) // 2
BTILES = 2 * PAIRS
RUN = 36
CAP = P * RUN
SCAN = 125
COLS = EDGES // SCAN
CHUNK = 5
CHUNKS = GROUPS // CHUNK
AV = D + HEADS + 1
RING = 7
BODIES = TILES // RING
PANEL = TILES * P
LO = 2048.0
APART = 3
SCALE = 64.0
TOP = 8192.0
EXACT = 16.0
EPS_LN, EPS_ATT, EPS_MSG = 1e-5, 1e-8, 1e-7
STEPS, ALPHA, BETA = 10, 0.1, 0.9
THETA = BETA ** STEPS + ALPHA * sum(BETA ** i for i in range(STEPS))


class Sig:

    def __init__(self, ctx, nc, name):
        self.sem = ctx.enter_context(nc.semaphore(name))
        self.count = 0
        self.frames = []

    def now(self, more=0):
        value = self.count + more
        for i, per in self.frames:
            if per:
                value = i * per + value
        return self, value

    def by(self, ins, n=1):
        ins.then_inc(self.sem, n)
        self.count += n
        return self.now()


def wait(eng, *tokens):
    for sig, value in tokens:
        if not isinstance(value, int) or value > 0:
            eng.wait_ge(sig.sem, value)


def settle(eng, spare):
    eng.sem_inc(spare.sem, 1)


class Net:
    def __init__(self, nc, ctx):
        self.nc = nc
        self.v, self.a, self.pe, self.pool, self.sp = nc.vector, nc.scalar, nc.tensor, nc.gpsimd, nc.sync
        self.sigs = []

        def sig(name):
            self.sigs.append((name, Sig(ctx, nc, name)))
            return self.sigs[-1][1]

        self.sv, self.sa, self.se, self.sg = sig("sv"), sig("sa"), sig("se"), sig("sg")
        self.ld = sig("ld")
        self.eg = sig("eg")
        self.kv = sig("kv")
        self.row = sig("row")
        self.spare = Sig(ctx, nc, "spare")
        self.used = sig("used")
        self.free = sig("free")
        self.done = sig("done")
        self.ring = [sig(f"ring{r}") for r in range(RING)]
        for s, start in ((self.se, 1), (self.used, RING - 1), (self.free, RING),
                         (self.done, RING)):
            self.pe.sem_inc(s.sem, start)
            s.count = start

    def buf(self, ctx, name, shape, dt):
        return ctx.enter_context(self.nc.sbuf_tensor(name, shape, dt))

    def bank(self, ctx, name, dt=F32):
        return ctx.enter_context(self.nc.psum_tensor(name, [P, 2048 // mybir.dt.size(dt)], dt))

    def V(self, ins):
        return self.sv.by(ins)

    def A(self, ins):
        return self.sa.by(ins)

    def E(self, ins):
        return self.se.by(ins)

    def G(self, ins):
        return self.sg.by(ins)

    def meet(self, *engines):
        own = [(self.v, self.sv), (self.a, self.sa), (self.pe, self.se), (self.pool, self.sg)]
        for e in engines:
            for _, s in own:
                wait(e, s.now())

    @contextmanager
    def loop(self, trips, **per):
        start = {n: s.count for n, s in self.sigs}
        if self.se.frames:
            for e in (self.v, self.a, self.pe, self.pool, self.sp):
                settle(e, self.spare)
        with self.nc.Fori(0, trips) as i:
            for n, s in self.sigs:
                s.frames.append((i, per.get(n, 0)))
            yield i
        found = {n: s.count - start[n] for n, s in self.sigs if s.count != start[n]}
        if found != per:
            raise ValueError(f"increments in one pass: {found}")
        for n, s in self.sigs:
            s.frames.pop()
            s.count = start[n] + trips * per.get(n, 0)


def over(ap, n):
    return ap.unsqueeze(2).to_broadcast([ap.shape[0], ap.shape[1], n])


def under(ap, n):
    return ap.unsqueeze(1).to_broadcast([ap.shape[0], n, ap.shape[1]])


def by_blocks(stages, start=(), apart=1):
    at = [list(start)] * BODIES
    for turn in range(apart * (BODIES - 1) + len(stages)):
        for k in reversed(range(len(stages))):
            b, rest = divmod(turn - k, apart)
            if rest == 0 and 0 <= b < BODIES:
                at[b] = stages[k](slice(b * RING, (b + 1) * RING), at[b])
    return at


def stage(n, *calls):
    def run(tiles, tokens):
        mine = []
        for eng, issue in calls:
            wait(eng, *tokens)
            mine.append(n.V(issue(tiles)) if eng is n.v else n.A(issue(tiles)))
        return mine
    return run


def layernorm_stages(n, s):
    v, a = n.v, n.a
    m, var, rstd = s.col
    return [
        stage(n, (v, lambda k: v.tensor_reduce(m[:, k], s.X[:, k, :], AX.X, ALU.add))),
        stage(n, (v, lambda k: v.tensor_scalar(m[:, k], m[:, k], 1.0 / D, None, ALU.mult))),
        stage(n, (v, lambda k: v.tensor_tensor(s.H[:, k, :], s.X[:, k, :], over(m[:, k], D), ALU.subtract))),
        stage(n, (a, lambda k: a.square(s.T[:, k, :], s.H[:, k, :]))),
        stage(n, (v, lambda k: v.tensor_reduce(var[:, k], s.T[:, k, :], AX.X, ALU.add))),
        stage(n, (v, lambda k: v.tensor_scalar(var[:, k], var[:, k], 1.0 / D, EPS_LN, ALU.mult, ALU.add))),
        stage(n, (a, lambda k: a.sqrt(rstd[:, k], var[:, k]))),
        stage(n, (v, lambda k: v.reciprocal(rstd[:, k], rstd[:, k]))),
        stage(n, (v, lambda k: v.scalar_tensor_tensor(s.H[:, k, :], s.H[:, k, :], 0.0, over(rstd[:, k], D),
                                                      ALU.max, ALU.mult)))]


def layernorm_relu(n, s):
    n.meet(n.v, n.a)
    by_blocks(layernorm_stages(n, s))
    n.meet(n.v, n.a)


def inv_sqrt(n, y, x, t):
    wait(n.a, t)
    t = n.A(n.a.sqrt(y[:], x[:]))
    wait(n.v, t)
    return n.V(n.v.reciprocal(y[:], y[:]))


def linear_banks(n, ctx, name):
    return [n.bank(ctx, f"{name}_tr{i}") for i in range(2)], [n.bank(ctx, f"{name}_mm{i}") for i in range(4)]


def linear_pass(n, s, banks, i, rows, w, cols, bias, finish, ready, before, staged=None):
    a, pe = n.a, n.pe
    tr, mm = banks
    rows_in = D + 1 if bias else D
    wait(pe, *ready)
    moved = []
    for j in range(RING):
        t = n.E(pe.transpose(tr[j // 4][0:D, (j % 4) * P:(j % 4 + 1) * P], rows(j), s.ident[:]))
        if j in (3, RING - 1):
            wait(a, *before, t)
            moved.append(n.A(a.activation(s.aT[0:D, (j // 4) * 4 * P:(j + 1) * P],
                                          tr[j // 4][0:D, 0:(j % 4 + 1) * P], ACT.Copy)))
    if staged is not None:
        staged()
    ends = []
    for j in range(RING):
        if j in (0, 4):
            wait(pe, moved[j // 4])
        if j >= 4:
            wait(pe, ends[j - 4])
        o = mm[j % 4][:, 0:cols]
        t = n.E(pe.matmul(o, s.aT[0:rows_in, j * P:(j + 1) * P], w[0:rows_in, 0:cols], start=True, stop=True))
        ends.append(finish(i, j, o, t))
    return t, ends[-1]


def linear(n, s, name, src, w, cols, bias, finish, **per):
    a, pe = n.a, n.pe
    n.meet(n.v, a, pe, n.pool)
    with ExitStack() as ctx:
        banks = linear_banks(n, ctx, name)

        def staged(i):
            n.A(a.activation(s.stage[:], src[:, bass.ds(RING * i, RING), :], ACT.Copy))

        def run(i, next_rows):
            linear_pass(n, s, banks, i, lambda j: s.stage[:, j, :], w, cols, bias, finish,
                        [n.sa.now(), n.sv.now()], [n.se.now()], next_rows)

        staged(0)
        with n.loop(BODIES - 1, **per) as i:
            run(i, lambda: staged(i + 1))
        run(BODIES - 1, None)
    n.meet(n.v, a, pe, n.pool)


def linear_stage(n, s, banks, src, w, cols, bias, finish):
    last = []

    def run(tiles, tokens):
        i = tiles.start // RING
        product, read = linear_pass(n, s, banks, i, lambda j: src[:, RING * i + j, :], w, cols, bias, finish,
                                    list(tokens) + last[1:], last[0:1])
        last[:] = [product, read]
        return [read]
    return run


def load_edges(n, s, src_in, dst_in):
    v, pe, sp = n.v, n.pe, n.sp
    with ExitStack() as ctx:
        below = n.buf(ctx, "below", [SCAN, GROUPS], F32)
        junk = n.buf(ctx, "junk", [SCAN, COLS], BF16)
        first_f = n.buf(ctx, "first_f", [1, GROUPS], F32)
        first = n.buf(ctx, "first", [1, GROUPS], I32)
        pc = n.bank(ctx, "pc")
        wait(v, n.eg.now())
        for g in range(GROUPS):
            t = n.V(v.tensor_scalar(junk[:], s.dall[:], float(g * GROUP), None, ALU.is_lt, ALU.add,
                                    accum_out=below[:, g:g + 1]))
            wait(v, t)
        wait(pe, t)
        t = n.E(pe.matmul(pc[0:1, 0:GROUPS], s.ones[0:SCAN, 0:1], below[:], start=True, stop=True))
        wait(v, t)
        t = n.V(v.tensor_scalar(first_f[:], pc[0:1, 0:GROUPS], float(EDGES - CAP), None, ALU.min))
        wait(v, t)
        t = n.V(v.tensor_copy(first[:], first_f[:]))
        wait(sp, t)
        for g in range(GROUPS):
            at = sp.value_load(first[0:1, g:g + 1], min_val=0, max_val=EDGES - CAP)
            for buf_, arr in ((s.es, src_in), (s.ed, dst_in)):
                sp.dma_start(buf_[:, g, :], arr[bass.ds(at, CAP)].rearrange("(p r) -> p r", p=P)).then_inc(n.eg.sem, 16)
        n.eg.count += 32 * GROUPS
    return n.eg.now()


def bucket_edges(n, s):
    v, a, pe, pool = n.v, n.a, n.pe, n.pool
    with ExitStack() as ctx:
        ti = n.buf(ctx, "ti", [P, GROUPS, RUN], I32)
        base = n.buf(ctx, "base", [P, GROUPS], F32)
        valid = n.buf(ctx, "valid", [P, GROUPS, RUN], F32)
        rel = n.buf(ctx, "rel", [P, GROUPS, RUN], F32)
        tile1 = n.buf(ctx, "tile1", [P, GROUPS, RUN], BF16)
        sloc = n.buf(ctx, "sloc", [P, GROUPS, RUN], BF16)
        dloc = n.buf(ctx, "dloc", [P, GROUPS, RUN], BF16)
        number = n.buf(ctx, "number", [P, TILES, RUN], BF16)
        keep = n.buf(ctx, "keep", [P, TILES, 2 + RUN], BF16)
        bt = [n.buf(ctx, f"bt{k}", [P, TILES, 2 + RUN], BF16) for k in range(2)]
        seen = n.buf(ctx, "seen", [P, TILES, 2 + RUN], BF16)
        vals = [n.buf(ctx, f"vals{k}", [P, 2, TILES, RUN], BF16) for k in range(2)]
        prod = n.buf(ctx, "prod", [P, TILES, RUN], BF16)
        rank = n.buf(ctx, "rank", [P, RUN], F32)
        onerank = n.buf(ctx, "onerank", [P, RUN, P], BF16)
        pc = n.bank(ctx, "pc2")
        pp = [n.bank(ctx, f"pp{k}") for k in range(2)]
        po = n.bank(ctx, "po")

        t = n.G(pool.iota(base[:], [[GROUP, GROUPS]], base=0, channel_multiplier=0,
                          allow_small_or_imprecise_dtypes=True))
        wait(v, t)
        t = n.V(v.memset(keep[:], 1.0))
        wait(v, t)
        n.V(v.memset(keep[:, :, 0:1], 0.0))
        for k in range(2):
            n.V(v.memset(bt[k][:, :, 0:1], 0.0))
        n.V(v.tensor_copy(number[:], over(s.count1[:, 0:TILES], RUN)))
        t = n.V(v.tensor_tensor(rel[:], s.ed[:], over(base[:], RUN), ALU.subtract))
        wait(v, t)
        t = n.V(v.tensor_scalar(valid[:], rel[:], float(GROUP - 1), None, ALU.is_le))
        wait(v, t)
        t = n.V(v.scalar_tensor_tensor(valid[:], rel[:], 0.0, valid[:], ALU.is_ge, ALU.mult))
        wait(v, t)
        n.V(v.tensor_scalar(dloc[:], rel[:], 1.0, None, ALU.add))
        t = n.V(v.tensor_scalar(ti[:], s.es[:], P - 1, None, ALU.bitwise_and))
        wait(v, t)
        t = n.V(v.tensor_scalar(sloc[:], ti[:], 1.0, None, ALU.add))
        wait(v, t)
        t = n.V(v.tensor_scalar(ti[:], s.es[:], 7, None, ALU.logical_shift_right))
        wait(v, t)
        t = n.V(v.scalar_tensor_tensor(tile1[:], ti[:], 1.0, valid[:], ALU.add, ALU.mult))
        n.meet(v, a, pe, pool)

        flat = "p k r -> p (k r)"

        def count(g, k):
            of_g = bass.ds(g, 1)
            wait(v, n.sv.now(), n.sg.now(), n.sa.now(-1))
            t = n.V(v.tensor_tensor(bt[k][:, :, 2:2 + RUN], number[:],
                                    under(tile1[:, of_g, :].rearrange("p g r -> p (g r)"), TILES), ALU.is_equal))
            wait(v, t, n.se.now())
            wait(pool, t, n.se.now())
            t_vals = []
            for i, (val, eng, by) in enumerate(((sloc, pool, n.G), (dloc, v, n.V))):
                spread = under(val[:, of_g, :].rearrange("p g r -> p (g r)"), TILES)
                t_vals.append(by(eng.tensor_tensor(vals[k][:, i, :, :], bt[k][:, :, 2:2 + RUN], spread, ALU.mult)))
            wait(pe, t, n.sa.now())
            for r in range(RUN):
                t = pe.matmul(pp[k][:, 0:TILES], s.tri[:], bt[k][:, :, 2 + r], start=r == 0, stop=r == RUN - 1)
            t = n.E(t)
            wait(a, t)
            return t_vals, n.A(a.activation(bt[k][:, :, 1], pp[k][:, 0:TILES], ACT.Copy))

        def place(g, k, t_vals, t_before, later=1):
            wait(v, t_before, n.sv.now(), n.se.now(-later))
            t = n.V(v.tensor_tensor_scan(seen[:].rearrange(flat), keep[:].rearrange(flat), bt[k][:].rearrange(flat), 0.0,
                                         ALU.mult, ALU.add))
            wait(v, t)
            t = n.V(v.tensor_tensor(prod[:], seen[:, :, 2:2 + RUN], bt[k][:, :, 2:2 + RUN], ALU.mult))
            wait(v, t)
            t = n.V(v.tensor_reduce(rank[:], prod[:].rearrange("p k r -> p r k"), AX.X, ALU.add))
            wait(v, t)
            third = RUN // 3
            for r0 in range(0, RUN, third):
                t = n.V(v.tensor_tensor(onerank[:, r0:r0 + third, :], under(s.count1[:, 0:P], third),
                                        over(rank[:, r0:r0 + third], P), ALU.is_equal))
                if r0 == 0:
                    wait(pe, *t_vals, n.sa.now(-later))
                wait(pe, t)
                for r in range(r0, r0 + third):
                    te = pe.matmul(po[:, 0:2 * TILES], onerank[:, r, :],
                                   vals[k][:, :, :, r].rearrange("p i k -> p (i k)"),
                                   start=r == 0, stop=r == RUN - 1)
            te = n.E(te)
            wait(a, te)
            n.A(a.activation(s.slots[:, :, 0:TILES, bass.ds(g, 1)],
                             po[:, 0:2 * TILES].rearrange("p (i k) -> p i k", i=2).unsqueeze(3), ACT.Copy))

        count(0, 0)
        with n.loop((GROUPS - 1) // 2, sv=2 * 8, sg=2, se=4, sa=4) as i:
            was = (n.sv.now(), n.sg.now()), n.sa.now()
            now = count(2 * i + 1, 1)
            place(2 * i, 0, *was)
            count(2 * i + 2, 0)
            place(2 * i + 1, 1, *now)
        place(GROUPS - 1, 0, (n.sv.now(), n.sg.now()), n.sa.now(), later=0)
        n.meet(v, a, pe, pool)
        t = n.V(v.tensor_scalar(base[:], base[:], -1.0, None, ALU.add))
        wait(v, t)
        n.V(v.scalar_tensor_tensor(s.idx[:], s.slots[:, 1, :, :], 1.0,
                                   under(base[:], BTILES), ALU.max, ALU.add))
        t = n.V(v.tensor_scalar(s.slotmax[:], s.slots[:, 0, :, :].rearrange("p k g -> p (k g)"), 0.5, None,
                                ALU.is_gt, ALU.add, accum_out=s.full[:]))
        wait(pe, t)
        t = n.E(pe.matmul(pc[0:1, 0:1], s.ones[:, 0:1], s.full[:], start=True, stop=True))
        wait(v, t)
        n.V(v.tensor_copy(s.filled[:], pc[0:1, 0:1]))
        n.meet(v, a, pe, pool)


def attention_and_adjacency(n, s, ctx):
    nc, v, a, pe, pool, sp = n.nc, n.v, n.a, n.pe, n.pool, n.sp
    CP = 2 * CHUNKS
    UP = GROUPS // 2 + 1
    HOT32 = 5

    class Stage:

        def __init__(self, name, per, primed=True):
            self.sem, self.per = ctx.enter_context(nc.semaphore(name)), per
            self.start = per if primed else 0
            if primed:
                pe.sem_inc(self.sem, per)

        def at(self, pair, e):
            return self, pair * self.per + (e + 1 + self.start)

        def by(self, ins):
            ins.then_inc(self.sem, 1)

    hot, turned, copied, wide = (Stage(f"at_{x}", CP) for x in ("hot", "turned", "copied", "wide"))
    queried, scored, clipped, exped = (Stage(f"at_{x}", CP) for x in ("queried", "scored", "clipped", "exped"))
    gathered = [Stage(f"at_kv{e}", 16 * CHUNK, primed=False) for e in range(CP)]
    indexed = Stage("at_ix", 2)
    weighted, summed = Stage("at_weighted", CP), Stage("at_summed", CP)
    q_in, normed, stored = Stage("at_q_in", 2), Stage("at_normed", 2), Stage("at_stored", 2)
    built_c, built_t, out_c, out_t = (Stage(f"at_{x}", 2 * UP) for x in ("built_c", "built_t", "out_c", "out_t"))

    ix = [n.buf(ctx, f"ix{i}", [P, GROUPS], I32) for i in range(2)]
    sd = [n.buf(ctx, f"sd{i}", [P, 2, GROUPS], F32) for i in range(2)]
    q3 = [n.buf(ctx, f"q3_{i}", [P, 3, D], BF16) for i in range(2)]
    kv = [n.buf(ctx, f"kv_{i}", [P, GROUPS, 2 * D], F32) for i in range(2)]
    row = [n.buf(ctx, f"row_{i}", [P, WIDE], F8) for i in range(2)]
    col = [n.buf(ctx, f"col_{i}", [P, 2 * GROUPS, P], F8) for i in range(2)]
    hs = [n.buf(ctx, f"hs{i}", [P, CHUNK, P], BF16) for i in range(2)]
    hd = [n.buf(ctx, f"hd{i}", [P, CHUNK, GROUP], BF16) for i in range(2)]
    hsT = [n.buf(ctx, f"hsT{i}", [P, CHUNK, P], BF16) for i in range(2)]
    hs32 = [n.buf(ctx, f"hs32_{i}", [P, CHUNK, P], F32) for i in range(HOT32)]
    qk = [n.buf(ctx, f"qk{i}", [P, CHUNK * D], F32) for i in range(2)]
    sc = [n.buf(ctx, f"sc{i}", [P, CHUNK * HEADS], F32) for i in range(2)]
    wv = [n.buf(ctx, f"wv{i}", [P, CHUNK, AV], F32) for i in range(2)]
    rden = [n.buf(ctx, f"rden{i}", [P, HEADS], F32) for i in range(2)]
    most = n.buf(ctx, "most", [P, 2 * UP], F32)
    pt = n.bank(ctx, "pt", BF16)
    pq = [n.bank(ctx, f"pq{i}") for i in range(2)]
    pr = n.bank(ctx, "pr")
    pa = [n.bank(ctx, f"pa{i}") for i in range(4)]

    def gather(X, b):
        for e in range(b * CHUNKS, (b + 1) * CHUNKS):
            wait(pool, weighted.at(X, e - CP))
            if e == b * CHUNKS:
                wait(pool, *(gathered[x].at(X, -1) for x in range(e, e + CHUNKS)))
                wait(pool, indexed.at(X, b - 1))
                indexed.by(pool.tensor_copy(ix[b][:], s.idx[:, 2 * X + b, :]))
                wait(pool, indexed.at(X, b))
            settle(pool, n.spare)
            for g in range(e % CHUNKS * CHUNK, (e % CHUNKS + 1) * CHUNK):
                pool.indirect_dma_start(kv[b][:, g, :], None, s.kv_d, bass.IndirectOffsetOnAxis(
                    ap=ix[b][:, g:g + 1], axis=0)).then_inc(gathered[e].sem, 16)

    def store(X, b):
        for t in (out_c.at(X, UP * (b + 1) - 1), out_t.at(X, UP * (b + 1) - 1)):
            wait(sp, t)
            settle(sp, n.spare)
        sp.dma_start(s.c_d[2 * X + b, :, :], row[b][:].bitcast(U8)).then_inc(n.row.sem, 16)
        sp.dma_start(s.t_d[2 * X + b, :, :], col[b][:].bitcast(U8).rearrange("p m e -> p (m e)")).then_inc(n.row.sem, 16)
        wait(sp, (n.row, X * 64 + 32 * (b + 1)))
        sp.sem_inc(stored.sem, 1)

    def units(e):
        g1 = (e % CHUNKS + 1) * CHUNK
        return [(g // 2 + UP * (e // CHUNKS), g - g % 2, g % 2 + 1)
                for g in range(g1 - CHUNK, g1) if g % 2 == 1 or g == GROUPS - 1]

    def one_hots(X, e):
        b, k, g0 = e // CHUNKS, e % 2, (e % CHUNKS) * CHUNK
        if g0 == 0:
            wait(v, hot.at(X, e - 1))
            t = n.V(v.tensor_copy(sd[b][:], s.slots[:, :, 2 * X + b, :]))
            wait(v, t)
        wait(v, queried.at(X, e - 2), wide.at(X, e - 2))
        for g in range(CHUNK):
            v.tensor_scalar(hs[k][:, g, :], s.count1[:, 0:P], sd[b][:, 0, g0 + g:g0 + g + 1], None, ALU.is_equal)
            t = v.tensor_scalar(hd[k][:, g, :], s.count1[:], sd[b][:, 1, g0 + g:g0 + g + 1], None, ALU.is_equal)
        hot.by(t)

    def turn(X, e):
        wait(pe, hot.at(X, e), copied.at(X, e - 1))
        for g in range(CHUNK):
            t = pe.transpose(pt[:, g * P:(g + 1) * P], hs[e % 2][:, g, :], s.identb[:])
        turned.by(t)

    def copy_turned(X, e):
        wait(a, turned.at(X, e), queried.at(X, e - 2))
        copied.by(a.activation(hsT[e % 2][:].rearrange("p g e -> p (g e)"), pt[:, 0:CHUNK * P], ACT.Copy))

    def copy_wide(X, e):
        wait(a, hot.at(X, e), summed.at(X, e - HOT32))
        wide.by(a.activation(hs32[e % HOT32][:], hs[e % 2][:], ACT.Copy))

    def copy_q(X, b):
        wait(a, queried.at(X, CHUNKS * (b + 1) - 1 - CP))
        q_in.by(a.activation(q3[b][:], s.q3[:, 2 * X + b, :, :], ACT.Copy))

    def query(X, e):
        b, k = e // CHUNKS, e % 2
        wait(pe, copied.at(X, e), scored.at(X, e - 2))
        if e % CHUNKS == 0:
            wait(pe, q_in.at(X, b))
        for g in range(CHUNK):
            for part in range(3):
                t = pe.matmul(pq[k][:, g * D:(g + 1) * D], hsT[k][:, g, :], q3[b][:, part, :],
                              start=part == 0, stop=part == 2)
        queried.by(t)

    def build(X, e):
        k, b, g0 = e % 2, e // CHUNKS, (e % CHUNKS) * CHUNK
        for g in range(CHUNK):
            at = g0 + g
            u, half = at // 2 + UP * b, at % 2
            last = half == 1 or at == GROUPS - 1
            bc, bt = pa[2 * (u % 2)], pa[2 * (u % 2) + 1]
            if half == 0:
                wait(pe, out_c.at(X, u - 2), out_t.at(X, u - 2))
            t = pe.matmul(bc[:, half * GROUP:(half + 1) * GROUP], hs[k][:, g, :], hd[k][:, g, :], start=True, stop=True)
            if last:
                built_c.by(t)
            for m in range(2):
                t = pe.matmul(bt[:, half * GROUP + m * P:half * GROUP + (m + 1) * P],
                              hd[k][:, g, m * P:(m + 1) * P], hs[k][:, g, :], start=True, stop=True)
            if last:
                built_t.by(t)

    def split_units(e, early):
        last_begun = ((e % CHUNKS + 1) * CHUNK - 1) // 2 + UP * (e // CHUNKS)
        return [x for x in units(e) if (x[0] + 2 <= last_begun) == early]

    def evacuate_c(X, e, early=False):
        b = e // CHUNKS
        if e % CHUNKS == 0:
            wait(v, stored.at(X, b - 2))
        for u, g, count in split_units(e, early):
            wait(v, built_c.at(X, u), out_c.at(X, u - 1))
            settle(v, n.spare)
            out_c.by(v.tensor_scalar(row[b][:, g * GROUP:(g + count) * GROUP], pa[2 * (u % 2)][:, 0:count * GROUP],
                                     0.0, most[:, u:u + 1], ALU.add, ALU.max, accum_out=most[:, u:u + 1],
                                     saturate=False))

    def evacuate_t(X, e, early=False):
        b = e // CHUNKS
        if e % CHUNKS == 0:
            wait(a, stored.at(X, b - 2))
        for u, g, count in split_units(e, early):
            wait(a, built_t.at(X, u))
            settle(a, n.spare)
            out_t.by(a.activation(col[b][:, 2 * g:2 * (g + count), :].rearrange("p m e -> p (m e)"),
                                  pa[2 * (u % 2) + 1][:, 0:count * GROUP], ACT.Copy, saturate=False))

    def score(X, e):
        b, k, g0 = e // CHUNKS, e % 2, (e % CHUNKS) * CHUNK
        wait(v, gathered[e].at(X, 16 * CHUNK - 1))
        wait(v, queried.at(X, e), clipped.at(X, e - 2), exped.at(X, e - 2))
        scored.by(v.tensor_tensor(qk[k][:].rearrange("p (g d) -> p g d", d=D),
                                  pq[k][:, 0:CHUNK * D].rearrange("p (g d) -> p g d", d=D),
                                  kv[b][:, g0:g0 + CHUNK, 0:D], ALU.mult))
        wait(v, scored.at(X, e))
        t = n.V(v.tensor_reduce(sc[k][:], qk[k][:].rearrange("p (h d) -> p h d", d=DH), AX.X, ALU.add))
        wait(v, t)
        clipped.by(v.tensor_scalar(sc[k][:], sc[k][:], 10.0, -10.0, ALU.min, ALU.max))

    def exponent(X, e):
        k = e % 2
        wait(a, clipped.at(X, e), summed.at(X, e - 2))
        exped.by(a.activation(wv[k][:, :, D:D + HEADS], sc[k][:].rearrange("p (g h) -> p g h", h=HEADS), ACT.Exp))

    def weigh(X, e):
        b, k, g0 = e // CHUNKS, e % 2, (e % CHUNKS) * CHUNK
        wait(v, exped.at(X, e))
        weighted.by(v.tensor_tensor(
            wv[k][:, :, 0:D].rearrange("p g (h d) -> p g h d", d=DH),
            kv[b][:, g0:g0 + CHUNK, D:2 * D].rearrange("p g (h d) -> p g h d", d=DH),
            wv[k][:, :, D:D + HEADS].unsqueeze(3).to_broadcast([P, CHUNK, HEADS, DH]), ALU.mult))

    def total(X, e):
        b, k, g0 = e // CHUNKS, e % 2, (e % CHUNKS) * CHUNK
        wait(pe, weighted.at(X, e), wide.at(X, e))
        if g0 == 0:
            wait(pe, normed.at(X, b - 1))
        for g in range(CHUNK):
            t = pe.matmul(pr[:, 0:AV], hs32[e % HOT32][:, g, :], wv[k][:, g, :],
                          start=g0 + g == 0, stop=g0 + g == GROUPS - 1)
        summed.by(t)

    def normalize(X, e):
        b = e // CHUNKS
        wait(v, summed.at(X, e), normed.at(X, b - 2))
        t = n.V(v.tensor_scalar(rden[b][:], pr[:, D:D + HEADS], EPS_ATT, None, ALU.add))
        wait(v, t)
        t = n.V(v.reciprocal(rden[b][:], rden[b][:]))
        wait(v, t)
        n.V(v.tensor_tensor(s.R[:, 2 * X + b, :].rearrange("p (h d) -> p h d", d=DH),
                            pr[:, 0:D].rearrange("p (h d) -> p h d", d=DH), over(rden[b][:], DH), ALU.mult))
        wait(v, n.sv.now())
        normed.by(v.tensor_copy(s.odeg[:, bass.ds(2 * X + b, 1)], pr[:, AV - 1:AV]))

    def step(X, c, first=False, chunks=CP):
        def behind(stages, lag):
            e = c - lag
            if e < 0 and not first:
                for f in stages:
                    f(X - 1, e + CP)
            elif 0 <= e < chunks:
                for f in stages:
                    f(X, e)

        behind([weigh, total], 3)
        behind([evacuate_t], 1)
        behind([one_hots, turn, copy_turned, copy_wide], 0)
        behind([evacuate_c], 1)
        if (c - 4) % CP in (CHUNKS - 1, CP - 1):
            behind([normalize], 4)
        if c % CP in (0, CHUNKS - 2) and c < chunks - 1:
            copy_q(X, int(c > 0))
        behind([query], 1)
        behind([build], 0)
        behind([score, exponent], 2)
        behind([lambda x, e: evacuate_c(x, e, True), lambda x, e: evacuate_t(x, e, True)], 0)
        if c % CHUNKS == 0:
            behind([lambda x, e: store(x, e // CHUNKS)], 1)

    n.meet(v, a, pe, pool)
    for i in range(2):
        n.V(v.memset(wv[i][:, :, AV - 1:AV], 1.0))
    n.V(v.memset(most[:], 0.0))
    n.meet(v, a, pe, pool)
    LAG = 4
    last_tiles = TILES - 2 * (PAIRS - 1)
    for b in range(2):
        gather(0, b)
    with pool.Fori(1, PAIRS - 1) as X:
        for b in range(2):
            gather(X, b)
    for b in range(last_tiles):
        gather(PAIRS - 1, b)
    for c in range(LAG):
        step(0, c, first=True)
    with n.loop(PAIRS - 1, sv=18) as i:
        for c in range(LAG, CP):
            step(i, c)
        for c in range(LAG):
            step(i + 1, c)
    for c in range(LAG, last_tiles * CHUNKS + LAG):
        step(PAIRS - 1, c, chunks=last_tiles * CHUNKS)
    n.row.count += 32 * TILES
    n.meet(v, a, pe, pool, sp)
    for e in (v, a, pe, pool, sp):
        wait(e, n.row.now(), normed.at(PAIRS - 1, last_tiles - 1), out_t.at(PAIRS - 1, last_tiles * UP - 1))
    t = n.V(v.tensor_reduce(s.most[:], most[:], AX.X, ALU.max))
    n.meet(v, a, pe, pool, sp)


def aggregate(n, s, ps, panels, U, cols, finish, ready=None):
    pe, sp = n.pe, n.sp
    mat = s.t_d if panels else s.c_d

    if not panels:
        wait(sp, n.done.now())

    def body(i):
        used0, free0, done0 = n.used.now(), n.free.now(), n.done.now()
        for r in range(RING):
            if panels or r == RING - 1:
                wait(sp, (n.done, done0[1] + (r + 1) - RING))
            else:
                wait(sp, (n.used, used0[1] + (r + 1) - (RING - 1)))
            settle(sp, n.spare)
            slot = s.ring[:, r, :]
            if panels:
                src = mat[RING * i + r, :, 0:PANEL]
                n.ring[r].by(sp.dma_start(slot, src), 16)
            else:
                src = mat[r * RING:(r + 1) * RING, :, bass.ds(i * (RING * P), RING * P)].rearrange("t p e -> p t e")
                n.ring[r].by(sp.dma_start(slot.rearrange("p (t e) -> p t e", t=RING), src), 16)
        w8 = s.ring[:].bitcast(F8)
        if panels:
            for r in range(RING):
                wait(pe, n.ring[r].now(), (n.free, free0[1] + (r + 1) - RING))
                settle(pe, n.spare)
                w = w8[:, r, :].rearrange("p (k e) -> p k e", e=P)
                for k in range(TILES):
                    if r == 0 and k == TILES - RING:
                        wait(pe, *ready)
                        settle(pe, n.spare)
                    t = pe.matmul(ps[r][:, 0:cols], w[:, k, :], U[:, k, 0:cols], start=k == 0, stop=k == TILES - 1)
                t = n.done.by(t)
                finish(i, r, ps[r], t)
        else:
            ends = []
            for r in range(RING):
                wait(pe, n.ring[r].now())
                if ready:
                    wait(pe, *ready[r])
                settle(pe, n.spare)
                w = w8[:, r, :].rearrange("p (t j e) -> p t j e", t=RING, j=RING)
                for q in range(RING):
                    for j in range(RING):
                        if r == 0 and q == 0:
                            wait(pe, (n.free, free0[1] + (j + 1) - RING))
                            settle(pe, n.spare)
                        t = pe.matmul(ps[j][:, 0:cols], w[:, q, j, :], U[:, r * RING + q, 0:cols],
                                      start=r == q == 0, stop=r == q == RING - 1)
                        if r == q == RING - 1:
                            ends.append(n.done.by(t))
                if r < RING - 1:
                    n.used.by(t)
            for j in range(RING):
                finish(i, j, ps[j], ends[j])
    return body


def split16_stages(n, src, U, at):
    v, a = n.v, n.a
    return [
        stage(n, (a, lambda k: a.activation(U[:, k, at:at + D], src[:, k, :], ACT.Copy))),
        stage(n, (v, lambda k: v.tensor_tensor(src[:, k, :], src[:, k, :], U[:, k, at:at + D], ALU.subtract))),
        stage(n, (a, lambda k: a.activation(U[:, k, at + D:at + 2 * D], src[:, k, :], ACT.Copy, scale=LO)))]


def softmax_dense(n, s, ps):
    v, a = n.v, n.a
    with ExitStack() as ctx:
        cols = 4 * D + 1
        U = n.buf(ctx, "u1", [P, TILES, cols], F16)
        lo = n.buf(ctx, "lo1", [P, RING, 2, D], F32)
        dn = n.buf(ctx, "dn1", [P, RING, 2, D], F32)
        e = n.buf(ctx, "e1", [P, RING, D], F32)
        Y = n.buf(ctx, "y1", [P, TILES, D], F32)
        n.V(v.memset(U[:, :, cols - 1:cols], 1.0))
        x_in = stage(n, (v, lambda k: v.tensor_tensor(s.X[:, k, :], s.X[:, k, :], s.T[:, k, :], ALU.add)))
        exps = stage(n, (a, lambda k: a.activation(s.T[:, k, :], s.H[:, k, :], ACT.Exp)))
        prods = stage(n, (v, lambda k: v.scalar_tensor_tensor(Y[:, k, :], s.H[:, k, :], 0.25, s.T[:, k, :],
                                                              ALU.mult, ALU.mult)))
        ready = by_blocks([x_in] + layernorm_stages(n, s) + [exps, prods] +
                          split16_stages(n, s.T, U, 0) + split16_stages(n, Y, U, 2 * D), [n.sv.now(), n.sa.now()], apart=APART)

        def finish(i, j, p_, t):
            sums = p_[:, 0:4 * D].rearrange("p (w h d) -> p w h d", w=2, h=2)
            wait(a, t)
            t = n.A(a.activation(lo[:, j, :, :], sums[:, :, 1, :], ACT.Copy, scale=1.0 / LO))
            wait(v, t)
            t = n.V(v.tensor_tensor(dn[:, j, :, :], lo[:, j, :, :], sums[:, :, 0, :], ALU.add))
            n.free.by(v.tensor_copy(s.ideg[:, bass.ds(RING * i + j, 1)], p_[:, cols - 1:cols]))
            if j < RING - 1:
                return
            tiles = bass.ds(RING * i, RING)
            den, num, inv = dn[:, :, 0, :], dn[:, :, 1, :], lo[:, :, 0, :]
            wait(v, t)
            n.V(v.tensor_scalar(e[:], den, 0.5, EPS_MSG, ALU.is_gt, ALU.mult))
            t = n.V(v.tensor_scalar(inv, den, 0.5, None, ALU.max))
            wait(v, t)
            t = n.V(v.reciprocal(inv, inv))
            wait(v, t)
            t = n.V(v.scalar_tensor_tensor(num, num, 4.0, inv, ALU.mult, ALU.mult))
            wait(v, t)
            t = n.V(v.tensor_tensor(num, num, e[:], ALU.add))
            wait(v, t)
            n.V(v.tensor_tensor(s.T[:, tiles, :], num, s.H[:, tiles, :], ALU.add))

        n.meet(v, a)
        body = aggregate(n, s, ps, False, U, cols, finish, ready)
        with n.loop(BODIES, used=RING - 1, free=RING, done=RING, sv=RING + 6, sa=RING,
                    **{f"ring{r}": 16 for r in range(RING)}) as i:
            n.meet(v, a)
            body(i)
        n.meet(v, a, n.pe, n.pool)


def degree_buffers(n, s, ctx):
    s.rc, s.out, s.g, s.dinv, s.dinv_out = (
        n.buf(ctx, x, [P, TILES], F32) for x in ("col_rc", "col_out", "col_g", "col_dinv", "col_dinv_out"))


def degree_columns(n, s):
    v = n.v
    n.meet(v, n.a)
    t = n.V(v.tensor_scalar(s.g[:], s.odeg[:, 0:TILES], 1.0, None, ALU.max))
    inv_sqrt(n, s.g, s.g, t)
    t = n.V(v.tensor_scalar(s.rc[:], s.ideg[:], 1.0, None, ALU.max))
    inv_sqrt(n, s.rc, s.rc, t)
    t = n.V(v.tensor_scalar(s.dinv[:], s.ideg[:], 1.0, None, ALU.add))
    t = inv_sqrt(n, s.dinv, s.dinv, t)
    wait(v, t)
    n.V(v.scalar_tensor_tensor(s.g[:], s.g[:], BETA, s.rc[:], ALU.mult, ALU.mult))
    t = n.V(v.reciprocal(s.out[:], s.rc[:]))
    n.V(v.tensor_scalar(s.dinv_out[:], s.dinv[:], 1.0 / SCALE, None, ALU.mult))
    wait(v, t)
    n.V(v.tensor_scalar(s.out[:], s.out[:], 1.0 / (SCALE * THETA), None, ALU.mult))
    n.meet(v, n.a)


def appnp_begin_stages(n, s):
    v = n.v
    return [
        stage(n, (v, lambda k: v.scalar_tensor_tensor(s.T[:, k, :], s.H[:, k, :], SCALE, over(s.rc[:, k], D),
                                                      ALU.mult, ALU.mult))),
        stage(n, (v, lambda k: v.tensor_scalar(s.H[:, k, :], s.T[:, k, :], ALPHA, None, ALU.mult)))]


def appnp_end_stages(n, s):
    v = n.v
    return [
        stage(n, (v, lambda k: v.tensor_tensor(s.T[:, k, :], s.T[:, k, :], over(s.out[:, k], D), ALU.mult))),
        stage(n, (v, lambda k: v.tensor_tensor(s.X[:, k, :], s.X[:, k, :], s.T[:, k, :], ALU.add)))]


def appnp_dense(n, s, w):
    v, a, pe = n.v, n.a, n.pe
    g = s.g
    with ExitStack() as ctx:
        Ua = n.buf(ctx, "u2a", [P, TILES, 2 * D], F16)
        Ub = n.buf(ctx, "u2b", [P, TILES, 2 * D], F16)
        lo = [n.buf(ctx, f"lo2_{j}", [P, D], F32) for j in range(RING)]
        z = [n.buf(ctx, f"z2_{j}", [P, D], F32) for j in range(RING)]
        uf = [n.buf(ctx, f"uf2_{j}", [P, D], F32) for j in range(RING)]
        res = [n.buf(ctx, f"r2_{j}", [P, D], F32) for j in range(RING)]
        degree_columns(n, s)
        with ExitStack() as first:
            by_blocks([linear_stage(n, s, linear_banks(n, first, "l1"), s.T, w, D, True, add_to_x(n, s))] +
                      layernorm_stages(n, s) + appnp_begin_stages(n, s) + split16_stages(n, s.T, Ua, 0))
            n.meet(v, a, pe)
        ps = [n.bank(ctx, f"sum2_{j}") for j in range(RING)]

        def finish_into(Un):
            def finish(i, j, p_, t):
                tile = bass.ds(RING * i + j, 1)
                wait(a, t)
                t = n.A(a.activation(lo[j][:], p_[:, D:2 * D], ACT.Copy, scale=1.0 / LO))
                wait(v, t)
                t = n.free.by(v.tensor_tensor(z[j][:], lo[j][:], p_[:, 0:D], ALU.add))
                wait(v, t)
                part = s.H[:, tile, :].rearrange("p a d -> p (a d)")
                t = n.V(v.scalar_tensor_tensor(uf[j][:], z[j][:], g[:, tile], part, ALU.mult, ALU.add))
                wait(a, t)
                hi = Un[:, tile, 0:D].rearrange("p a d -> p (a d)")
                t = n.A(a.activation(hi, uf[j][:], ACT.Copy))
                n.A(a.activation(s.T[:, tile, :], uf[j][:].unsqueeze(1), ACT.Copy))
                wait(v, t)
                t = n.V(v.tensor_tensor(res[j][:], uf[j][:], hi, ALU.subtract))
                wait(a, t)
                n.A(a.activation(Un[:, tile, D:2 * D].rearrange("p a d -> p (a d)"), res[j][:], ACT.Copy, scale=LO))
            return finish

        per = dict(free=RING, done=RING, sv=2 * RING, sa=4 * RING,
                   **{f"ring{r}": 16 for r in range(RING)})
        with n.loop(STEPS // 2, **{k: 2 * BODIES * c for k, c in per.items()}):
            for U, Un in ((Ua, Ub), (Ub, Ua)):
                wait(pe, n.sv.now(-2 * RING), n.sa.now(-4 * RING))
                body = aggregate(n, s, ps, True, U, 2 * D, finish_into(Un), [n.sv.now(), n.sa.now()])
                with n.loop(BODIES, **per) as i:
                    n.meet(v, a)
                    body(i)
        n.meet(v, a, pe, n.pool)


def add_self_loop(n, s, i, t, z, UD, scale):
    v = n.v
    tiles = bass.ds(RING * i, RING)
    wait(v, t)
    t = n.V(v.tensor_tensor(z[:], z[:], UD[:, tiles, :], ALU.add))
    wait(v, t)
    n.V(v.tensor_tensor(s.T[:, tiles, :], z[:], over(scale[:, tiles], D), ALU.mult))


def gcn_dense(n, s, ps):
    v, a, pe = n.v, n.a, n.pe
    dinv, g = s.dinv, s.dinv_out
    ring_per = dict(used=RING - 1, free=RING, done=RING, **{f"ring{r}": 16 for r in range(RING)})
    with ExitStack() as ctx:
        U = n.buf(ctx, "u3", [P, TILES, 3 * D], F16)
        UD = n.buf(ctx, "ud3", [P, TILES, D], F32)
        lo = n.buf(ctx, "lo3", [P, RING, D], F32)
        z = n.buf(ctx, "z3", [P, RING, D], F32)
        scaled = stage(n, (v, lambda k: v.scalar_tensor_tensor(UD[:, k, :], s.H[:, k, :], SCALE, over(dinv[:, k], D),
                                                               ALU.mult, ALU.mult)))
        again = stage(n, (a, lambda k: a.activation(s.T[:, k, :], UD[:, k, :], ACT.Copy)))
        ready = by_blocks(appnp_end_stages(n, s) + layernorm_stages(n, s) + [scaled, again] +
                          split16_stages(n, s.T, U, 0), [n.sv.now(), n.sa.now()], apart=APART)

        def finish(i, j, p_, t):
            wait(a, t)
            t = n.A(a.activation(lo[:, j, :], p_[:, D:2 * D], ACT.Copy, scale=1.0 / LO))
            wait(v, t)
            t = n.free.by(v.tensor_tensor(z[:, j, :], lo[:, j, :], p_[:, 0:D], ALU.add))
            if j == RING - 1:
                add_self_loop(n, s, i, t, z, UD, g)

        n.meet(v, a)
        body = aggregate(n, s, ps, False, U, 2 * D, finish, ready)
        with n.loop(BODIES, sv=2, sa=RING, **ring_per) as i:
            n.meet(v, a)
            body(i)
        n.meet(v, a, pe, n.pool)


def gcn_second_dense(n, s, ps):
    v, a, pe = n.v, n.a, n.pe
    dinv = s.dinv
    ring_per = dict(used=RING - 1, free=RING, done=RING, **{f"ring{r}": 16 for r in range(RING)})
    with ExitStack() as ctx:
        U = n.buf(ctx, "u4", [P, TILES, 2 * D], F16)
        UD = n.buf(ctx, "ud4", [P, TILES, D], F32)
        lo = n.buf(ctx, "lo4", [P, RING, D], F32)
        z = n.buf(ctx, "z4", [P, RING, D], F32)
        high = n.buf(ctx, "high4", [P, D], F32)
        unit = n.buf(ctx, "unit4", [P, D], F32)
        per_unit = n.buf(ctx, "per_unit4", [P, D], F32)
        diag = n.buf(ctx, "diag4", [D, D], F32)

        t = n.V(v.tensor_tensor(UD[:], s.H[:], over(dinv[:], D), ALU.mult))
        wait(v, t)
        t = n.V(v.tensor_reduce(high[:], UD[:].rearrange("p k d -> p d k"), AX.X, ALU.max))
        wait(pe, t)
        t = n.E(pe.transpose(ps[0][0:D, 0:P], high[:], s.ident[:]))
        wait(v, t)
        t = n.V(v.tensor_reduce(unit[0:D, 0:1], ps[0][0:D, 0:P], AX.X, ALU.max))
        wait(v, t)
        t = n.V(v.tensor_scalar(unit[0:D, 0:1], unit[0:D, 0:1], 1e-30, 1.0 / TOP, ALU.max, ALU.mult))
        wait(v, t)
        t = n.V(v.tensor_scalar(diag[:], s.ident[0:D, 0:D], unit[0:D, 0:1], None, ALU.mult))
        wait(pe, t)
        t = n.E(pe.matmul(ps[1][:, 0:D], s.ones[0:D, :], diag[:], start=True, stop=True))
        wait(v, t)
        t = n.V(v.tensor_copy(unit[:], ps[1][:, 0:D]))
        wait(v, t)
        t = n.V(v.reciprocal(per_unit[:], unit[:]))
        scaled = stage(n, (v, lambda k: v.tensor_tensor(s.T[:, k, :], UD[:, k, :], under(per_unit[:], RING), ALU.mult)))
        ready = by_blocks([scaled] + split16_stages(n, s.T, U, 0), [t, n.sa.now()])

        def finish(i, j, p_, t):
            wait(a, t)
            t = n.A(a.activation(lo[:, j, :], p_[:, D:2 * D], ACT.Copy, scale=1.0 / LO))
            wait(v, t)
            t = n.free.by(v.tensor_tensor(z[:, j, :], lo[:, j, :], p_[:, 0:D], ALU.add))
            if j == RING - 1:
                wait(v, t)
                t = n.V(v.tensor_tensor(z[:], z[:], under(unit[:], RING), ALU.mult))
                add_self_loop(n, s, i, t, z, UD, dinv)

        n.meet(v, a)
        body = aggregate(n, s, ps, False, U, 2 * D, finish, ready)
        with n.loop(BODIES, sv=3, sa=RING, **ring_per) as i:
            n.meet(v, a)
            body(i)
        n.meet(v, a, pe, n.pool)


class Store:
    pass


def add_to_x(n, s):
    def finish(i, j, p_, t):
        x = s.X[:, bass.ds(RING * i + j, 1), :].rearrange("p a d -> p (a d)")
        wait(n.v, t)
        return n.V(n.v.tensor_tensor(x, p_, x, ALU.add))
    return finish


def relu_to_h(n, s):
    def finish(i, j, p_, t):
        wait(n.a, t)
        return n.A(n.a.activation(s.H[:, bass.ds(RING * i + j, 1), :].rearrange("p a d -> p (a d)"), p_, ACT.Relu))
    return finish


def relu_add_to_x(n, s):
    def finish(i, j, p_, t):
        x = s.X[:, bass.ds(RING * i + j, 1), :].rearrange("p a d -> p (a d)")
        wait(n.v, t)
        return n.V(n.v.scalar_tensor_tensor(x, p_, 0.0, x, ALU.max, ALU.add))
    return finish


def keep_tile(n, into):
    def finish(i, j, p_, t):
        wait(n.v, t)
        return n.V(n.v.tensor_copy(into[:, bass.ds(RING * i + j, 1), :].rearrange("p a d -> p (a d)"), p_))
    return finish


def split_q(n, s, q):
    half = TILES // 2
    parts = [slice(0, half), slice(half, TILES)]
    at = [n.sv.now()] * 2
    for part in range(3):
        for h, tiles in enumerate(parts):
            wait(n.a, at[h])
            at[h] = n.A(n.a.activation(s.q3[:, tiles, part, :], q[:, tiles, :], ACT.Copy))
        for h, tiles in enumerate(parts):
            if part < 2:
                wait(n.v, at[h])
                at[h] = n.V(n.v.tensor_tensor(q[:, tiles, :], q[:, tiles, :], s.q3[:, tiles, part, :], ALU.subtract))


def gnn(nc, x_in, src_in, dst_in, qw, kw, vw, w1, b1, w31, b31, w32, b32, out):
    with ExitStack() as top:
        n = Net(nc, top)
        v, a, pe, pool, sp = n.v, n.a, n.pe, n.pool, n.sp
        s = Store()
        s.kv_d = nc.dram_tensor("kv_rows", [NODES, 2 * D], F32).ap()
        s.c_d = nc.dram_tensor("adjacency", [BTILES, P, WIDE], U8).ap()
        s.t_d = nc.dram_tensor("adjacency_t", [BTILES, P, WIDE], U8).ap()
        s.X = n.buf(top, "X", [P, TILES, D], F32)
        s.H = n.buf(top, "H", [P, TILES, D], F32)
        s.R = n.buf(top, "T", [P, BTILES, D], F32)
        s.T = s.R[:, 0:TILES, :]
        s.ident = n.buf(top, "ident", [P, P], F32)
        s.identb = n.buf(top, "identb", [P, P], BF16)
        s.count1 = n.buf(top, "count1", [P, GROUP], BF16)
        s.tri = n.buf(top, "tri", [P, P], BF16)
        s.ones = n.buf(top, "ones", [P, P], F32)
        s.odeg = n.buf(top, "odeg", [P, BTILES], F32)
        s.ideg = n.buf(top, "ideg", [P, TILES], F32)
        s.most = n.buf(top, "most_all", [P, 1], F32)
        s.full = n.buf(top, "full", [P, 1], F32)
        fits = n.buf(top, "fits", [1, 1], I32)
        s.filled = n.buf(top, "filled", [1, 1], F32)
        s.col = [n.buf(top, f"col{i}", [P, TILES], F32) for i in range(3)]
        s.stage = n.buf(top, "stage", [P, RING, D], F32)
        s.aT = n.buf(top, "aT", [P, RING * P], F32)
        wq = n.buf(top, "wq", [D, 3 * D], F32)
        wl = [n.buf(top, f"wl{i}", [D + 1, D], F32) for i in range(3)]

        n.G(pool.memset(s.ones[:], 1.0))
        n.G(pool.memset(s.ident[:], 0.0))
        t = n.G(pool.iota(s.count1[:], [[1, GROUP]], base=1, channel_multiplier=0,
                          allow_small_or_imprecise_dtypes=True))
        wait(pool, t)
        n.G(pool.affine_select(out=s.ident[:], in_=s.ident[:], compare_op=ALU.not_equal, fill=1.0, base=0,
                               pattern=[[-1, P]], channel_multiplier=1))
        t_const = n.G(pool.affine_select(out=s.tri[:], in_=s.ones[:], compare_op=ALU.is_gt, fill=0.0, base=0,
                                         pattern=[[1, P]], channel_multiplier=-1))
        wait(v, t_const)
        n.V(v.tensor_copy(s.identb[:], s.ident[:]))
        n.V(v.memset(s.aT[D:D + 1, :], 1.0))
        wait(pe, t_const)

        with ExitStack() as ctx:
            s.q3 = n.buf(ctx, "q3", [P, BTILES, 3, D], BF16)
            s.slots = n.buf(ctx, "slots", [P, 2, BTILES, GROUPS], F32)
            s.idx = n.buf(ctx, "idx", [P, BTILES, GROUPS], I32)
            s.slotmax = n.buf(ctx, "slotmax", [P, BTILES * GROUPS], BF16)
            with ExitStack() as c2:
                s.es = n.buf(c2, "es", [P, GROUPS, RUN], I32)
                s.ed = n.buf(c2, "ed", [P, GROUPS, RUN], I32)
                s.dall = n.buf(c2, "dall", [SCAN, COLS], I32)
                n.eg.by(sp.dma_start(s.dall[:], dst_in.rearrange("(p e) -> p e", p=SCAN)), 16)
                t = n.V(v.memset(s.X[:, TILES - 1, :], 0.0))
                for i, w in enumerate((qw, kw, vw)):
                    sp.dma_start(wq[:, i * D:(i + 1) * D], w).then_inc(n.ld.sem, 16)
                for b_, w, bias in zip(wl, (w1, w31, w32), (b1, b31, b32)):
                    sp.dma_start(b_[0:D, :], w).then_inc(n.ld.sem, 16)
                    sp.dma_start(b_[D:D + 1, :], bias.rearrange("(a n) -> a n", a=1)).then_inc(n.ld.sem, 16)
                sp.dma_start(s.X[:, 0:TILES - 1, :],
                             x_in[0:NODES - LAST, :].rearrange("(k p) f -> p k f", p=P)).then_inc(n.ld.sem, 16)
                wait(sp, t)
                sp.dma_start(s.X[0:LAST, TILES - 1, :], x_in[NODES - LAST:NODES, :]).then_inc(n.ld.sem, 16)
                n.ld.count += 16 * 11
                t_loaded = n.ld.now()
                t_edges = load_edges(n, s, src_in, dst_in)
                for e in (v, a, pe):
                    wait(e, t_loaded)
                layernorm_relu(n, s)
                n.V(v.memset(s.q3[:, TILES:BTILES, :, :], 0.0))
                n.V(v.memset(s.slots[:, :, TILES:BTILES, :], 0.0))
                for e in (v, a, pe, pool):
                    wait(e, t_edges)
                with ExitStack() as c3:
                    qkv = n.buf(c3, "qkv", [P, TILES, 3 * D], F32)
                    linear(n, s, "qkv", s.H, wq, 3 * D, False, keep_tile(n, qkv), sv=RING, sa=3, se=2 * RING)
                    wait(sp, n.sv.now())
                    sp.dma_start(s.kv_d[0:NODES - LAST, :].rearrange("(k p) f -> p k f", p=P),
                                 qkv[:, 0:TILES - 1, D:3 * D]).then_inc(n.ld.sem, 16)
                    sp.dma_start(s.kv_d[NODES - LAST:NODES, :], qkv[0:LAST, TILES - 1, D:3 * D]).then_inc(n.ld.sem, 16)
                    n.ld.count += 32
                    split_q(n, s, qkv[:, :, 0:D])
                    for e in (v, pool, sp, a):
                        wait(e, n.ld.now())
                    n.meet(v, a, pe, pool)
                n.G(pool.tensor_tensor(s.X[:], s.X[:], s.H[:], ALU.add))
                bucket_edges(n, s)
            attention_and_adjacency(n, s, ctx)
        with ExitStack() as ctx:
            pf = n.bank(ctx, "pf")
            high = n.buf(ctx, "high", [1, 1], F32)
            wait(pe, n.sv.now())
            t = n.E(pe.matmul(pf[0:1, 0:P], s.most[:], s.ident[:], start=True, stop=True))
            wait(v, t)
            t = n.V(v.tensor_reduce(high[:], pf[0:1, 0:P], AX.X, ALU.max))
            wait(v, t)
            t = n.V(v.tensor_scalar(high[:], high[:], EXACT, None, ALU.is_le))
            wait(v, t)
            t = n.V(v.tensor_scalar(s.filled[:], s.filled[:], float(EDGES), None, ALU.is_equal))
            wait(v, t)
            t = n.V(v.tensor_tensor(fits[:], s.filled[:], high[:], ALU.mult))
            for e in (v, a, pe, pool, sp):
                wait(e, t)
            dense = nc.values_load(fits[0:1, 0:1], min_val=0, max_val=1)
            n.meet(v, a, pe, pool, sp)
        degree_buffers(n, s, top)
        before = [sig.count for _, sig in n.sigs]
        with nc.If(dense > 0):
            dense_layers(n, s, wl, out)
        for (_, sig), count in zip(n.sigs, before):
            sig.count = count
        with nc.Else():
            edge_layers(n, s, wq, wl, src_in, dst_in, out)


def store_x(n, s, out):
    wait(n.sp, n.sv.now())
    n.sp.dma_start(out[0:NODES - LAST, :].rearrange("(k p) f -> p k f", p=P),
                   s.X[:, 0:TILES - 1, :]).then_inc(n.ld.sem, 16)
    n.sp.dma_start(out[NODES - LAST:NODES, :], s.X[0:LAST, TILES - 1, :]).then_inc(n.ld.sem, 16)
    n.ld.count += 32
    wait(n.sp, n.ld.now())


def dense_layers(n, s, wl, out):
    with ExitStack() as ctx:
        s.ring = n.buf(ctx, "ring", [P, RING, PANEL], U8)
        with ExitStack() as banks:
            ps = [n.bank(banks, f"sum1_{j}") for j in range(RING)]
            softmax_dense(n, s, ps)
        appnp_dense(n, s, wl[0])
        with ExitStack() as banks:
            ps = [n.bank(banks, f"sum3a_{j}") for j in range(RING)]
            gcn_dense(n, s, ps)
        linear(n, s, "l3a", s.T, wl[1], D, True, relu_to_h(n, s), sa=3 + RING, se=2 * RING)
        with ExitStack() as banks:
            ps = [n.bank(banks, f"sum3_{j}") for j in range(RING)]
            gcn_second_dense(n, s, ps)
        linear(n, s, "l3b", s.T, wl[2], D, True, relu_add_to_x(n, s), sv=RING, sa=3, se=2 * RING)
    store_x(n, s, out)


class Edges:

    def __init__(self, n, s, ctx, src_in, dst_in):
        self.n, self.s = n, s
        self.src = n.buf(ctx, "e_src", [SCAN, COLS], I32)
        self.dst = n.buf(ctx, "e_dst", [SCAN, COLS], I32)
        self.ix = n.buf(ctx, "e_ix", [SCAN, 2], I32)
        self.rel = n.buf(ctx, "e_rel", [SCAN, 1], F32)
        self.hot = n.buf(ctx, "e_hot", [SCAN, P], F32)
        self.count0 = n.buf(ctx, "e_count0", [SCAN, P], F32)
        self.row = n.buf(ctx, "e_row", [SCAN, 3 * D], F32)
        self.msg = n.buf(ctx, "e_msg", [SCAN, 2 * D + 1], F32)
        self.sc = n.buf(ctx, "e_sc", [SCAN, HEADS], F32)
        self.acc = n.buf(ctx, "e_acc", [P, TILES, 2 * D + 1], F32)
        self.ps = n.bank(ctx, "e_ps")
        self.m_d = n.nc.dram_tensor("e_pairs", [TILES * P, 2 * D + 1], F32).ap()
        self.u_d = n.nc.dram_tensor("e_rows", [TILES * P, D], F32).ap()
        for b, arr in ((self.src, src_in), (self.dst, dst_in)):
            n.sp.dma_start(b[:], arr.rearrange("(p e) -> p e", p=SCAN)).then_inc(n.ld.sem, 16)
        n.ld.count += 32
        n.V(n.v.tensor_scalar(self.count0[:], s.count1[0:SCAN, 0:P], 1.0, None, ALU.subtract))
        wait(n.v, n.ld.now())
        wait(n.pool, n.ld.now())

    def publish(self, table, rows):
        n = self.n
        n.meet(n.sp)
        n.sp.dma_start(table.rearrange("(k p) f -> p k f", p=P), rows).then_inc(n.ld.sem, 16)
        n.ld.count += 16
        for e in (n.v, n.a, n.pool):
            wait(e, n.ld.now())

    def sum(self, loads, key, width, message=None, **per):
        n, s = self.n, self.s
        v, a, pe, pool = n.v, n.a, n.pe, n.pool
        acc = self.acc[:, :, 0:width]
        n.meet(v, a, pe, pool)
        n.V(v.memset(acc, 0.0))
        per = {"sv": per.get("sv", 0) + 1 + 3 * TILES, "sa": per.get("sa", 0), "se": TILES,
               "sg": len(loads), "kv": 16 * len(loads)}
        with n.loop(COLS, **{k: c for k, c in per.items() if c}) as e:
            n.meet(v, a, pe, pool)
            for m, (table, index, into) in enumerate(loads):
                t = n.G(pool.tensor_copy(self.ix[:, m:m + 1], index[:, bass.ds(e, 1)]))
                wait(pool, t)
                settle(pool, n.spare)
                n.kv.by(pool.indirect_dma_start(into, None, table, bass.IndirectOffsetOnAxis(
                    ap=self.ix[:, m:m + 1], axis=0)), 16)
            n.V(v.tensor_copy(self.rel[:], key[:, bass.ds(e, 1)]))
            wait(v, n.kv.now())
            wait(a, n.kv.now())
            wait(pe, n.kv.now())
            if message is not None:
                message()
            with n.loop(TILES, sv=3, se=1) as b:
                n.meet(v, pe)
                t = n.V(v.tensor_scalar(self.hot[:], self.count0[:], self.rel[:], None, ALU.is_equal))
                wait(pe, t)
                tp = n.E(pe.matmul(self.ps[:, 0:width], self.hot[:], self.msg[:, 0:width], start=True, stop=True))
                wait(v, t)
                n.V(v.tensor_scalar(self.rel[:], self.rel[:], float(P), None, ALU.subtract))
                wait(v, tp)
                part = acc[:, bass.ds(b, 1), :].rearrange("p a d -> p (a d)")
                n.V(v.tensor_tensor(part, part, self.ps[:, 0:width], ALU.add))
        n.meet(v, a, pe, pool)


def edge_layers(n, s, wq, wl, src_in, dst_in, out):
    v, a, nc = n.v, n.a, n.nc
    with ExitStack() as ctx:
        qkv = n.buf(ctx, "e_all", [P, TILES, 3 * D], F32)

        def keep(i, j, p_, t):
            wait(a, t)
            return n.A(a.activation(qkv[:, bass.ds(RING * i + j, 1), :].rearrange("p a d -> p (a d)"), p_, ACT.Copy))

        linear(n, s, "e_qkv_lin", s.H, wq, 3 * D, False, keep, sa=3 + RING, se=2 * RING)
        q_d = nc.dram_tensor("e_qkv", [TILES * P, 3 * D], F32).ap()
        n.meet(n.sp)
        n.sp.dma_start(q_d.rearrange("(k p) f -> p k f", p=P), qkv[:]).then_inc(n.ld.sem, 16)
        n.ld.count += 16
        for e in (v, a, n.sp, n.pool):
            wait(e, n.ld.now())
    with ExitStack() as ctx:
        E = Edges(n, s, ctx, src_in, dst_in)
        E.q_d = q_d
        kv = n.buf(ctx, "e_kv", [SCAN, 3 * D], F32)
        wide = n.buf(ctx, "e_wide", [P, TILES, 2 * D + 1], F32)

        def attend():
            q, k, val = E.row[:, 0:D], kv[:, D:2 * D], kv[:, 2 * D:3 * D]
            t = n.V(v.tensor_tensor(E.msg[:, 0:D], q, k, ALU.mult))
            wait(v, t)
            t = n.V(v.tensor_reduce(E.sc[:], E.msg[:, 0:D].rearrange("p (h d) -> p h d", d=DH), AX.X, ALU.add))
            wait(v, t)
            t = n.V(v.tensor_scalar(E.sc[:], E.sc[:], 10.0, -10.0, ALU.min, ALU.max))
            wait(a, t)
            t = n.A(a.activation(E.msg[:, D:D + HEADS], E.sc[:], ACT.Exp))
            n.V(v.memset(E.msg[:, D + HEADS:AV], 1.0))
            wait(v, t)
            n.V(v.tensor_tensor(E.msg[:, 0:D].rearrange("p (h d) -> p h d", d=DH),
                                val.rearrange("p (h d) -> p h d", d=DH), over(E.msg[:, D:D + HEADS], DH), ALU.mult))

        E.sum([(E.q_d, E.src, E.row[:]), (E.q_d, E.dst, kv[:])], E.src, AV, attend, sv=5, sa=1)
        den = wide[:, :, 0:HEADS]
        t = n.V(v.tensor_scalar(den, E.acc[:, :, D:D + HEADS], EPS_ATT, None, ALU.add))
        wait(v, t)
        t = n.V(v.reciprocal(den, den))
        wait(v, t)
        for h in range(HEADS):
            t = n.V(v.tensor_tensor(s.T[:, :, h * DH:(h + 1) * DH], E.acc[:, :, h * DH:(h + 1) * DH],
                                    den[:, :, h:h + 1].to_broadcast([P, TILES, DH]), ALU.mult))
        n.V(v.tensor_copy(s.odeg[:, 0:TILES], E.acc[:, :, AV - 1]))
        wait(v, t)
        n.V(v.tensor_tensor(s.X[:], s.X[:], s.T, ALU.add))

        layernorm_relu(n, s)
        t = n.A(a.activation(wide[:, :, 0:D], s.H[:], ACT.Exp))
        wait(v, t)
        n.V(v.tensor_tensor(wide[:, :, D:2 * D], s.H[:], wide[:, :, 0:D], ALU.mult))
        n.V(v.memset(wide[:, :, 2 * D:2 * D + 1], 1.0))
        E.publish(E.m_d, wide[:])
        E.sum([(E.m_d, E.src, E.msg[:])], E.dst, 2 * D + 1)
        e, m = wide[:, :, 0:D], wide[:, :, D:2 * D]
        den, num = E.acc[:, :, 0:D], E.acc[:, :, D:2 * D]
        n.V(v.tensor_scalar(e, den, 0.5, EPS_MSG, ALU.is_gt, ALU.mult))
        t = n.V(v.tensor_scalar(m, den, 0.5, None, ALU.max))
        wait(v, t)
        t = n.V(v.reciprocal(m, m))
        wait(v, t)
        t = n.V(v.tensor_tensor(m, m, num, ALU.mult))
        wait(v, t)
        t = n.V(v.tensor_tensor(m, m, e, ALU.add))
        wait(v, t)
        n.V(v.tensor_tensor(s.T, m, s.H[:], ALU.add))
        n.V(v.tensor_copy(s.ideg[:], E.acc[:, :, 2 * D]))
        linear(n, s, "e_l1", s.T, wl[0], D, True, add_to_x(n, s), sv=RING, sa=3, se=2 * RING)

        degree_columns(n, s)
        layernorm_relu(n, s)
        by_blocks(appnp_begin_stages(n, s))
        n.meet(v)
        with n.loop(STEPS, sv=1 + COLS * (1 + 3 * TILES) + 2, se=COLS * TILES, sg=COLS, kv=16 * COLS, ld=16):
            E.publish(E.u_d, s.T)
            E.sum([(E.u_d, E.dst, E.msg[:, 0:D])], E.src, D)
            t = n.V(v.tensor_tensor(s.T, E.acc[:, :, 0:D], over(s.g[:], D), ALU.mult))
            wait(v, t)
            n.V(v.tensor_tensor(s.T, s.T, s.H[:], ALU.add))
        n.meet(v)
        by_blocks(appnp_end_stages(n, s))

        layernorm_relu(n, s)
        dinv = s.dinv
        for name, w, finish, per in (("e_l3a", wl[1], relu_to_h, dict(sa=3 + RING)),
                                     ("e_l3b", wl[2], relu_add_to_x, dict(sv=RING, sa=3))):
            n.meet(v)
            t = n.V(v.tensor_tensor(s.T, s.H[:], over(dinv[:], D), ALU.mult))
            E.publish(E.u_d, s.T)
            E.sum([(E.u_d, E.src, E.msg[:, 0:D])], E.dst, D)
            t = n.V(v.tensor_tensor(s.T, s.T, E.acc[:, :, 0:D], ALU.add))
            wait(v, t)
            n.V(v.tensor_tensor(s.T, s.T, over(dinv[:], D), ALU.mult))
            linear(n, s, name, s.T, w, D, True, finish(n, s), se=2 * RING, **per)
    store_x(n, s, out)


_INS = ["x", "src", "dst", "L0_gnn_qW", "L0_gnn_kW", "L0_gnn_vW", "L1_gnn_W", "L1_gnn_b",
        "L3_gnn_W1", "L3_gnn_b1", "L3_gnn_W2", "L3_gnn_b2"]
_OUTS = [((NODES, D), "float32")]


def kernel(**inputs):
    import numpy as np
    import concourse.bacc as bacc
    from concourse.bass_utils import run_bass_kernel_spmd as run

    nc = bacc.Bacc("TRN2", target_bir_lowering=False, num_devices=1)
    arrays, args = {}, []
    for name in _INS:
        arr = np.ascontiguousarray(inputs[name])
        arrays[f"in_{name}_dram"] = arr
        args.append(nc.dram_tensor(f"in_{name}_dram", arr.shape, mybir.dt.from_np(arr.dtype), kind="ExternalInput").ap())
    for i, (shape, dtype) in enumerate(_OUTS):
        args.append(nc.dram_tensor(f"out_{i}_dram", shape, mybir.dt.from_np(np.dtype(dtype)), kind="ExternalOutput").ap())
    gnn(nc, *args)
    r = run(nc, [arrays], core_ids=[0])
    return r.results[0]["out_0_dram"]
```
